# Optimizing a Trainium2 kernel written in Bass

```python
import numpy as np
import jax
import jax.numpy as jnp

def _softmax(x, axis=-1):
    return jax.nn.softmax(x, axis=axis)

def _gelu(x):
    return jax.nn.gelu(x, approximate=True)

def _silu(x):
    return jax.nn.silu(x)

def _sigmoid(x):
    return jax.nn.sigmoid(x)

def _layernorm(x, axis=-1, eps=1e-05):
    m = jnp.mean(x, axis=axis, keepdims=True)
    v = jnp.var(x, axis=axis, keepdims=True)
    return (x - m) / jnp.sqrt(v + eps)

def _scatter_add(tgt, idx, src, axis=0):
    return tgt.at[idx].add(src)

def _segment_sum(src, seg, n):
    return jax.ops.segment_sum(src, seg, n)
kernel_name = 'mk_flamingo_gated_d2_seqx_r8_063cfb'

def setup_inputs(seed: int=0):
    np.random.seed(seed)
    _w = jnp.asarray

    def _rec_inputs():
        import jax
        import jax.numpy as jnp
        _rk = jax.random.key(seed)
        x = -9.806e-05 + 1 * jax.random.normal(jax.random.fold_in(_rk, 1), (1, 1024, 128), jnp.float32)
        _lenS = 1024 - jax.random.randint(jax.random.fold_in(_rk, 7), (1,), 0, max(1, 1024 // 4) + 1, jnp.int32)
        _lenS2 = 6404 - jax.random.randint(jax.random.fold_in(_rk, 8), (1,), 0, max(1, 6404 // 4) + 1, jnp.int32)
        _ctx_1024P = jax.random.normal(jax.random.fold_in(_rk, 11), (1, 16, 128), jnp.float32)
        _ctx_1024c = jax.random.dirichlet(jax.random.fold_in(_rk, 511), 0.3 * jnp.ones((16,), jnp.float32), (1, 6404))
        _ctx_1024t = jnp.einsum('bsk,bkd->bsd', _ctx_1024c, _ctx_1024P)
        _ctx_1024t = _ctx_1024t * jax.lax.rsqrt(jnp.mean(jnp.square(_ctx_1024t)) + 1e-12) * 0.953939
        ctx_1024 = -1.52775e-05 + 0.999936 * (_ctx_1024t + 0.3 * jax.random.normal(jax.random.fold_in(_rk, 611), (1, 6404, 128), jnp.float32))
        _g = jax.random.normal(jax.random.fold_in(_rk, 9001), (2, 2), jnp.float32)
        _g = jnp.sign(_g) * jnp.maximum(jnp.abs(_g), 1.0) + (_g == 0) * 1.0
        g_xattn = _g[0]
        g_ffn = _g[1]
        return (x, ctx_1024, g_xattn, g_ffn)
    x, ctx_1024, g_xattn, g_ffn = _rec_inputs()

    def _L0_xattn_setup():
        import jax, jax.numpy as jnp
        import numpy as np
        D = 128
        NUM_ITERS = 3
        EPS = 1e-06
        SCALE = D ** (-0.5)

        def rmsnorm(x, w, eps=EPS):
            return x * jax.lax.rsqrt(jnp.mean(x * x, axis=-1, keepdims=True) + eps) * w

        def gru_cell(x, h, wih, whh, bih, bhh):
            gx = x @ wih.T + bih
            gh = h @ whh.T + bhh
            xr, xz, xn = jnp.split(gx, 3, axis=-1)
            hr, hz, hn = jnp.split(gh, 3, axis=-1)
            r = jax.nn.sigmoid(xr + hr)
            z = jax.nn.sigmoid(xz + hz)
            n = jnp.tanh(xn + r * hn)
            return (1.0 - z) * n + z * h
        key = jax.random.key(seed)
        ks = jax.random.split(key, 8)
        B, K, M, d = (8, 64, 512, D)
        w_std = d ** (-0.5)
        return {'slots': jax.random.normal(ks[0], (B, K, d), jnp.float32), 'P': jax.random.normal(ks[1], (B, M, d), jnp.float32), 'Wq': jax.random.normal(ks[2], (d, d), jnp.float32) * w_std, 'Wk': jax.random.normal(ks[3], (d, d), jnp.float32) * w_std, 'Wv': jax.random.normal(ks[4], (d, d), jnp.float32) * w_std, 'gru_wih': jax.random.normal(ks[5], (3 * d, d), jnp.float32) * w_std, 'gru_whh': jax.random.normal(ks[6], (3 * d, d), jnp.float32) * w_std, 'gru_bih': jnp.zeros((3 * d,), jnp.float32), 'gru_bhh': jnp.zeros((3 * d,), jnp.float32), 'slot_norm_w': jnp.ones((d,), jnp.float32), 'input_norm_w': jnp.ones((d,), jnp.float32)}
    _L0_xattn_all = _L0_xattn_setup()
    _L0_xattn_in = {k: v for k, v in _L0_xattn_all.items() if k in ('Wq', 'Wk', 'Wv', 'gru_wih', 'gru_whh', 'gru_bih', 'gru_bhh', 'slot_norm_w', 'input_norm_w')}
    del _L0_xattn_all

    def _L0_ffn_setup():
        import jax, jax.numpy as jnp
        import numpy as np
        TOP_K = 8
        key = jax.random.key(seed)
        ks = jax.random.split(key, 6)
        B, S, D, F, E = (2, 128, 128, 64, 64)
        x = jax.random.normal(ks[0], (B, S, D), dtype=jnp.float32)
        centroids = jax.random.normal(ks[1], (E, D), dtype=jnp.float32) * 0.05
        expert_biases = jnp.zeros((E,), dtype=jnp.float32)
        Ws_up = jax.random.normal(ks[2], (D, F), dtype=jnp.float32) / np.sqrt(D)
        Ws_down = jax.random.normal(ks[3], (F, D), dtype=jnp.float32) / np.sqrt(F)
        W_up = jax.random.normal(ks[4], (E, D, F), dtype=jnp.float32) / np.sqrt(D)
        W_down = jax.random.normal(ks[5], (E, F, D), dtype=jnp.float32) / np.sqrt(F)
        return {'x': x, 'centroids': centroids, 'expert_biases': expert_biases, 'Ws_up': Ws_up, 'Ws_down': Ws_down, 'W_up': W_up, 'W_down': W_down}
    _L0_ffn_all = _L0_ffn_setup()
    _L0_ffn_in = {k: v for k, v in _L0_ffn_all.items() if k in ('centroids', 'expert_biases', 'Ws_up', 'Ws_down', 'W_up', 'W_down')}
    del _L0_ffn_all

    def _L1_xattn_setup():
        import jax, jax.numpy as jnp
        import numpy as np
        DIM = 128
        DIM_HEAD = 64
        HEADS = 16
        INNER = DIM_HEAD * HEADS

        def _layernorm(x, g, b, eps=1e-05):
            mu = jnp.mean(x, axis=-1, keepdims=True)
            var = jnp.var(x, axis=-1, keepdims=True)
            return (x - mu) * jax.lax.rsqrt(var + eps) * g + b
        key = jax.random.key(seed)
        ks = jax.random.split(key, 8)
        B, Nq, Nk = (2, 256, 256)
        x = jax.random.normal(ks[0], (B, Nq, DIM), dtype=jnp.float32)
        context = jax.random.normal(ks[1], (B, Nk, DIM), dtype=jnp.float32)
        s = 1.0 / np.sqrt(DIM)
        Wq = jax.random.normal(ks[2], (DIM, INNER), dtype=jnp.float32) * s
        Wkv = jax.random.normal(ks[3], (DIM, 2 * INNER), dtype=jnp.float32) * s
        Wo = jax.random.normal(ks[4], (INNER, DIM), dtype=jnp.float32) * (1.0 / np.sqrt(INNER))
        ln_g = jnp.ones((DIM,), dtype=jnp.float32)
        ln_b = jnp.zeros((DIM,), dtype=jnp.float32)
        return {'x': x, 'context': context, 'Wq': Wq, 'Wkv': Wkv, 'Wo': Wo, 'ln_g': ln_g, 'ln_b': ln_b}
    _L1_xattn_all = _L1_xattn_setup()
    _L1_xattn_in = {k: v for k, v in _L1_xattn_all.items() if k in ('Wq', 'Wkv', 'Wo', 'ln_g', 'ln_b')}
    del _L1_xattn_all

    def _L1_ffn_setup():
        import jax, jax.numpy as jnp
        import numpy as np
        B, S, H = (2, 128, 128)
        E, F = (8, 512)
        GATE_TEMP = 0.1
        key = jax.random.key(seed)
        ks = jax.random.split(key, 6)
        s_h = 1.0 / np.sqrt(H)
        s_f = 1.0 / np.sqrt(F)
        return {'hidden_states': jax.random.normal(ks[0], (B, S, H), dtype=jnp.float32), 'w_router': jax.random.normal(ks[1], (H, E), dtype=jnp.float32) * s_h, 'w_gating': jax.random.normal(ks[2], (H, E), dtype=jnp.float32) * s_h, 'w_gate': jax.random.normal(ks[3], (E, H, F), dtype=jnp.float32) * s_h, 'w_up': jax.random.normal(ks[4], (E, H, F), dtype=jnp.float32) * s_h, 'w_down': jax.random.normal(ks[5], (E, F, H), dtype=jnp.float32) * s_f}
    _L1_ffn_all = _L1_ffn_setup()
    _L1_ffn_in = {k: v for k, v in _L1_ffn_all.items() if k in ('w_router', 'w_gating', 'w_gate', 'w_up', 'w_down')}
    del _L1_ffn_all
    return {'x': x, 'ctx_1024': ctx_1024, 'g_xattn': g_xattn, 'g_ffn': g_ffn, 'L0_xattn_Wq': _L0_xattn_in['Wq'], 'L0_xattn_Wk': _L0_xattn_in['Wk'], 'L0_xattn_Wv': _L0_xattn_in['Wv'], 'L0_xattn_gru_wih': _L0_xattn_in['gru_wih'], 'L0_xattn_gru_whh': _L0_xattn_in['gru_whh'], 'L0_xattn_gru_bih': _L0_xattn_in['gru_bih'], 'L0_xattn_gru_bhh': _L0_xattn_in['gru_bhh'], 'L0_xattn_slot_norm_w': _L0_xattn_in['slot_norm_w'], 'L0_xattn_input_norm_w': _L0_xattn_in['input_norm_w'], 'L0_ffn_centroids': _L0_ffn_in['centroids'], 'L0_ffn_expert_biases': _L0_ffn_in['expert_biases'], 'L0_ffn_Ws_up': _L0_ffn_in['Ws_up'], 'L0_ffn_Ws_down': _L0_ffn_in['Ws_down'], 'L0_ffn_W_up': _L0_ffn_in['W_up'], 'L0_ffn_W_down': _L0_ffn_in['W_down'], 'L1_xattn_Wq': _L1_xattn_in['Wq'], 'L1_xattn_Wkv': _L1_xattn_in['Wkv'], 'L1_xattn_Wo': _L1_xattn_in['Wo'], 'L1_xattn_ln_g': _L1_xattn_in['ln_g'], 'L1_xattn_ln_b': _L1_xattn_in['ln_b'], 'L1_ffn_w_router': _L1_ffn_in['w_router'], 'L1_ffn_w_gating': _L1_ffn_in['w_gating'], 'L1_ffn_w_gate': _L1_ffn_in['w_gate'], 'L1_ffn_w_up': _L1_ffn_in['w_up'], 'L1_ffn_w_down': _L1_ffn_in['w_down']}

def reference(x, ctx_1024, g_xattn, g_ffn, L0_xattn_Wq, L0_xattn_Wk, L0_xattn_Wv, L0_xattn_gru_wih, L0_xattn_gru_whh, L0_xattn_gru_bih, L0_xattn_gru_bhh, L0_xattn_slot_norm_w, L0_xattn_input_norm_w, L0_ffn_centroids, L0_ffn_expert_biases, L0_ffn_Ws_up, L0_ffn_Ws_down, L0_ffn_W_up, L0_ffn_W_down, L1_xattn_Wq, L1_xattn_Wkv, L1_xattn_Wo, L1_xattn_ln_g, L1_xattn_ln_b, L1_ffn_w_router, L1_ffn_w_gating, L1_ffn_w_gate, L1_ffn_w_up, L1_ffn_w_down):
    import jax
    import jax.numpy as jnp

    def _L0_xattn_ref(slots, P, Wq, Wk, Wv, gru_wih, gru_whh, gru_bih, gru_bhh, slot_norm_w, input_norm_w):
        import jax, jax.numpy as jnp
        import numpy as np
        D = 128
        NUM_ITERS = 3
        EPS = 1e-06
        SCALE = D ** (-0.5)

        def rmsnorm(x, w, eps=EPS):
            return x * jax.lax.rsqrt(jnp.mean(x * x, axis=-1, keepdims=True) + eps) * w

        def gru_cell(x, h, wih, whh, bih, bhh):
            gx = x @ wih.T + bih
            gh = h @ whh.T + bhh
            xr, xz, xn = jnp.split(gx, 3, axis=-1)
            hr, hz, hn = jnp.split(gh, 3, axis=-1)
            r = jax.nn.sigmoid(xr + hr)
            z = jax.nn.sigmoid(xz + hz)
            n = jnp.tanh(xn + r * hn)
            return (1.0 - z) * n + z * h
        Pn = rmsnorm(P, input_norm_w)
        k_proj = Pn @ Wk.T
        v_proj = Pn @ Wv.T
        for _ in range(NUM_ITERS):
            sn = rmsnorm(slots, slot_norm_w)
            q_proj = sn @ Wq.T
            scores = jnp.einsum('bkd,bmd->bkm', q_proj, k_proj) * SCALE
            attn = jax.nn.softmax(scores, axis=-2)
            attn = attn / (jnp.sum(attn, axis=-1, keepdims=True) + EPS)
            updates = jnp.einsum('bkm,bmd->bkd', attn, v_proj)
            slots = gru_cell(updates, slots, gru_wih, gru_whh, gru_bih, gru_bhh)
        return slots

    def _L0_ffn_ref(x, centroids, expert_biases, Ws_up, Ws_down, W_up, W_down):
        import jax, jax.numpy as jnp
        import numpy as np
        TOP_K = 8
        B, S, D = x.shape
        E = centroids.shape[0]
        T = B * S
        xf = x.reshape(T, D)
        shared = jax.nn.silu(xf @ Ws_up) @ Ws_down
        aff = xf @ centroids.T
        biased = aff + expert_biases
        _, idx = jax.lax.top_k(biased, TOP_K)
        sel = jnp.take_along_axis(aff, idx, axis=1)
        w = jax.nn.sigmoid(sel)
        w = w / (jnp.sum(w, axis=-1, keepdims=True) + 1e-08)
        cw = jnp.zeros((T, E), dtype=x.dtype).at[jnp.arange(T)[:, None], idx].add(w)
        h = jax.nn.silu(jnp.einsum('td,edf->etf', xf, W_up))
        y = jnp.einsum('etf,efd->etd', h, W_down)
        routed = jnp.einsum('etd,te->td', y, cw)
        return (shared + routed).reshape(B, S, D)

    def _L1_xattn_ref(x, context, Wq, Wkv, Wo, ln_g, ln_b):
        import jax, jax.numpy as jnp
        import numpy as np
        DIM = 128
        DIM_HEAD = 64
        HEADS = 16
        INNER = DIM_HEAD * HEADS

        def _layernorm(x, g, b, eps=1e-05):
            mu = jnp.mean(x, axis=-1, keepdims=True)
            var = jnp.var(x, axis=-1, keepdims=True)
            return (x - mu) * jax.lax.rsqrt(var + eps) * g + b
        B, Nq, _ = x.shape
        scale = DIM_HEAD ** (-0.5)
        ctx = _layernorm(context, ln_g, ln_b)
        q = x @ Wq
        kv = ctx @ Wkv
        k, v = jnp.split(kv, 2, axis=-1)

        def split_heads(t):
            b, n, _ = t.shape
            return t.reshape(b, n, HEADS, DIM_HEAD).transpose(0, 2, 1, 3)
        q, k, v = map(split_heads, (q, k, v))
        sim = jnp.einsum('bhid,bhjd->bhij', q, k) * scale
        attn = jax.nn.softmax(sim, axis=-1)
        out = jnp.einsum('bhij,bhjd->bhid', attn, v)
        out = out.transpose(0, 2, 1, 3).reshape(B, Nq, INNER)
        return out @ Wo

    def _L1_ffn_ref(hidden_states, w_router, w_gating, w_gate, w_up, w_down):
        import jax, jax.numpy as jnp
        import numpy as np
        B, S, H = (2, 128, 128)
        E, F = (8, 512)
        GATE_TEMP = 0.1
        x = hidden_states
        router_probs = jax.nn.softmax(jnp.einsum('bsh,he->bse', x, w_router), axis=-1)
        gate_weights = jax.nn.softmax(jnp.einsum('bsh,he->bse', x, w_gating) / GATE_TEMP, axis=-1)
        g = jnp.einsum('bsh,ehf->ebsf', x, w_gate)
        u = jnp.einsum('bsh,ehf->ebsf', x, w_up)
        h = jax.nn.silu(g) * u
        expert_out = jnp.einsum('ebsf,efh->ebsh', h, w_down)
        cw = router_probs * gate_weights
        cw = cw / (jnp.sum(cw, axis=-1, keepdims=True) + 1e-09)
        out = jnp.einsum('ebsh,bse->bsh', expert_out, cw)
        return out
    x = x + jnp.tanh(g_xattn[0]) * _L0_xattn_ref(_layernorm(x, axis=-1), ctx_1024, L0_xattn_Wq, L0_xattn_Wk, L0_xattn_Wv, L0_xattn_gru_wih, L0_xattn_gru_whh, L0_xattn_gru_bih, L0_xattn_gru_bhh, L0_xattn_slot_norm_w, L0_xattn_input_norm_w)
    x = x + jnp.tanh(g_ffn[0]) * _L0_ffn_ref(_layernorm(x, axis=-1), L0_ffn_centroids, L0_ffn_expert_biases, L0_ffn_Ws_up, L0_ffn_Ws_down, L0_ffn_W_up, L0_ffn_W_down)
    x = x + jnp.tanh(g_xattn[1]) * _L1_xattn_ref(_layernorm(x, axis=-1), ctx_1024, L1_xattn_Wq, L1_xattn_Wkv, L1_xattn_Wo, L1_xattn_ln_g, L1_xattn_ln_b)
    x = x + jnp.tanh(g_ffn[1]) * _L1_ffn_ref(_layernorm(x, axis=-1), L1_ffn_w_router, L1_ffn_w_gating, L1_ffn_w_gate, L1_ffn_w_up, L1_ffn_w_down)
    return x

_drawn_inputs = setup_inputs


def setup_inputs(seed=0):
    import zlib

    import numpy as np

    out = dict(_drawn_inputs(seed))
    spreads = {'g_ffn': (-1.0, 0.6),
     'L0_xattn_gru_bih': (0.0, 0.1),
     'L0_xattn_gru_bhh': (0.0, 0.1),
     'L0_xattn_slot_norm_w': (1.0, 0.2),
     'L0_xattn_input_norm_w': (1.0, 0.2),
     'L0_ffn_expert_biases': (0.0, 0.1),
     'L1_xattn_ln_g': (1.0, 0.2),
     'L1_xattn_ln_b': (0.0, 0.1)}
    factors = {}
    for name, (base, spread) in spreads.items():
        noise = np.random.default_rng([zlib.crc32(name.encode()), seed]).standard_normal(out[name].shape)
        drawn = base * np.exp(spread * noise) if base else spread * noise
        out[name] = jnp.asarray(drawn.astype(out[name].dtype))
    for name, factor in factors.items():
        out[name] = (out[name] * factor).astype(out[name].dtype)
    return out
```

```python
import math

import concourse.bass as bass
from concourse import mybir
from contextlib import ExitStack

FP32 = mybir.dt.float32
BF16 = mybir.dt.bfloat16
FP16 = mybir.dt.float16
ALU = mybir.AluOpType
ACT = mybir.ActivationFunctionType
AX = mybir.AxisListType

P = 128
D = 128
T = 1024
TT = T // P
M = 6404
GT = 4
G = -(-M // (P * GT))
MT = G * GT
MP = MT * P
FULL = M // P
TAIL = M - FULL * P
HEADS, DH = 16, 64
NITER = 3
SLOT_SCALE = D ** -0.5
HEAD_SCALE = DH ** -0.5
LIFT = 12 * math.log(2.0)
VAL_SCALE = float(2 ** 20)
SLOT_EPS = 1e-6
E0, F0 = 64, 64
CH0 = E0 // 2 + 1
E1, F1 = 8, 512
CPE = F1 // P
TOPK = 8
CREDIT = 2
C_WIN, C_WSLOT, C_BIR, C_BIZ, C_BIN, C_BHR, C_BHZ, C_BHN, C_LNG, C_LNB = range(10)


def top(ap):
    return ap.bitcast(BF16).rearrange("p (n b) -> p b n", b=2)[:, 1, :]


def half(h):
    return slice(512 * h, 512 * h + 512)


def tile(i):
    return slice(P * i, P * i + P)


class Chain:

    def __init__(self, eng, sem, base=0):
        self.eng, self.sem, self.n = eng, sem, base

    def __call__(self, ins):
        self.n = self.n + 1
        ins.then_inc(self.sem, 1)
        self.eng.wait_ge(self.sem, self.n)


class Core:

    def __init__(self, nc, ctx):
        self.nc, self.ctx = nc, ctx

    def sb(self, name, shape, dt=FP32, ctx=None):
        return (ctx or self.ctx).enter_context(self.nc.sbuf_tensor(name, shape, dt))

    def sem(self, name):
        return self.ctx.enter_context(self.nc.semaphore(name))


def build(nc, x, ctx_rows, cols, gates, slot_w, cent_t, bias_e, wq1, wkv1, wo1, rout_w, ffn0_w, ffn1_w, out):
    with ExitStack() as stack:
        k = Core(nc, stack)
        k.x = k.sb("x_rows", [P, TT, D])
        k.cols = k.sb("cols_sb", [P, 10])
        k.gates = k.sb("gates_sb", [P, 4])
        k.tg = k.sb("tanh_gates", [P, 4])
        k.cent = k.sb("centroids_t", [P, E0])
        k.bias_e = k.sb("expert_bias", [P, E0])
        k.rout = k.sb("router_w", [P, 2 * E1])
        k.ident = k.sb("ident", [P, P])
        k.ident_h = k.sb("ident_h", [P, P], FP16)
        k.mean_w = k.sb("mean_w", [P, P])
        k.zero_h = k.sb("zero_h", [P, 512], FP16)
        k.eps5 = k.sb("eps5", [P, 1])
        k.eps6 = k.sb("eps6", [P, 1])
        k.bsum = k.sb("gru_bias_sum", [P, 2])
        k.win_s = k.sb("win_scaled", [P, 1])
        k.mask = k.sb("row_mask", [P, MT])
        k.ch = k.sb("ctx_t_hi", [P, MP], FP16)
        k.cl = k.sb("ctx_t_lo", [P, MP], FP16)
        k.xt = k.sb("xn_t", [P, T])
        k.xth = k.sb("xn_t_hi", [P, T], FP16)
        k.xtl = k.sb("xn_t_lo", [P, T], FP16)
        k.e = k.sb("exps", [P, 2, T])
        k.el = k.sb("exps_lo", [P, 2, T], FP16)
        k.stats = k.sb("stats", [P, TT, 6])
        k.mv = k.sb("mean_var", [P, TT, 2])
        k.small = k.sb("small", [P, 8, 64])
        k.ps = stack.enter_context(nc.psum_tensor("ps", [P, 8, 512], FP32))

        with ExitStack() as l0:
            k.pn = k.sb("ctx_rms", [P, MT, D + 1], FP32, l0)
            k.pth = k.sb("ctx_rms_t_hi", [P, MP], FP16, l0)
            k.ptl = k.sb("ctx_rms_t_lo", [P, MP], FP16, l0)
            with ExitStack() as pro:
                prologue(k, pro, x, ctx_rows, cols, gates, cent_t, bias_e, rout_w)
            with ExitStack() as at:
                slot_attention(k, at, slot_w)
        with ExitStack() as f0:
            normed(k, "n1")
            cwt = k.sb("ffn0_cw", [P, 2, T], FP16, f0)
            with ExitStack() as r:
                top_experts(k, r, cwt)
            experts(k, f0, "f0", cwt, ffn0_w, 1)
        with ExitStack() as a1:
            normed(k, "n2")
            cross_attention(k, a1, wq1, wkv1, wo1)
        with ExitStack() as f1:
            normed(k, "n3")
            cwt = k.sb("ffn1_cw", [P, 2, T], FP16, f1)
            with ExitStack() as r:
                soft_experts(k, r, cwt)
            experts(k, f1, "f1", cwt, ffn1_w, 3)
        out_done = k.sem("out_done")
        with nc.Block() as block:
            @block.sync
            def _(sp):
                sp.dma_start(out[0].rearrange("(i p) d -> p i d", p=P), k.x[:, :, :]).then_inc(out_done, 16)
                sp.wait_ge(out_done, 16)


def prologue(k, scope, x, ctx_rows, cols, gates, cent_t, bias_e, rout_w):
    nc, ps = k.nc, k.ps
    CH = 13
    rows = k.sb("ctx_rows", [P, MT, D], FP32, scope)
    st = k.sb("ctx_stats", [P, MT, 6], FP32, scope)
    mv = k.sb("ctx_mv", [P, MT, 2], FP32, scope)
    rms = k.sb("ctx_rms_r", [P, MT], FP32, scope)
    lnr = k.sb("ctx_ln_r", [P, MT], FP32, scope)
    lnm = k.sb("ctx_ln_m", [P, MT], FP32, scope)
    sd = k.sb("ctx_sd", [P, 2, MT], FP32, scope)
    rn = k.sb("ctx_rn", [P, 2, GT, D], FP32, scope)
    ln = k.sb("ctx_ln", [P, 2, GT, D], FP32, scope)
    lt = k.sb("ctx_ln_t", [P, 2, 512], FP32, scope)
    ld_small, ld_x = k.sem("ld_small"), k.sem("ld_x")
    ld_ctx = [k.sem(f"ld_ctx{c}") for c in range(MT // CH)]
    ready = k.sem("pro_consts")
    d_ch, g_ch = k.sem("pro_dve"), k.sem("pro_pool")
    stats_done, aggr_done, msq_ready, sd_ready = (k.sem(n) for n in ("c_stats", "c_aggr", "c_msq", "c_sd"))
    mask_ready, rms_ready = k.sem("c_mask"), k.sem("c_rms")
    pn_ready, ln_ready, pt_ready, lt_ps, pth_done, lt_done, ch_done, ptl_done, cl_done = (
        k.sem(n) for n in ("pn_ready", "ln_ready", "pt_ready", "lt_ps", "pth_done", "lt_done", "ch_done", "ptl_done", "cl_done"))

    def groups(eng, body):
        with eng.Fori(0, G // 2) as i:
            body(i * 2, 0)
            body(i * 2 + 1, 1)
        body(G - 1, 0)

    with nc.Block() as block:
        @block.sync
        def _(sp):
            body = ctx_rows[0, 0:FULL * P, :].rearrange("(j p) d -> p j d", p=P)
            last = ctx_rows[0, M - P:M, :]
            for c in range(MT // CH):
                hi = min(FULL, CH * (c + 1))
                sp.dma_start(rows[:, CH * c:hi, :], body[:, CH * c:hi, :]).then_inc(ld_ctx[c], 16)
            for j in range(FULL, MT):
                sp.dma_start(rows[:, j, :], last).then_inc(ld_ctx[-1], 16)
            for dst, src in ((k.cols, cols), (k.gates, gates), (k.cent, cent_t), (k.bias_e, bias_e), (k.rout, rout_w)):
                sp.dma_start(dst[:, :], src).then_inc(ld_small, 16)
            sp.dma_start(k.x[:, :, :], x[0].rearrange("(i p) d -> p i d", p=P)).then_inc(ld_x, 16)
            sp.wait_ge(ld_x, 16)

        @block.gpsimd
        def _(pool):
            chain = Chain(pool, g_ch)
            chain(pool.memset(k.ident[:, :], 0.0))
            chain(pool.affine_select(out=k.ident[:, :], in_=k.ident[:, :], compare_op=ALU.not_equal, fill=1.0,
                                     base=0, pattern=[[-1, P]], channel_multiplier=1))
            pool.tensor_copy(k.ident_h[:, :], k.ident[:, :]).then_inc(ready, 1)
            chain(pool.memset(k.mask[:, :], 1.0))
            chain(pool.memset(k.mask[:, FULL + 1:MT], 0.0))
            pool.affine_select(out=k.mask[:, FULL:FULL + 1], in_=k.mask[:, FULL:FULL + 1], compare_op=ALU.is_ge,
                               fill=0.0, base=TAIL - P, pattern=[[0, 1]], channel_multiplier=1).then_inc(mask_ready, 1)

        @block.vector
        def _(dve):
            chain = Chain(dve, d_ch)
            dve.memset(k.mean_w[:, :], 1.0 / D)
            dve.memset(k.zero_h[:, :], 0.0)
            dve.memset(k.eps5[:, :], 1e-5)
            chain(dve.memset(k.eps6[:, :], 1e-6))
            for c in range(MT // CH):
                dve.wait_ge(ld_ctx[c], 16 * (1 + (c == MT // CH - 1) * (MT - FULL)))
                with dve.Fori(CH * c, CH * c + CH) as j:
                    dve.bn_stats(st[:, j, :], rows[:, j, :]).then_inc(stats_done, 1)
            dve.wait_ge(stats_done, MT)
            for j in range(MT):
                dve.bn_aggr(mv[:, j, :], st[:, j, :]).then_inc(aggr_done, 1)
            dve.wait_ge(aggr_done, MT)
            chain(dve.tensor_tensor(lnm[:, :], mv[:, :, 0], mv[:, :, 0], ALU.mult))
            dve.tensor_tensor(rms[:, :], lnm[:, :], mv[:, :, 1], ALU.add).then_inc(msq_ready, 1)
            dve.wait_ge(sd_ready, 2)
            chain(dve.reciprocal(rms[:, :], sd[:, 0, :]))
            chain(dve.reciprocal(lnr[:, :], sd[:, 1, :]))
            dve.scalar_tensor_tensor(out=lnm[:, :], in0=mv[:, :, 0], scalar=-1.0, in1=lnr[:, :],
                                     op0=ALU.mult, op1=ALU.mult)
            dve.wait_ge(mask_ready, 1)
            dve.tensor_copy(k.pn[:, :, D], k.mask[:, :])
            dve.tensor_tensor(rms[:, :], rms[:, :], k.mask[:, :], ALU.mult).then_inc(rms_ready, 1)
            dve.wait_ge(rms_ready, 1)
            dve.wait_ge(ld_small, 16 * 5)
            dve.tensor_tensor(k.bsum[:, :], k.cols[:, C_BIR:C_BIZ + 1], k.cols[:, C_BHR:C_BHZ + 1], ALU.add)
            dve.tensor_scalar(k.win_s[:, :], k.cols[:, C_WIN:C_WIN + 1], SLOT_SCALE, None, ALU.mult)

            def rows_of(g, b):
                dve.wait_ge(pt_ready, g + 1)
                for u in range(GT):
                    j = g * GT + u
                    ins = dve.tensor_scalar(rn[:, b, u, :], rows[:, j, :], rms[:, bass.ds(j, 1)], None, ALU.mult)
                ins.then_inc(pn_ready, 1)
                dve.wait_ge(lt_ps, g + 1)
                for u in range(GT):
                    j = g * GT + u
                    ins = dve.tensor_scalar(ln[:, b, u, :], rows[:, j, :], lnr[:, bass.ds(j, 1)], lnm[:, bass.ds(j, 1)],
                                            ALU.mult, ALU.add)
                ins.then_inc(ln_ready, 1)
                dve.wait_ge(pth_done, g + 1)
                dve.tensor_tensor(k.ptl[:, bass.ds(g * 512, 512)], ps[:, b, :], k.pth[:, bass.ds(g * 512, 512)],
                                  ALU.subtract).then_inc(ptl_done, 1)
                dve.wait_ge(ch_done, g + 1)
                dve.tensor_tensor(k.cl[:, bass.ds(g * 512, 512)], lt[:, b, :], k.ch[:, bass.ds(g * 512, 512)],
                                  ALU.subtract).then_inc(cl_done, 1)

            groups(dve, rows_of)

        @block.tensor
        def _(pe):
            pe.sem_inc(lt_ps, CREDIT)
            pe.sem_inc(pt_ready, CREDIT)
            pe.wait_ge(ready, 1)

            def turn(g, b):
                pe.wait_ge(pn_ready, g + 1)
                pe.wait_ge(ptl_done, g + 1)
                for u in range(GT):
                    ins = pe.transpose(ps[:, b, tile(u)], rn[:, b, u, :], k.ident[:, :])
                ins.then_inc(pt_ready, 1)
                pe.wait_ge(ln_ready, g + 1)
                pe.wait_ge(lt_done, g + 1)
                for u in range(GT):
                    ins = pe.transpose(ps[:, 2 + b, tile(u)], ln[:, b, u, :], k.ident[:, :])
                ins.then_inc(lt_ps, 1)

            groups(pe, turn)

        @block.scalar
        def _(act):
            act.sem_inc(lt_done, CREDIT)
            act.sem_inc(ptl_done, CREDIT)
            act.sem_inc(cl_done, CREDIT)
            act.wait_ge(msq_ready, 1)
            act.activation(sd[:, 0, :], rms[:, :], ACT.Sqrt, bias=k.eps6[:, :]).then_inc(sd_ready, 1)
            act.activation(sd[:, 1, :], mv[:, :, 1], ACT.Sqrt, bias=k.eps5[:, :]).then_inc(sd_ready, 1)
            act.wait_ge(ld_small, 16 * 5)
            act.wait_ge(rms_ready, 1)

            def split(g, b):
                for u in range(GT):
                    j = g * GT + u
                    act.activation(k.pn[:, j, 0:D], rows[:, j, :], ACT.Copy, scale=rms[:, bass.ds(j, 1)])
                act.wait_ge(pt_ready, g + 1 + CREDIT)
                act.activation(k.pth[:, bass.ds(g * 512, 512)], ps[:, b, :], ACT.Copy).then_inc(pth_done, 1)
                act.wait_ge(lt_ps, g + 1 + CREDIT)
                act.wait_ge(cl_done, g + 1)
                act.activation(lt[:, b, :], ps[:, 2 + b, :], ACT.Identity, bias=k.cols[:, C_LNB:C_LNB + 1],
                               scale=k.cols[:, C_LNG:C_LNG + 1]).then_inc(lt_done, 1)
                act.wait_ge(lt_done, g + 1 + CREDIT)
                act.activation(k.ch[:, bass.ds(g * 512, 512)], lt[:, b, :], ACT.Copy).then_inc(ch_done, 1)

            groups(act, split)
            act.activation(k.tg[:, :], k.gates[:, :], ACT.Tanh)

    norm_rows(k, scope, "n0")


def normed(k, tag):
    with ExitStack() as scope:
        norm_rows(k, scope, tag)


def norm_rows(k, scope, tag):
    nc, ps = k.nc, k.ps
    xn = k.sb(f"{tag}_rows", [P, TT, D], FP32, scope)
    sd = k.sb(f"{tag}_sd", [P, 3, TT], FP32, scope)
    stats_done, aggr_done, sd_ready, rows_ready, turned, hi_ready, d_ch = (
        k.sem(f"{tag}_{n}") for n in ("stats", "aggr", "sdr", "rows_ready", "turned", "hi", "dve"))
    with nc.Block() as block:
        @block.vector
        def _(dve):
            chain = Chain(dve, d_ch)
            for i in range(TT):
                dve.bn_stats(k.stats[:, i, :], k.x[:, i, :]).then_inc(stats_done, 1)
            dve.wait_ge(stats_done, TT)
            for i in range(TT):
                dve.bn_aggr(k.mv[:, i, :], k.stats[:, i, :]).then_inc(aggr_done, 1)
            dve.wait_ge(sd_ready, 1)
            chain(dve.reciprocal(sd[:, 1, :], sd[:, 0, :]))
            chain(dve.scalar_tensor_tensor(out=sd[:, 2, :], in0=k.mv[:, :, 0], scalar=-1.0, in1=sd[:, 1, :],
                                           op0=ALU.mult, op1=ALU.mult))
            for i in range(TT):
                dve.tensor_scalar(xn[:, i, :], k.x[:, i, :], sd[:, 1, i:i + 1], sd[:, 2, i:i + 1],
                                  ALU.mult, ALU.add).then_inc(rows_ready, 1)
            for h in range(2):
                dve.wait_ge(hi_ready, h + 1)
                dve.tensor_tensor(k.xtl[:, half(h)], ps[:, h, :], k.xth[:, half(h)], ALU.subtract)

        @block.scalar
        def _(act):
            act.wait_ge(aggr_done, TT)
            act.activation(sd[:, 0, :], k.mv[:, :, 1], ACT.Sqrt, bias=k.eps5[:, :]).then_inc(sd_ready, 1)
            for h in range(2):
                act.wait_ge(turned, h + 1)
                act.activation(k.xt[:, half(h)], ps[:, h, :], ACT.Copy)
                act.activation(k.xth[:, half(h)], ps[:, h, :], ACT.Copy).then_inc(hi_ready, 1)

        @block.tensor
        def _(pe):
            for h in range(2):
                for i in range(4 * h, 4 * h + 4):
                    pe.wait_ge(rows_ready, i + 1)
                    ins = pe.transpose(ps[:, h, tile(i - 4 * h)], xn[:, i, :], k.ident[:, :])
                ins.then_inc(turned, 1)


def residual(k, tag, src_t, gate):
    nc, ps = k.nc, k.ps
    turned = k.sem(f"{tag}_turned")
    with nc.Block() as block:
        @block.tensor
        def _(pe):
            for i in range(TT):
                ins = pe.transpose(ps[:, i // 4, tile(i % 4)], src_t[:, tile(i)], k.ident[:, :])
                if i % 4 == 3:
                    ins.then_inc(turned, 1)

        @block.vector
        def _(dve):
            for h in range(2):
                dve.wait_ge(turned, h + 1)
                rows = k.x[:, 4 * h:4 * h + 4, :].rearrange("p i d -> p (i d)")
                dve.scalar_tensor_tensor(out=rows, in0=ps[:, h, :], scalar=k.tg[:, gate:gate + 1], in1=rows,
                                         op0=ALU.mult, op1=ALU.add)


def slot_attention(k, scope, slot_w):
    nc, ps = k.nc, k.ps
    w = k.sb("slot_w", [P, 3 * D + 6 * D], FP32, scope)
    wq, wk, wv = (w[:, D * n:D * n + D] for n in range(3))
    wih = [w[:, D * (3 + n):D * (4 + n)] for n in range(3)]
    whh = [w[:, D * (6 + n):D * (7 + n)] for n in range(3)]
    slots = k.xt
    t = [k.sb(f"slot_t{n}", [P, T], FP32, scope) for n in range(5)]
    qh, ql = (k.sb(n, [P, T], FP16, scope) for n in ("slot_qh", "slot_ql"))
    mx = k.sb("slot_mx", [P, 2, 1], FP32, scope)
    nb = k.sb("slot_nb", [P, 2, 1], FP32, scope)
    sums = k.sb("slot_sums", [P, 2, 1], FP32, scope)
    rec = k.sb("slot_rec", [P, 2, 2], FP32, scope)
    vh, vl = (k.sb(n, [P, 2, D + 1], FP16, scope) for n in ("slot_vh", "slot_vl"))
    den = k.sb("slot_den", [P, 2, TT], FP32, scope)
    ld = k.sem("slot_ld")
    sq_ready, ss_ready, rs_ready, sn_ready, q_ps, q_sb, qk_ps, qf_ready, qh_ready, q_act, q_dve = (
        k.sem(f"sq_{n}") for n in ("sq", "ss", "rs", "sn", "q_ps", "q_sb", "qk_ps", "qf", "qh", "act", "dve"))
    s_ready, nb_ready, exp_done, el_ready, v_ready, pv_done, m_dve = (
        k.sem(f"sm_{n}") for n in ("s", "nb", "exp", "el", "v", "pv", "dve"))
    u_ready, ut_ps, ut_sb, up_ps, up_sb, gate_ps, gates_ready, rh_ready, n_ready, g_dve, g_act = (
        k.sem(f"sg_{n}") for n in ("u", "ut_ps", "ut_sb", "up_ps", "up_sb", "gate_ps", "gates", "rh", "n", "dve", "act"))
    acc = [ps[:, 4 + i // 3, (D + 1) * (i % 3):(D + 1) * (i % 3) + D + 1] for i in range(TT)]

    with nc.Block() as block:
        @block.sync
        def _(sp):
            sp.dma_start(w[:, :], slot_w).then_inc(ld, 16)
            sp.wait_ge(ld, 16)

        @block.scalar
        def _(act):
            act.sem_inc(exp_done, CREDIT)

        @block.tensor
        def _(pe):
            pe.sem_inc(pv_done, CREDIT)

    with nc.Fori(0, NITER) as it:
        with nc.Block() as block:
            @block.scalar
            def _(act):
                act.activation(t[0][:, :], slots[:, :], ACT.Square).then_inc(sq_ready, 1)
                act.wait_ge(ss_ready, it + 1)
                act.activation(t[1][:, :].rearrange("p (h n) -> p h n", h=2), ps[:, 0:2, :], ACT.Ln,
                               bias=k.eps6[:, :]).then_inc(q_act, 1)
                act.wait_ge(q_act, it + 1)
                act.activation(t[2][:, :], t[1][:, :], ACT.Exp, scale=-0.5).then_inc(rs_ready, 1)
                for h in range(2):
                    act.wait_ge(q_ps, it * 2 + h + 1)
                    act.activation(t[1][:, half(h)], ps[:, 2 + h, :], ACT.Copy).then_inc(q_sb, 1)
                for h in range(2):
                    act.wait_ge(qf_ready, it * 2 + h + 1)
                    act.activation(qh[:, half(h)], t[0][:, half(h)], ACT.Copy).then_inc(qh_ready, 1)

            @block.vector
            def _(dve):
                dve.wait_ge(rs_ready, it + 1)
                dve.scalar_tensor_tensor(out=t[3][:, :], in0=slots[:, :], scalar=k.cols[:, C_WSLOT:C_WSLOT + 1],
                                         in1=t[2][:, :], op0=ALU.mult, op1=ALU.mult).then_inc(sn_ready, 1)
                for h in range(2):
                    dve.wait_ge(qk_ps, it * 2 + h + 1)
                    dve.tensor_scalar(t[0][:, half(h)], ps[:, 4 + h, :], k.win_s[:, :], None,
                                      ALU.mult).then_inc(qf_ready, 1)
                for h in range(2):
                    dve.wait_ge(qh_ready, it * 2 + h + 1)
                    dve.tensor_tensor(ql[:, half(h)], t[0][:, half(h)], qh[:, half(h)], ALU.subtract)

            @block.tensor
            def _(pe):
                pe.wait_ge(sq_ready, it + 1)
                for h in range(2):
                    ins = pe.matmul(ps[:, h, :], k.mean_w[:, :], t[0][:, half(h)], start=True, stop=True)
                ins.then_inc(ss_ready, 1)
                pe.wait_ge(sn_ready, it + 1)
                for h in range(2):
                    pe.matmul(ps[:, 2 + h, :], wq, t[3][:, half(h)], start=True, stop=True).then_inc(q_ps, 1)
                for h in range(2):
                    pe.wait_ge(q_sb, it * 2 + h + 1)
                    pe.matmul(ps[:, 4 + h, :], wk, t[1][:, half(h)], start=True, stop=True).then_inc(qk_ps, 1)

        with nc.Block() as block:
            n0 = it * MT

            @block.tensor
            def _(pe):
                def scores(j, b):
                    pe.wait_ge(exp_done, n0 + j + 1)
                    cols_j = bass.ds(j * P, P)
                    for h in range(2):
                        pe.matmul(ps[:, 2 * b + h, :], k.pth[:, cols_j], qh[:, half(h)], start=True, stop=False)
                        pe.matmul(ps[:, 2 * b + h, :], k.pth[:, cols_j], ql[:, half(h)], start=False, stop=False)
                        ins = pe.matmul(ps[:, 2 * b + h, :], k.ptl[:, cols_j], qh[:, half(h)], start=False, stop=True)
                    ins.then_inc(s_ready, 1)

                def values(j, b):
                    pe.wait_ge(v_ready, n0 + j + 1)
                    pe.wait_ge(el_ready, n0 + j + 1)
                    for i in range(TT):
                        eh = top(k.e[:, b, tile(i)])
                        pe.matmul(acc[i], eh, vh[:, b, :], start=False, stop=False, skip_group_check=True)
                        pe.matmul(acc[i], eh, vl[:, b, :], start=False, stop=False, skip_group_check=True)
                        ins = pe.matmul(acc[i], k.el[:, b, tile(i)], vh[:, b, :], start=False, stop=False,
                                        skip_group_check=True)
                    ins.then_inc(pv_done, 1)

                for n in range(3):
                    pe.matmul(ps[:, 4 + n, :], k.zero_h[:, 0:P], k.zero_h[:, :], start=True, stop=False,
                              skip_group_check=True)
                scores(0, 0)
                with pe.Fori(0, MT // 2 - 1) as i:
                    scores(i * 2 + 1, 1)
                    values(i * 2, 0)
                    scores(i * 2 + 2, 0)
                    values(i * 2 + 1, 1)
                scores(MT - 1, 1)
                values(MT - 2, 0)
                values(MT - 1, 1)

            @block.scalar
            def _(act):
                with act.Fori(0, MT // 2) as i:
                    for b in range(2):
                        j = i * 2 + b
                        act.wait_ge(nb_ready, n0 + j + 1)
                        act.wait_ge(pv_done, n0 + j + 1)
                        act.activation(k.e[:, b, :].rearrange("p (h n) -> p h n", h=2), ps[:, 2 * b:2 * b + 2, :],
                                       ACT.Exp, bias=nb[:, b, :], accum_out=sums[:, b, :]).then_inc(exp_done, 1)

            @block.gpsimd
            def _(pool):
                with pool.Fori(0, MT // 2) as i:
                    for b in range(2):
                        j = i * 2 + b
                        pool.wait_ge(exp_done, n0 + j + 1 + CREDIT)
                        pool.wait_ge(pv_done, n0 + j + 1)
                        pool.tensor_tensor(k.el[:, b, :], k.e[:, b, :], top(k.e[:, b, :]),
                                           ALU.subtract).then_inc(el_ready, 1)

            @block.vector
            def _(dve):
                STEPS = 4

                def shift(j, b):
                    dve.wait_ge(s_ready, n0 + j + 1)
                    dve.tensor_reduce(mx[:, b, :], ps[:, 2 * b:2 * b + 2, :], AX.XY, ALU.max).then_inc(m_dve, 1)

                def bias(j, b, n):
                    dve.wait_ge(m_dve, n)
                    dve.tensor_scalar(nb[:, b, :], mx[:, b, :], -1.0, LIFT, ALU.mult, ALU.add).then_inc(nb_ready, 1)

                def scaled(j, b, n):
                    dve.wait_ge(exp_done, n0 + j + 1 + CREDIT)
                    dve.reciprocal(rec[:, b, 0:1], sums[:, b, :]).then_inc(m_dve, 1)
                    dve.wait_ge(m_dve, n + 1)
                    dve.tensor_scalar(rec[:, b, 1:2], rec[:, b, 0:1], VAL_SCALE, None, ALU.mult).then_inc(m_dve, 1)
                    dve.wait_ge(m_dve, n + 2)
                    dve.wait_ge(pv_done, n0 + j + 1)
                    dve.tensor_scalar(vh[:, b, :], k.pn[:, j, :], rec[:, b, 1:2], None, ALU.mult).then_inc(m_dve, 1)
                    dve.wait_ge(m_dve, n + 3)
                    dve.scalar_tensor_tensor(out=vl[:, b, :], in0=k.pn[:, j, :], scalar=rec[:, b, 1:2],
                                             in1=vh[:, b, :], op0=ALU.mult, op1=ALU.subtract).then_inc(v_ready, 1)

                base = it * (MT * STEPS)
                shift(0, 0)
                bias(0, 0, base + 1)
                with dve.Fori(0, MT // 2 - 1) as i:
                    n = base + i * (2 * STEPS) + 1
                    shift(i * 2 + 1, 1)
                    bias(i * 2 + 1, 1, n + 1)
                    scaled(i * 2, 0, n + 1)
                    shift(i * 2 + 2, 0)
                    bias(i * 2 + 2, 0, n + 5)
                    scaled(i * 2 + 1, 1, n + 5)
                n = base + (MT // 2 - 1) * 2 * STEPS + 1
                shift(MT - 1, 1)
                bias(MT - 1, 1, n + 1)
                scaled(MT - 2, 0, n + 1)
                scaled(MT - 1, 1, n + 4)

        with nc.Block() as block:
            r, z, hn_r, n_t, u_t = t[0], t[1], t[2], t[3], t[4]

            @block.vector
            def _(dve):
                chain = Chain(dve, g_dve, it * 5)
                for n in range(3):
                    m = min(3, TT - 3 * n)
                    sums_n = ps[:, 4 + n, 0:m * (D + 1)].rearrange("p (i d) -> p i d", d=D + 1)[:, :, D]
                    ins = dve.tensor_scalar(den[:, 0, 3 * n:3 * n + m], sums_n, SLOT_EPS * VAL_SCALE, None, ALU.add)
                chain(ins)
                chain(dve.reciprocal(den[:, 1, :], den[:, 0, :]))
                for i in range(TT):
                    dve.tensor_scalar(t[3][:, tile(i)], acc[i][:, 0:D], den[:, 1, i:i + 1], None,
                                      ALU.mult).then_inc(u_ready, 1)
                dve.wait_ge(gates_ready, it + 1)
                chain(dve.scalar_tensor_tensor(out=hn_r[:, :].rearrange("p (h n) -> p h n", h=2), in0=ps[:, 6:8, :],
                                               scalar=k.cols[:, C_BHN:C_BHN + 1],
                                               in1=r[:, :].rearrange("p (h n) -> p h n", h=2),
                                               op0=ALU.add, op1=ALU.mult))
                dve.tensor_tensor(hn_r[:, :].rearrange("p (h n) -> p h n", h=2), ps[:, 4:6, :],
                                  hn_r[:, :].rearrange("p (h n) -> p h n", h=2), ALU.add).then_inc(rh_ready, 1)
                dve.wait_ge(n_ready, it + 1)
                chain(dve.tensor_tensor(hn_r[:, :], slots[:, :], n_t[:, :], ALU.subtract))
                chain(dve.tensor_tensor(hn_r[:, :], hn_r[:, :], z[:, :], ALU.mult))
                dve.tensor_tensor(slots[:, :], n_t[:, :], hn_r[:, :], ALU.add)

            @block.tensor
            def _(pe):
                for i in range(TT):
                    pe.wait_ge(u_ready, it * TT + i + 1)
                    ins = pe.transpose(ps[:, i // 4, tile(i % 4)], t[3][:, tile(i)], k.ident[:, :])
                    if i % 4 == 3:
                        ins.then_inc(ut_ps, 1)
                for h in range(2):
                    pe.wait_ge(ut_sb, it * 2 + h + 1)
                    pe.matmul(ps[:, 2 + h, :], wv, u_t[:, half(h)], start=True, stop=True).then_inc(up_ps, 1)
                pe.wait_ge(up_sb, it * 2 + 2)
                for h in range(2):
                    pe.matmul(ps[:, 4 + h, :], wih[2], t[2][:, half(h)], start=True, stop=True)
                    pe.matmul(ps[:, 6 + h, :], whh[2], slots[:, half(h)], start=True, stop=True)
                    for n in range(2):
                        pe.matmul(ps[:, 2 * n + h, :], wih[n], t[2][:, half(h)], start=True, stop=False)
                        ins = pe.matmul(ps[:, 2 * n + h, :], whh[n], slots[:, half(h)], start=False, stop=True)
                    ins.then_inc(gate_ps, 1)

            @block.scalar
            def _(act):
                for h in range(2):
                    act.wait_ge(ut_ps, it * 2 + h + 1)
                    act.activation(u_t[:, half(h)], ps[:, h, :], ACT.Copy,
                                   scale=k.cols[:, C_WIN:C_WIN + 1]).then_inc(ut_sb, 1)
                for h in range(2):
                    act.wait_ge(up_ps, it * 2 + h + 1)
                    act.activation(t[2][:, half(h)], ps[:, 2 + h, :], ACT.Copy).then_inc(up_sb, 1)
                act.wait_ge(gate_ps, it * 2 + 2)
                act.activation(r[:, :].rearrange("p (h n) -> p h n", h=2), ps[:, 0:2, :], ACT.Sigmoid,
                               bias=k.bsum[:, 0:1])
                act.activation(z[:, :].rearrange("p (h n) -> p h n", h=2), ps[:, 2:4, :], ACT.Sigmoid,
                               bias=k.bsum[:, 1:2]).then_inc(gates_ready, 1)
                act.wait_ge(rh_ready, it + 1)
                act.activation(n_t[:, :], hn_r[:, :], ACT.Tanh, bias=k.cols[:, C_BIN:C_BIN + 1]).then_inc(n_ready, 1)

    residual(k, "slot_res", slots, 0)


def widen(k, scope, tag, cwt, weigh):
    nc, ps = k.nc, k.ps
    turned, hi_ready = k.sem(f"{tag}_turned"), k.sem(f"{tag}_hi")
    with nc.Block() as block:
        @block.tensor
        def _(pe):
            for i in range(TT):
                ins = pe.transpose(ps[:, i // 4, tile(i % 4)], weigh[:, i, :], k.ident[:, :])
            ins.then_inc(turned, 1)

        @block.scalar
        def _(act):
            act.wait_ge(turned, 1)
            act.activation(cwt[:, 0, :].rearrange("p (h n) -> p h n", h=2), ps[:, 0:2, :], ACT.Copy).then_inc(hi_ready, 1)

        @block.vector
        def _(dve):
            dve.wait_ge(hi_ready, 1)
            dve.tensor_tensor(cwt[:, 1, :].rearrange("p (h n) -> p h n", h=2), ps[:, 0:2, :],
                              cwt[:, 0, :].rearrange("p (h n) -> p h n", h=2), ALU.subtract)


def top_experts(k, scope, cwt):
    nc, ps = k.nc, k.ps
    biased = k.sb("top_biased", [P, TT, E0], FP32, scope)
    rest = k.sb("top_rest", [P, TT, E0], FP32, scope)
    sig = k.sb("top_sig", [P, TT, E0], FP32, scope)
    best = k.sb("top_best", [P, TT, 8], FP32, scope)
    total = k.sb("top_total", [P, 2, TT], FP32, scope)
    weigh = k.sb("top_weigh", [P, TT, P], FP32, scope)
    aff_ready, e_ready, w_zero, d_ch, best_done = (k.sem(f"top_{n}") for n in ("aff", "exp", "zero", "dve", "best"))
    aff = ps[:, 0, :].rearrange("p (i e) -> p i e", e=E0)
    with nc.Block() as block:
        @block.tensor
        def _(pe):
            for i in range(TT):
                ins = pe.matmul(aff[:, i, :], k.xt[:, tile(i)], k.cent[:, :], start=True, stop=True)
            ins.then_inc(aff_ready, 1)

        @block.scalar
        def _(act):
            act.wait_ge(d_ch, 1)
            act.activation(sig[:, :, :], aff, ACT.Exp, scale=-1.0).then_inc(e_ready, 1)

        @block.gpsimd
        def _(pool):
            pool.memset(weigh[:, :, :], 0.0).then_inc(w_zero, 1)
            pool.wait_ge(w_zero, 1)
            pool.memset(weigh[:, :, E0], 1.0).then_inc(w_zero, 1)

        @block.vector
        def _(dve):
            chain = Chain(dve, d_ch)
            dve.wait_ge(aff_ready, 1)
            chain(dve.tensor_tensor(biased[:, :, :], aff, k.bias_e[:, :].unsqueeze(1).to_broadcast([P, TT, E0]), ALU.add))
            for i in range(TT):
                dve.max(best[:, i, :], biased[:, i, :]).then_inc(best_done, 1)
            for i in range(TT):
                dve.wait_ge(best_done, i + 1)
                ins = dve.match_replace(rest[:, i, :], best[:, i, :], biased[:, i, :], -3.0e38)
            chain(ins)
            chain(dve.tensor_tensor(rest[:, :, :], rest[:, :, :], biased[:, :, :], ALU.not_equal))
            dve.wait_ge(e_ready, 1)
            chain(dve.tensor_scalar(sig[:, :, :], sig[:, :, :], 1.0, None, ALU.add))
            chain(dve.reciprocal(sig[:, :, :], sig[:, :, :]))
            chain(dve.tensor_tensor(sig[:, :, :], sig[:, :, :], rest[:, :, :], ALU.mult))
            chain(dve.tensor_reduce(total[:, 0, :], sig[:, :, :], AX.X, ALU.add))
            chain(dve.tensor_scalar(total[:, 0, :], total[:, 0, :], 1e-8, None, ALU.add))
            chain(dve.reciprocal(total[:, 1, :], total[:, 0, :]))
            dve.wait_ge(w_zero, 2)
            dve.tensor_tensor(weigh[:, :, 0:E0], sig[:, :, :],
                              total[:, 1, :].unsqueeze(2).to_broadcast([P, TT, E0]), ALU.mult)

    widen(k, scope, "top", cwt, weigh)


def soft_experts(k, scope, cwt):
    nc, ps = k.nc, k.ps
    logit = k.sb("soft_logit", [P, TT, 2, E1], FP32, scope)
    prob = k.sb("soft_prob", [P, TT, 2, E1], FP32, scope)
    mx = k.sb("soft_mx", [P, TT, 2], FP32, scope)
    total = k.sb("soft_total", [P, 2, TT, 2], FP32, scope)
    cw = k.sb("soft_cw", [P, TT, E1], FP32, scope)
    cs = k.sb("soft_cs", [P, 2, TT], FP32, scope)
    weigh = k.sb("soft_weigh", [P, TT, P], FP32, scope)
    lg_ready, x_ready, e_ready, w_zero, d_ch = (k.sem(f"soft_{n}") for n in ("lg", "x", "exp", "zero", "dve"))
    lg = ps[:, 0, 0:TT * 2 * E1].rearrange("p (i g e) -> p i g e", g=2, e=E1)
    with nc.Block() as block:
        @block.tensor
        def _(pe):
            for i in range(TT):
                ins = pe.matmul(ps[:, 0, 2 * E1 * i:2 * E1 * (i + 1)], k.xt[:, tile(i)], k.rout[:, :],
                                start=True, stop=True)
            ins.then_inc(lg_ready, 1)

        @block.scalar
        def _(act):
            act.wait_ge(x_ready, 1)
            act.activation(prob[:, :, 0, :], logit[:, :, 0, :], ACT.Exp)
            act.activation(prob[:, :, 1, :], logit[:, :, 1, :], ACT.Exp, scale=10.0).then_inc(e_ready, 1)

        @block.gpsimd
        def _(pool):
            pool.memset(weigh[:, :, :], 0.0).then_inc(w_zero, 1)

        @block.vector
        def _(dve):
            chain = Chain(dve, d_ch)
            dve.wait_ge(lg_ready, 1)
            chain(dve.tensor_reduce(mx[:, :, :], lg, AX.X, ALU.max))
            dve.tensor_tensor(logit[:, :, :, :], lg, mx[:, :, :].unsqueeze(3).to_broadcast([P, TT, 2, E1]),
                              ALU.subtract).then_inc(x_ready, 1)
            dve.wait_ge(e_ready, 1)
            chain(dve.tensor_reduce(total[:, 0, :, :], prob[:, :, :, :], AX.X, ALU.add))
            chain(dve.reciprocal(total[:, 1, :, :], total[:, 0, :, :]))
            chain(dve.tensor_tensor(prob[:, :, :, :], prob[:, :, :, :],
                                    total[:, 1, :, :].unsqueeze(3).to_broadcast([P, TT, 2, E1]), ALU.mult))
            chain(dve.tensor_tensor(cw[:, :, :], prob[:, :, 0, :], prob[:, :, 1, :], ALU.mult))
            chain(dve.tensor_reduce(cs[:, 0, :], cw[:, :, :], AX.X, ALU.add))
            chain(dve.tensor_scalar(cs[:, 0, :], cs[:, 0, :], 1e-9, None, ALU.add))
            chain(dve.reciprocal(cs[:, 1, :], cs[:, 0, :]))
            dve.wait_ge(w_zero, 1)
            dve.tensor_tensor(weigh[:, :, 0:E1], cw[:, :, :], cs[:, 1, :].unsqueeze(2).to_broadcast([P, TT, E1]),
                              ALU.mult)

    widen(k, scope, "soft", cwt, weigh)


def experts(k, scope, tag, cwt, w_dram, gate):
    nc, ps = k.nc, k.ps
    gated = w_dram.shape[2] == 3 * P
    nch = w_dram.shape[0]
    nw = w_dram.shape[2] // P
    STEP = CPE if gated else 3
    npick = E1 if gated else CH0
    RAW = 4
    pick = k.sb(f"{tag}_pick", [P, npick, P], FP16, scope)
    raw = k.sb(f"{tag}_raw", [P, RAW, nw * P], FP32, scope)
    wh = k.sb(f"{tag}_wh", [P, 2, nw * P], FP16, scope)
    wl = k.sb(f"{tag}_wl", [P, 2, nw * P], FP16, scope)
    inner = k.sb(f"{tag}_inner", [P, 2, 512], FP32, scope)
    a = k.sb(f"{tag}_a", [P, 2, 512], FP32, scope)
    ah = k.sb(f"{tag}_ah", [P, 2, 512], FP16, scope)
    al = k.sb(f"{tag}_al", [P, 2, 512], FP16, scope)
    y = k.sb(f"{tag}_y", [P, T], FP32, scope)
    ld = [k.sem(f"{tag}_ld{n}") for n in range(RAW)]
    wh_ready, wl_ready, up_ready, in_ready, a_ready, ah_ready, al_ready, down_done, pk, y_ready, m_ready, d_ch = (
        k.sem(f"{tag}_{n}") for n in ("wh", "wl", "up", "in", "a", "ah", "al", "down", "pick", "y", "m", "dve"))
    down_w = slice((nw - 1) * P, nw * P)
    SPREAD = 4 if gated else 2
    BODIES = nch // STEP
    assert nch % STEP == 0

    with nc.Block() as block:
        @block.gpsimd
        def _(pool):
            pool.memset(pick[:, :, :], 0.0).then_inc(pk, 1)
            pool.wait_ge(pk, 1)
            if gated:
                pat, view = [[-1, npick], [0, P]], pick[:, :, :]
            else:
                pat = [[-2, npick], [-1, 2], [0, F0]]
                view = pick[:, :, :].rearrange("p c (e f) -> p c e f", e=2)
            pool.affine_select(out=view, in_=view, compare_op=ALU.not_equal, fill=1.0, base=0, pattern=pat,
                               channel_multiplier=1)

        @block.tensor
        def _(pe):
            pe.sem_inc(down_done, CREDIT)

        @block.vector
        def _(dve):
            dve.sem_inc(a_ready, CREDIT)

    with nc.Block() as block:
        def bodies(eng, body):
            with eng.Fori(0, BODIES) as i:
                for s in range(STEP):
                    body(i * STEP + s, s)

        @block.sync
        def _(sp):
            def load(c, r):
                sp.dma_start(raw[:, r, :], w_dram[c]).then_inc(ld[r], 16)

            for c in range(RAW):
                load(c, c)
            with sp.Fori(1, nch // RAW) as i:
                for r in range(RAW):
                    sp.wait_ge(wl_ready, (i - 1) * RAW + r + 1)
                    sp.dma_start(raw[:, r, :], w_dram[bass.ds(i * RAW + r, 1)].rearrange("c p n -> (c p) n")).then_inc(ld[r], 16)
            for c in range(nch // RAW * RAW, nch):
                sp.wait_ge(wl_ready, c - RAW + 1)
                load(c, c % RAW)
            for r in range(RAW):
                sp.wait_ge(ld[r], 16 * ((nch - 1 - r) // RAW + 1))

        def split_loop(eng, weights, halves):
            weights(0, 0, 16)
            n = (nch - 1) // RAW
            with eng.Fori(0, n) as i:
                for r in range(RAW):
                    weights(i * RAW + r + 1, (r + 1) % RAW, i * 16 + 16 * (1 + (r + 1) // RAW))
                    halves(i * RAW + r)
            for c in range(n * RAW, nch):
                if c + 1 < nch:
                    weights(c + 1, (c + 1) % RAW, 16 * ((c + 1) // RAW + 1))
                halves(c)

        @block.gpsimd
        def _(pool):
            def low(c, r, loaded):
                pool.wait_ge(wh_ready, c + 1)
                pool.tensor_tensor(wl[:, r % 2, :], raw[:, r, :], wh[:, r % 2, :], ALU.subtract).then_inc(wl_ready, 1)

            def halves(c):
                for h in range(2):
                    n = c * 2 + h
                    pool.wait_ge(ah_ready, n + 1)
                    pool.wait_ge(down_done, n + 1)
                    pool.tensor_tensor(al[:, h, :], a[:, h, :], ah[:, h, :], ALU.subtract).then_inc(al_ready, 1)

            split_loop(pool, low, halves)

        @block.scalar
        def _(act):
            def high(c, r, loaded):
                act.wait_ge(ld[r], loaded)
                act.wait_ge(down_done, c * 2)
                act.activation(wh[:, r % 2, :], raw[:, r, :], ACT.Copy).then_inc(wh_ready, 1)

            def halves(c):
                for h in range(2):
                    n = c * 2 + h
                    act.wait_ge(up_ready, n + 1)
                    act.wait_ge(a_ready, n + 1)
                    act.activation(inner[:, h, :], ps[:, h, :], ACT.Silu).then_inc(in_ready, 1)
                for h in range(2):
                    n = c * 2 + h
                    act.wait_ge(a_ready, n + 1 + CREDIT)
                    act.wait_ge(down_done, n + 1)
                    act.activation(ah[:, h, :], a[:, h, :], ACT.Copy).then_inc(ah_ready, 1)

            split_loop(act, high, halves)
            act.wait_ge(down_done, 2 * nch + CREDIT)
            act.activation(y[:, :].rearrange("p (h n) -> p h n", h=2), ps[:, 6:8, :], ACT.Copy)

        @block.vector
        def _(dve):
            def weigh(c, s):
                for h in range(2):
                    n = c * 2 + h
                    dve.wait_ge(in_ready, n + 1)
                    if gated:
                        dve.tensor_tensor(inner[:, h, :], inner[:, h, :], ps[:, 2 + h, :], ALU.mult).then_inc(m_ready, 1)
                        dve.wait_ge(m_ready, n + 1)
                    dve.wait_ge(down_done, n + 1)
                    dve.tensor_tensor(a[:, h, :], inner[:, h, :], ps[:, SPREAD + h, :], ALU.mult).then_inc(a_ready, 1)
            bodies(dve, weigh)

        @block.tensor
        def _(pe):
            def product(bank, w, h, first, last):
                b = w[0]
                pe.matmul(ps[:, bank, :], wh[:, b, w[1]], k.xth[:, half(h)], start=True, stop=False)
                pe.matmul(ps[:, bank, :], wh[:, b, w[1]], k.xtl[:, half(h)], start=False, stop=False)
                return pe.matmul(ps[:, bank, :], wl[:, b, w[1]], k.xth[:, half(h)], start=False, stop=True)

            def up(c, b, pick_at):
                pe.wait_ge(wl_ready, c + 1)
                for h in range(2):
                    pe.wait_ge(a_ready, c * 2 + h + 1)
                    for m in range(nw - 1):
                        product(2 * m + h, (b, slice(m * P, m * P + P)), h, True, True)
                    pe.matmul(ps[:, SPREAD + h, :], pick[:, pick_at, :], cwt[:, 0, half(h)], start=True, stop=False)
                    pe.matmul(ps[:, SPREAD + h, :], pick[:, pick_at, :], cwt[:, 1, half(h)], start=False,
                              stop=True).then_inc(up_ready, 1)

            def down(c, b):
                for h in range(2):
                    pe.wait_ge(al_ready, c * 2 + h + 1)
                    pe.matmul(ps[:, 6 + h, :], wh[:, b, down_w], ah[:, h, :], start=False, stop=False, skip_group_check=True)
                    pe.matmul(ps[:, 6 + h, :], wl[:, b, down_w], ah[:, h, :], start=False, stop=False, skip_group_check=True)
                    pe.matmul(ps[:, 6 + h, :], wh[:, b, down_w], al[:, h, :], start=False, stop=False,
                              skip_group_check=True).then_inc(down_done, 1)

            for h in range(2):
                pe.matmul(ps[:, 6 + h, :], k.zero_h[:, 0:P], k.zero_h[:, :], start=True, stop=False,
                          skip_group_check=True)

            def at(c):
                return c // CPE if gated else c

            up(0, 0, at(0))
            if gated:
                with pe.Fori(0, E1 - 1) as i:
                    for s in range(CPE):
                        up(i * CPE + s + 1, (s + 1) % 2, i + (s + 1) // CPE)
                        down(i * CPE + s, s % 2)
                for c in range(nch - CPE, nch - 1):
                    up(c + 1, (c + 1) % 2, at(c + 1))
                    down(c, c % 2)
            else:
                with pe.Fori(0, (nch - 1) // 2) as i:
                    for s in range(2):
                        up(i * 2 + s + 1, (s + 1) % 2, i * 2 + s + 1)
                        down(i * 2 + s, s % 2)
            down(nch - 1, (nch - 1) % 2)

    residual(k, f"{tag}_res", y, gate)


def cross_attention(k, scope, wq1, wkv1, wo1):
    nc, ps = k.nc, k.ps
    QUSES, GUSES = 2, 2 + 2 * GT
    USES = QUSES + G * GUSES + 2
    ka, kb = (k.sb(n, [P, 2, MP], FP16, scope) for n in ("keys_a", "keys_b"))
    v = k.sb("values", [P, 2, MT, 2 * DH + 1], FP16, scope)
    qa, qb = (k.sb(n, [P, 2, T], FP16, scope) for n in ("q_a", "q_b"))
    wqh, wql, wkh, wkl = (k.sb(n, [P, HEADS * P], FP16, scope) for n in ("wq_h", "wq_l", "wk_h", "wk_l"))
    wvh, wvl = (k.sb(n, [P, HEADS * DH], FP16, scope) for n in ("wv_h", "wv_l"))
    vt = k.sb("v_tmp", [P, GT, DH], FP32, scope)
    runmax = k.sb("run_max", [P, TT, G], FP32, scope)
    cmax = k.sb("c_max", [P, TT], FP32, scope)
    cz = k.sb("c_spread", [P, TT, P], FP16, scope)
    rec = k.sb("o_rec", [P, 2, GT], FP32, scope)
    att = k.sb("att_rows", [P, 2, GT, HEADS * DH], FP32, scope)
    acc = ps[:, 4:6, 0:GT * (DH + 1)].rearrange("p a (i d) -> p a i d", d=DH + 1)

    ld_w, h_ready, w_ch = k.sem("a1_ldw"), k.sem("a1_wh"), k.sem("a1_wch")
    with ExitStack() as ws:
        w = att[:, :, :, :].rearrange("p a i d -> p (a i d)")[:, 0:3 * HEADS * DH]
        with nc.Block() as block:
            @block.sync
            def _(sp):
                sp.dma_start(w[:, 0:HEADS * DH], wq1).then_inc(ld_w, 16)
                sp.dma_start(w[:, HEADS * DH:3 * HEADS * DH], wkv1).then_inc(ld_w, 16)

            @block.scalar
            def _(act):
                act.wait_ge(ld_w, 32)
                for n, hi in ((0, wqh), (1, wkh)):
                    src = w[:, n * HEADS * DH:(n + 1) * HEADS * DH].rearrange("p (h d) -> p h d", d=DH)
                    for s in range(2):
                        act.activation(hi[:, :].rearrange("p (h s d) -> p h s d", s=2, d=DH)[:, :, s, :], src,
                                       ACT.Copy).then_inc(h_ready, 1)
                act.activation(wvh[:, :], w[:, 2 * HEADS * DH:3 * HEADS * DH], ACT.Copy).then_inc(h_ready, 1)

            @block.vector
            def _(dve):
                dve.wait_ge(h_ready, 5)
                for n, hi, lo in ((0, wqh, wql), (1, wkh, wkl)):
                    src = w[:, n * HEADS * DH:(n + 1) * HEADS * DH].rearrange("p (h d) -> p h d", d=DH)
                    for s in range(2):
                        at = [x[:, :].rearrange("p (h s d) -> p h s d", s=2, d=DH)[:, :, s, :] for x in (lo, hi)]
                        dve.tensor_tensor(at[0], src, at[1], ALU.subtract)
                dve.tensor_tensor(wvl[:, :], w[:, 2 * HEADS * DH:3 * HEADS * DH], wvh[:, :], ALU.subtract)
                for b in range(2):
                    dve.tensor_copy(v[:, b, :, DH], k.mask[:, :])
                dve.wait_ge(w_ch, 2)
                for b in range(2):
                    dve.memset(kb[DH:DH + 1, b, :], 1.0)

            @block.gpsimd
            def _(pool):
                for b in range(2):
                    pool.memset(qb[DH:P, b, :], 0.0)
                    pool.memset(kb[DH:P, b, :], 0.0).then_inc(w_ch, 1)
                pool.wait_ge(w_ch, 2)
                pool.memset(cz[:, :, :], 0.0)

    side_ready, side_free, qc_ready, kc_ready, v_made, p_dve, c_ready, cu_ready, side_dve = (
        k.sem(f"ap_{n}") for n in ("side_ready", "side_free", "qc", "kc", "v", "dve", "c", "cu", "sdve"))
    s_ready, exp_done, el_ready, pv_done, o_free, o_dve = (
        k.sem(f"am_{n}") for n in ("s", "exp", "el", "pv", "o_free", "odve"))

    with nc.Block() as block:
        @block.scalar
        def _(act):
            act.sem_inc(exp_done, CREDIT)

        @block.tensor
        def _(pe):
            pe.sem_inc(pv_done, CREDIT)

        @block.vector
        def _(dve):
            dve.sem_inc(side_free, CREDIT)
            dve.sem_inc(o_free, 1)

    with nc.Block() as block:
        def walk(eng, start, group, stop):
            def run(h, hb, n, nb):
                if start:
                    start(h, hb, n, nb)
                with eng.Fori(0, G - 1) as g:
                    group(h, hb, n, nb, g, False)
                group(h, hb, n, nb, G - 1, True)
                if stop:
                    stop(h, hb, n, nb)
            run(None, 1, 0, 0)
            with eng.Fori(0, HEADS // 2 - 1) as hp:
                run(hp * 2, 0, hp * 2 + 1, 1)
                run(hp * 2 + 1, 1, hp * 2 + 2, 0)
            run(HEADS - 2, 0, HEADS - 1, 1)
            run(HEADS - 1, 1, None, 0)

        @block.tensor
        def _(pe):
            def side(use, bank, products, inc=True):
                pe.wait_ge(side_free, use + 1)
                for n, (o, l, r, first, last) in enumerate(products):
                    ins = pe.matmul(o, l, r, start=first, stop=last)
                ins.then_inc(side_ready, 1)

            def scores(h, hb, j, b):
                pe.wait_ge(exp_done, h * MT + j + 1)
                at = bass.ds(j * P, P)
                for n in range(2):
                    pe.matmul(ps[:, 2 * b + n, :], ka[:, hb, at], qa[:, hb, half(n)], start=True, stop=False)
                    ins = pe.matmul(ps[:, 2 * b + n, :], kb[:, hb, at], qb[:, hb, half(n)], start=False, stop=True)
                ins.then_inc(s_ready, 1)

            def values(h, hb, j, b):
                pe.wait_ge(el_ready, h * MT + j + 1)
                for i in range(TT):
                    o = acc[:, i // GT, i % GT, :]
                    eh = top(k.e[:, b, tile(i)])
                    pe.matmul(o, eh, v[:, hb, j, 0:DH + 1], start=False, stop=False, skip_group_check=True)
                    pe.matmul(o[:, 0:DH], eh, v[:, hb, j, DH + 1:2 * DH + 1], start=False, stop=False, skip_group_check=True)
                    ins = pe.matmul(o, k.el[:, b, tile(i)], v[:, hb, j, 0:DH + 1], start=False, stop=False,
                                    skip_group_check=True)
                ins.then_inc(pv_done, 1)

            def start(h, hb, n, nb):
                if h is not None:
                    pe.wait_ge(cu_ready, h + 1)
                    pe.wait_ge(o_free, h + 1)
                    for c in range(2):
                        pe.matmul(ps[:, 4 + c, :], k.zero_h[:, 0:P], k.zero_h[:, :], start=True, stop=False,
                                  skip_group_check=True)
                    scores(h, hb, 0, 0)
                if n is not None:
                    at = bass.ds(n * P, P)
                    for c in range(2):
                        o = ps[:, 6 + c, :]
                        side(n * USES + c, c, [(o, wqh[:, at], k.xth[:, half(c)], True, False),
                                               (o, wqh[:, at], k.xtl[:, half(c)], False, False),
                                               (o, wql[:, at], k.xth[:, half(c)], False, True)])

            def group(h, hb, n, nb, g, last):
                if n is not None:
                    use = n * USES + QUSES + g * GUSES
                    at, cols_g = bass.ds(n * P, P), bass.ds(g * 512, 512)
                    o = ps[:, 6, :]
                    side(use, 0, [(o, wkh[:, at], k.ch[:, cols_g], True, False),
                                  (o, wkh[:, at], k.cl[:, cols_g], False, False),
                                  (o, wkl[:, at], k.ch[:, cols_g], False, True)])
                    prods = []
                    for u in range(GT):
                        o = ps[:, 7, DH * u:DH * u + DH]
                        rows = bass.ds(g * 512 + u * P, P)
                        wat = bass.ds(n * DH, DH)
                        prods += [(o, k.ch[:, rows], wvh[:, wat], True, False),
                                  (o, k.ch[:, rows], wvl[:, wat], False, False),
                                  (o, k.cl[:, rows], wvh[:, wat], False, True)]
                    side(use + 1, 1, prods)
                for u in range(GT):
                    if h is not None:
                        if not (last and u == GT - 1):
                            scores(h, hb, g * GT + u + 1, (u + 1) % 2)
                        values(h, hb, g * GT + u, u % 2)
                    if n is not None:
                        if u == 0:
                            pe.wait_ge(kc_ready, n * (2 * G) + g * 2 + 2)
                        for c in range(2):
                            i = 2 * u + c
                            side(use + 2 + i, c, [(ps[:, 6 + c, :], qa[:, nb, tile(i)], ka[:, nb, cols_g], True, True)])

            def stop(h, hb, n, nb):
                if n is not None:
                    pe.wait_ge(c_ready, n + 1)
                    for c in range(2):
                        side(n * USES + USES - 2 + c, c,
                             [(ps[:, 6 + c, tile(i)], cz[:, 4 * c + i, :], k.ident_h[:, :], True, True) for i in range(4)])

            walk(pe, start, group, stop)

        @block.scalar
        def _(act):
            def start(h, hb, n, nb):
                if n is not None:
                    for c in range(2):
                        act.wait_ge(side_ready, n * USES + c + 1)
                        act.activation(qa[:, nb, half(c)], ps[:, 6 + c, :], ACT.Copy, scale=HEAD_SCALE).then_inc(qc_ready, 1)

            def group(h, hb, n, nb, g, last):
                if n is not None:
                    act.wait_ge(side_ready, n * USES + QUSES + g * GUSES + 1)
                    act.activation(kb[0:DH, nb, bass.ds(g * 512, 512)], ps[0:DH, 6, :], ACT.Copy)
                    act.activation(ka[:, nb, bass.ds(g * 512, 512)], ps[:, 6, :], ACT.Copy).then_inc(kc_ready, 1)
                if h is not None:
                    for u in range(GT):
                        j, b = g * GT + u, u % 2
                        act.wait_ge(s_ready, h * MT + j + 1)
                        act.wait_ge(pv_done, h * MT + j + 1)
                        act.activation(k.e[:, b, :].rearrange("p (h n) -> p h n", h=2), ps[:, 2 * b:2 * b + 2, :],
                                       ACT.Exp).then_inc(exp_done, 1)

            walk(act, start, group, None)

        @block.gpsimd
        def _(pool):
            def group(h, hb, n, nb, g, last):
                if h is not None:
                    for u in range(GT):
                        j, b = g * GT + u, u % 2
                        pool.wait_ge(exp_done, h * MT + j + 1 + CREDIT)
                        pool.wait_ge(pv_done, h * MT + j + 1)
                        pool.tensor_tensor(k.el[:, b, :], k.e[:, b, :], top(k.e[:, b, :]),
                                           ALU.subtract).then_inc(el_ready, 1)

            walk(pool, None, group, None)

        @block.vector
        def _(dve):
            def start(h, hb, n, nb):
                if n is not None:
                    for c in range(2):
                        dve.wait_ge(qc_ready, n * 2 + c + 1)
                        dve.scalar_tensor_tensor(out=qb[0:DH, nb, half(c)], in0=ps[0:DH, 6 + c, :], scalar=HEAD_SCALE,
                                                 in1=qa[0:DH, nb, half(c)], op0=ALU.mult,
                                                 op1=ALU.subtract).then_inc(side_free, 1)

            def group(h, hb, n, nb, g, last):
                if n is None:
                    return
                use = n * USES + QUSES + g * GUSES
                cols_g = bass.ds(g * 512, 512)
                dve.wait_ge(kc_ready, n * (2 * G) + g * 2 + 1)
                ins = dve.tensor_tensor(ka[DH:P, nb, cols_g], ps[DH:P, 6, :], ka[DH:P, nb, cols_g], ALU.subtract)
                ins.then_inc(side_free, 1)
                dve.wait_ge(side_free, use + 1 + CREDIT)
                dve.sem_inc(kc_ready, 1)
                dve.wait_ge(side_ready, use + 2)
                dve.tensor_tensor(vt[:, :, :], ps[:, 7, 0:GT * DH].rearrange("p (u d) -> p u d", d=DH),
                                  k.mask[:, bass.ds(g * GT, GT)].unsqueeze(2).to_broadcast([P, GT, DH]),
                                  ALU.mult).then_inc(side_free, 1)
                dve.wait_ge(side_free, use + 2 + CREDIT)
                rows = bass.ds(g * GT, GT)
                dve.tensor_copy(v[:, nb, rows, 0:DH], vt[:, :, :]).then_inc(p_dve, 1)
                dve.wait_ge(p_dve, n * G + g + 1)
                dve.tensor_tensor(v[:, nb, rows, DH + 1:2 * DH + 1], vt[:, :, :], v[:, nb, rows, 0:DH],
                                  ALU.subtract).then_inc(v_made, 1)
                for i in range(TT):
                    dve.wait_ge(side_ready, use + 3 + i)
                    dve.tensor_reduce(runmax[:, i, bass.ds(g, 1)], ps[:, 6 + i % 2, :], AX.X,
                                      ALU.max).then_inc(side_free, 1)

            def stop(h, hb, n, nb):
                if n is not None:
                    dve.wait_ge(side_free, n * USES + USES - 2 + CREDIT)
                    dve.tensor_reduce(cmax[:, :], runmax[:, :, :], AX.X, ALU.max).then_inc(side_dve, 1)
                    dve.wait_ge(side_dve, n + 1)
                    dve.tensor_scalar(cz[:, :, DH], cmax[:, :], -1.0, LIFT, ALU.mult, ALU.add).then_inc(c_ready, 1)
                if h is not None:
                    dve.wait_ge(pv_done, h * MT + MT + CREDIT)
                    dve.reciprocal(rec[:, :, :], acc[:, :, :, DH]).then_inc(o_dve, 1)
                    dve.wait_ge(o_dve, h + 1)
                    for a in range(2):
                        ins = dve.tensor_tensor(att[:, a, :, bass.ds(h * DH, DH)], acc[:, a, :, 0:DH],
                                                rec[:, a, :].unsqueeze(2).to_broadcast([P, GT, DH]), ALU.mult)
                    ins.then_inc(o_free, 1)
                if n is not None:
                    dve.wait_ge(side_ready, n * USES + USES)
                    dve.tensor_copy(qb[DH:DH + 1, nb, :].rearrange("p (h n) -> p h n", h=2),
                                    ps[DH:DH + 1, 6:8, :]).then_inc(side_free, 2)
                    dve.wait_ge(side_free, n * USES + USES + CREDIT)
                    dve.sem_inc(cu_ready, 1)

            walk(dve, start, group, stop)

    output_projection(k, att, wo1)


def output_projection(k, att, wo1):
    nc, ps = k.nc, k.ps
    NCK = HEADS * DH // P
    wo = k.ch[:, 0:NCK * P * 2].bitcast(FP32).rearrange("p (c d) -> p c d", c=NCK)
    at = k.e
    ld, turned, copied, y_ready = (k.sem(f"wo_{n}") for n in ("ld", "turned", "copied", "y"))
    with nc.Block() as block:
        @block.sync
        def _(sp):
            sp.dma_start(wo, wo1.rearrange("(c p) d -> p c d", p=P)).then_inc(ld, 16)

        @block.tensor
        def _(pe):
            for n in range(2):
                pe.matmul(ps[:, 4 + n, :], k.zero_h[:, 0:P], k.zero_h[:, :], start=True, stop=False, skip_group_check=True)

            def turn(c):
                if c >= 2:
                    pe.wait_ge(copied, c - 1)
                for i in range(TT):
                    ins = pe.transpose(ps[:, 2 * (c % 2) + i // GT, tile(i % GT)], att[:, i // GT, i % GT, tile(c)], k.ident[:, :])
                ins.then_inc(turned, 1)

            turn(0)
            pe.wait_ge(ld, 16)
            for c in range(NCK):
                if c + 1 < NCK:
                    turn(c + 1)
                pe.wait_ge(copied, c + 1)
                for i in range(TT):
                    ins = pe.matmul(ps[:, 4 + i // GT, tile(i % GT)], at[:, c % 2, tile(i)], wo[:, c, :],
                                    start=False, stop=False, skip_group_check=True)
            ins.then_inc(y_ready, 1)

        @block.scalar
        def _(act):
            for c in range(NCK):
                act.wait_ge(turned, c + 1)
                b = c % 2
                act.activation(at[:, b, :].rearrange("p (h n) -> p h n", h=2), ps[:, 2 * b:2 * b + 2, :],
                               ACT.Copy).then_inc(copied, 1)

        @block.vector
        def _(dve):
            dve.wait_ge(y_ready, 1)
            rows = k.x[:, :, :].rearrange("p (a i) d -> p a (i d)", a=2)
            dve.scalar_tensor_tensor(out=rows, in0=ps[:, 4:6, :], scalar=k.tg[:, 2:3], in1=rows, op0=ALU.mult, op1=ALU.add)


def kernel(**inputs):
    import numpy as np
    import concourse.bacc as bacc
    from concourse import mybir as my
    from concourse.bass_utils import run_bass_kernel_spmd as run

    a = {n: np.asarray(v) for n, v in inputs.items()}
    f = np.float32
    x = np.ascontiguousarray(a["x"])
    bih, bhh = (a[f"L0_xattn_gru_{n}"].reshape(3, 128) for n in ("bih", "bhh"))
    arrays = {
        "x": x,
        "ctx": np.ascontiguousarray(a["ctx_1024"]),
        "cols": np.ascontiguousarray(np.stack(
            [a["L0_xattn_input_norm_w"], a["L0_xattn_slot_norm_w"], *bih, *bhh, a["L1_xattn_ln_g"], a["L1_xattn_ln_b"]], 1)),
        "gates": np.ascontiguousarray(np.broadcast_to(
            np.stack([a["g_xattn"], a["g_ffn"]], 1).reshape(1, 4), (128, 4))),
        "slot_w": np.ascontiguousarray(np.concatenate(
            [a["L0_xattn_Wq"].T, a["L0_xattn_Wk"], a["L0_xattn_Wv"].T, a["L0_xattn_gru_wih"].T, a["L0_xattn_gru_whh"].T], 1)),
        "cent_t": np.ascontiguousarray(a["L0_ffn_centroids"].T),
        "bias_e": np.ascontiguousarray(np.broadcast_to(a["L0_ffn_expert_biases"][None], (128, 64))),
        "wq1": np.ascontiguousarray(a["L1_xattn_Wq"]),
        "wkv1": np.ascontiguousarray(a["L1_xattn_Wkv"]),
        "wo1": np.ascontiguousarray(a["L1_xattn_Wo"]),
        "rout_w": np.ascontiguousarray(np.concatenate([a["L1_ffn_w_router"], a["L1_ffn_w_gating"]], 1)),
    }
    up = a["L0_ffn_W_up"].reshape(32, 2, 128, 64).transpose(0, 2, 1, 3).reshape(32, 128, 128)
    dn = a["L0_ffn_W_down"].reshape(32, 128, 128)
    w0 = np.zeros((33, 128, 256), f)
    w0[:32, :, :128], w0[:32, :, 128:] = up, dn
    w0[32, :, :64], w0[32, :64, 128:] = a["L0_ffn_Ws_up"], a["L0_ffn_Ws_down"]
    arrays["ffn0_w"] = w0
    gt, up = (a[n].reshape(8, 128, 4, 128).transpose(0, 2, 1, 3).reshape(32, 128, 128) for n in ("L1_ffn_w_gate", "L1_ffn_w_up"))
    dn = a["L1_ffn_w_down"].reshape(32, 128, 128)
    arrays["ffn1_w"] = np.ascontiguousarray(np.concatenate([gt, up, dn], 2))

    nc = bacc.Bacc("TRN2", target_bir_lowering=False, num_devices=1)
    args = {n: nc.dram_tensor(f"in_{n}", v.shape, my.dt.from_np(v.dtype), kind="ExternalInput").ap() for n, v in arrays.items()}
    out = nc.dram_tensor("out", (1, 1024, 128), my.dt.float32, kind="ExternalOutput").ap()
    build(nc, args["x"], args["ctx"], *(args[n] for n in (
        "cols", "gates", "slot_w", "cent_t", "bias_e", "wq1", "wkv1", "wo1", "rout_w", "ffn0_w", "ffn1_w")), out)
    r = run(nc, [{f"in_{n}": v for n, v in arrays.items()}], core_ids=[0])
    return r.results[0]["out"]
```

```python
import math

import concourse.bass as bass
from concourse import mybir
from contextlib import ExitStack

FP32 = mybir.dt.float32
BF16 = mybir.dt.bfloat16
FP16 = mybir.dt.float16
ALU = mybir.AluOpType
ACT = mybir.ActivationFunctionType
AX = mybir.AxisListType

P = 128
D = 128
T = 1024
TT = T // P
M = 6404
GT = 4
G = -(-M // (P * GT))
MT = G * GT
MP = MT * P
FULL = M // P
TAIL = M - FULL * P
HEADS, DH = 16, 64
NITER = 3
SLOT_SCALE = D ** -0.5
HEAD_SCALE = DH ** -0.5
LIFT = 12 * math.log(2.0)
VAL_SCALE = float(2 ** 20)
SLOT_EPS = 1e-6
E0, F0 = 64, 64
CH0 = E0 // 2 + 1
E1, F1 = 8, 512
CPE = F1 // P
TOPK = 8
CREDIT = 2
C_WIN, C_WSLOT, C_BIR, C_BIZ, C_BIN, C_BHR, C_BHZ, C_BHN, C_LNG, C_LNB = range(10)


def top(ap):
    return ap.bitcast(BF16).rearrange("p (n b) -> p b n", b=2)[:, 1, :]


def half(h):
    return slice(512 * h, 512 * h + 512)


def tile(i):
    return slice(P * i, P * i + P)


class Chain:

    def __init__(self, eng, sem, base=0):
        self.eng, self.sem, self.n = eng, sem, base

    def __call__(self, ins):
        self.n = self.n + 1
        ins.then_inc(self.sem, 1)
        self.eng.wait_ge(self.sem, self.n)


class Core:

    def __init__(self, nc, ctx):
        self.nc, self.ctx = nc, ctx

    def sb(self, name, shape, dt=FP32, ctx=None):
        return (ctx or self.ctx).enter_context(self.nc.sbuf_tensor(name, shape, dt))

    def sem(self, name):
        return self.ctx.enter_context(self.nc.semaphore(name))


def build(nc, x, ctx_rows, cols, gates, slot_w, cent_t, bias_e, wq1, wkv1, wo1, rout_w, ffn0_w, ffn1_w, out):
    with ExitStack() as stack:
        k = Core(nc, stack)
        k.x = k.sb("x_rows", [P, TT, D])
        k.cols = k.sb("cols_sb", [P, 10])
        k.gates = k.sb("gates_sb", [P, 4])
        k.tg = k.sb("tanh_gates", [P, 4])
        k.cent = k.sb("centroids_t", [P, E0])
        k.bias_e = k.sb("expert_bias", [P, E0])
        k.rout = k.sb("router_w", [P, 2 * E1])
        k.ident = k.sb("ident", [P, P])
        k.ident_h = k.sb("ident_h", [P, P], FP16)
        k.mean_w = k.sb("mean_w", [P, P])
        k.zero_h = k.sb("zero_h", [P, 512], FP16)
        k.eps5 = k.sb("eps5", [P, 1])
        k.eps6 = k.sb("eps6", [P, 1])
        k.bsum = k.sb("gru_bias_sum", [P, 2])
        k.win_s = k.sb("win_scaled", [P, 1])
        k.mask = k.sb("row_mask", [P, MT])
        k.ch = k.sb("ctx_t_hi", [P, MP], FP16)
        k.cl = k.sb("ctx_t_lo", [P, MP], FP16)
        k.xt = k.sb("xn_t", [P, T])
        k.xth = k.sb("xn_t_hi", [P, T], FP16)
        k.xtl = k.sb("xn_t_lo", [P, T], FP16)
        k.e = k.sb("exps", [P, 2, T])
        k.el = k.sb("exps_lo", [P, 2, T], FP16)
        k.stats = k.sb("stats", [P, TT, 6])
        k.mv = k.sb("mean_var", [P, TT, 2])
        k.small = k.sb("small", [P, 8, 64])
        k.ps = stack.enter_context(nc.psum_tensor("ps", [P, 8, 512], FP32))

        with ExitStack() as l0:
            k.pn = k.sb("ctx_rms", [P, MT, D + 1], FP32, l0)
            k.pth = k.sb("ctx_rms_t_hi", [P, MP], FP16, l0)
            k.ptl = k.sb("ctx_rms_t_lo", [P, MP], FP16, l0)
            with ExitStack() as pro:
                prologue(k, pro, x, ctx_rows, cols, gates, cent_t, bias_e, rout_w)
            with ExitStack() as at:
                slot_attention(k, at, slot_w)
        with ExitStack() as f0:
            normed(k, "n1")
            cwt = k.sb("ffn0_cw", [P, 2, T], FP16, f0)
            with ExitStack() as r:
                top_experts(k, r, cwt)
            experts(k, f0, "f0", cwt, ffn0_w, 1)
        with ExitStack() as a1:
            normed(k, "n2")
            cross_attention(k, a1, wq1, wkv1, wo1)
        with ExitStack() as f1:
            normed(k, "n3")
            cwt = k.sb("ffn1_cw", [P, 2, T], FP16, f1)
            with ExitStack() as r:
                soft_experts(k, r, cwt)
            experts(k, f1, "f1", cwt, ffn1_w, 3)
        out_done = k.sem("out_done")
        with nc.Block() as block:
            @block.sync
            def _(sp):
                sp.dma_start(out[0].rearrange("(i p) d -> p i d", p=P), k.x[:, :, :]).then_inc(out_done, 16)
                sp.wait_ge(out_done, 16)


def prologue(k, scope, x, ctx_rows, cols, gates, cent_t, bias_e, rout_w):
    nc, ps = k.nc, k.ps
    CH = 13
    rows = k.sb("ctx_rows", [P, MT, D], FP32, scope)
    st = k.sb("ctx_stats", [P, MT, 6], FP32, scope)
    mv = k.sb("ctx_mv", [P, MT, 2], FP32, scope)
    rms = k.sb("ctx_rms_r", [P, MT], FP32, scope)
    lnr = k.sb("ctx_ln_r", [P, MT], FP32, scope)
    lnm = k.sb("ctx_ln_m", [P, MT], FP32, scope)
    sd = k.sb("ctx_sd", [P, 2, MT], FP32, scope)
    rn = k.sb("ctx_rn", [P, 2, GT, D], FP32, scope)
    ln = k.sb("ctx_ln", [P, 2, GT, D], FP32, scope)
    lt = k.sb("ctx_ln_t", [P, 2, 512], FP32, scope)
    ld_small, ld_x = k.sem("ld_small"), k.sem("ld_x")
    ld_ctx = [k.sem(f"ld_ctx{c}") for c in range(MT // CH)]
    ready = k.sem("pro_consts")
    d_ch, g_ch = k.sem("pro_dve"), k.sem("pro_pool")
    stats_done, aggr_done, msq_ready, sd_ready = (k.sem(n) for n in ("c_stats", "c_aggr", "c_msq", "c_sd"))
    mask_ready, rms_ready = k.sem("c_mask"), k.sem("c_rms")
    pn_ready, ln_ready, pt_ready, lt_ps, pth_done, lt_done, ch_done, ptl_done, cl_done = (
        k.sem(n) for n in ("pn_ready", "ln_ready", "pt_ready", "lt_ps", "pth_done", "lt_done", "ch_done", "ptl_done", "cl_done"))

    def groups(eng, body):
        with eng.Fori(0, G // 2) as i:
            body(i * 2, 0)
            body(i * 2 + 1, 1)
        body(G - 1, 0)

    with nc.Block() as block:
        @block.sync
        def _(sp):
            body = ctx_rows[0, 0:FULL * P, :].rearrange("(j p) d -> p j d", p=P)
            last = ctx_rows[0, M - P:M, :]
            for c in range(MT // CH):
                hi = min(FULL, CH * (c + 1))
                sp.dma_start(rows[:, CH * c:hi, :], body[:, CH * c:hi, :]).then_inc(ld_ctx[c], 16)
            for j in range(FULL, MT):
                sp.dma_start(rows[:, j, :], last).then_inc(ld_ctx[-1], 16)
            for dst, src in ((k.cols, cols), (k.gates, gates), (k.cent, cent_t), (k.bias_e, bias_e), (k.rout, rout_w)):
                sp.dma_start(dst[:, :], src).then_inc(ld_small, 16)
            sp.dma_start(k.x[:, :, :], x[0].rearrange("(i p) d -> p i d", p=P)).then_inc(ld_x, 16)
            sp.wait_ge(ld_x, 16)

        @block.gpsimd
        def _(pool):
            chain = Chain(pool, g_ch)
            chain(pool.memset(k.ident[:, :], 0.0))
            chain(pool.affine_select(out=k.ident[:, :], in_=k.ident[:, :], compare_op=ALU.not_equal, fill=1.0,
                                     base=0, pattern=[[-1, P]], channel_multiplier=1))
            pool.tensor_copy(k.ident_h[:, :], k.ident[:, :]).then_inc(ready, 1)
            chain(pool.memset(k.mask[:, :], 1.0))
            chain(pool.memset(k.mask[:, FULL + 1:MT], 0.0))
            pool.affine_select(out=k.mask[:, FULL:FULL + 1], in_=k.mask[:, FULL:FULL + 1], compare_op=ALU.is_ge,
                               fill=0.0, base=TAIL - P, pattern=[[0, 1]], channel_multiplier=1).then_inc(mask_ready, 1)

        @block.vector
        def _(dve):
            chain = Chain(dve, d_ch)
            dve.memset(k.mean_w[:, :], 1.0 / D)
            dve.memset(k.zero_h[:, :], 0.0)
            dve.memset(k.eps5[:, :], 1e-5)
            chain(dve.memset(k.eps6[:, :], 1e-6))
            for c in range(MT // CH):
                dve.wait_ge(ld_ctx[c], 16 * (1 + (c == MT // CH - 1) * (MT - FULL)))
                with dve.Fori(CH * c, CH * c + CH) as j:
                    dve.bn_stats(st[:, j, :], rows[:, j, :]).then_inc(stats_done, 1)
            dve.wait_ge(stats_done, MT)
            for j in range(MT):
                dve.bn_aggr(mv[:, j, :], st[:, j, :]).then_inc(aggr_done, 1)
            dve.wait_ge(aggr_done, MT)
            chain(dve.tensor_tensor(lnm[:, :], mv[:, :, 0], mv[:, :, 0], ALU.mult))
            dve.tensor_tensor(rms[:, :], lnm[:, :], mv[:, :, 1], ALU.add).then_inc(msq_ready, 1)
            dve.wait_ge(sd_ready, 2)
            chain(dve.reciprocal(rms[:, :], sd[:, 0, :]))
            chain(dve.reciprocal(lnr[:, :], sd[:, 1, :]))
            dve.scalar_tensor_tensor(out=lnm[:, :], in0=mv[:, :, 0], scalar=-1.0, in1=lnr[:, :],
                                     op0=ALU.mult, op1=ALU.mult)
            dve.wait_ge(mask_ready, 1)
            dve.tensor_copy(k.pn[:, :, D], k.mask[:, :])
            dve.tensor_tensor(rms[:, :], rms[:, :], k.mask[:, :], ALU.mult).then_inc(rms_ready, 1)
            dve.wait_ge(rms_ready, 1)
            dve.wait_ge(ld_small, 16 * 5)
            dve.tensor_tensor(k.bsum[:, :], k.cols[:, C_BIR:C_BIZ + 1], k.cols[:, C_BHR:C_BHZ + 1], ALU.add)
            dve.tensor_scalar(k.win_s[:, :], k.cols[:, C_WIN:C_WIN + 1], SLOT_SCALE, None, ALU.mult)

            def rows_of(g, b):
                dve.wait_ge(pt_ready, g + 1)
                for u in range(GT):
                    j = g * GT + u
                    ins = dve.tensor_scalar(rn[:, b, u, :], rows[:, j, :], rms[:, bass.ds(j, 1)], None, ALU.mult)
                ins.then_inc(pn_ready, 1)
                dve.wait_ge(lt_ps, g + 1)
                for u in range(GT):
                    j = g * GT + u
                    ins = dve.tensor_scalar(ln[:, b, u, :], rows[:, j, :], lnr[:, bass.ds(j, 1)], lnm[:, bass.ds(j, 1)],
                                            ALU.mult, ALU.add)
                ins.then_inc(ln_ready, 1)

            def lows(g, b):
                dve.wait_ge(pth_done, g + 1)
                dve.tensor_tensor(k.ptl[:, bass.ds(g * 512, 512)], ps[:, b, :], k.pth[:, bass.ds(g * 512, 512)],
                                  ALU.subtract).then_inc(ptl_done, 1)
                dve.wait_ge(ch_done, g + 1)
                dve.tensor_tensor(k.cl[:, bass.ds(g * 512, 512)], lt[:, b, :], k.ch[:, bass.ds(g * 512, 512)],
                                  ALU.subtract).then_inc(cl_done, 1)

            rows_of(0, 0)
            with dve.Fori(0, G // 2) as i:
                for b in range(2):
                    rows_of(i * 2 + b + 1, 1 - b)
                    lows(i * 2 + b, b)
            lows(G - 1, 0)

        @block.tensor
        def _(pe):
            pe.sem_inc(lt_ps, CREDIT)
            pe.sem_inc(pt_ready, CREDIT)
            pe.wait_ge(ready, 1)

            def turn(g, b):
                pe.wait_ge(pn_ready, g + 1)
                pe.wait_ge(ptl_done, g + 1)
                for u in range(GT):
                    ins = pe.transpose(ps[:, b, tile(u)], rn[:, b, u, :], k.ident[:, :])
                ins.then_inc(pt_ready, 1)
                pe.wait_ge(ln_ready, g + 1)
                pe.wait_ge(lt_done, g + 1)
                for u in range(GT):
                    ins = pe.transpose(ps[:, 2 + b, tile(u)], ln[:, b, u, :], k.ident[:, :])
                ins.then_inc(lt_ps, 1)

            groups(pe, turn)

        @block.scalar
        def _(act):
            act.sem_inc(lt_done, CREDIT)
            act.sem_inc(ptl_done, CREDIT)
            act.sem_inc(cl_done, CREDIT)
            act.wait_ge(msq_ready, 1)
            act.activation(sd[:, 0, :], rms[:, :], ACT.Sqrt, bias=k.eps6[:, :]).then_inc(sd_ready, 1)
            act.activation(sd[:, 1, :], mv[:, :, 1], ACT.Sqrt, bias=k.eps5[:, :]).then_inc(sd_ready, 1)
            act.wait_ge(ld_small, 16 * 5)
            act.wait_ge(rms_ready, 1)

            def split(g, b):
                for u in range(GT):
                    j = g * GT + u
                    act.activation(k.pn[:, j, 0:D], rows[:, j, :], ACT.Copy, scale=rms[:, bass.ds(j, 1)])
                act.wait_ge(pt_ready, g + 1 + CREDIT)
                act.activation(k.pth[:, bass.ds(g * 512, 512)], ps[:, b, :], ACT.Copy).then_inc(pth_done, 1)
                act.wait_ge(lt_ps, g + 1 + CREDIT)
                act.wait_ge(cl_done, g + 1)
                act.activation(lt[:, b, :], ps[:, 2 + b, :], ACT.Identity, bias=k.cols[:, C_LNB:C_LNB + 1],
                               scale=k.cols[:, C_LNG:C_LNG + 1]).then_inc(lt_done, 1)
                act.wait_ge(lt_done, g + 1 + CREDIT)
                act.activation(k.ch[:, bass.ds(g * 512, 512)], lt[:, b, :], ACT.Copy).then_inc(ch_done, 1)

            groups(act, split)
            act.activation(k.tg[:, :], k.gates[:, :], ACT.Tanh)

    norm_rows(k, scope, "n0")


def normed(k, tag):
    with ExitStack() as scope:
        norm_rows(k, scope, tag)


def norm_rows(k, scope, tag):
    nc, ps = k.nc, k.ps
    xn = k.sb(f"{tag}_rows", [P, TT, D], FP32, scope)
    sd = k.sb(f"{tag}_sd", [P, 3, TT], FP32, scope)
    stats_done, aggr_done, sd_ready, rows_ready, turned, hi_ready, d_ch = (
        k.sem(f"{tag}_{n}") for n in ("stats", "aggr", "sdr", "rows_ready", "turned", "hi", "dve"))
    with nc.Block() as block:
        @block.vector
        def _(dve):
            chain = Chain(dve, d_ch)
            for i in range(TT):
                dve.bn_stats(k.stats[:, i, :], k.x[:, i, :]).then_inc(stats_done, 1)
            dve.wait_ge(stats_done, TT)
            for i in range(TT):
                dve.bn_aggr(k.mv[:, i, :], k.stats[:, i, :]).then_inc(aggr_done, 1)
            dve.wait_ge(sd_ready, 1)
            chain(dve.reciprocal(sd[:, 1, :], sd[:, 0, :]))
            chain(dve.scalar_tensor_tensor(out=sd[:, 2, :], in0=k.mv[:, :, 0], scalar=-1.0, in1=sd[:, 1, :],
                                           op0=ALU.mult, op1=ALU.mult))
            for i in range(TT):
                dve.tensor_scalar(xn[:, i, :], k.x[:, i, :], sd[:, 1, i:i + 1], sd[:, 2, i:i + 1],
                                  ALU.mult, ALU.add).then_inc(rows_ready, 1)
            for h in range(2):
                dve.wait_ge(hi_ready, h + 1)
                dve.tensor_tensor(k.xtl[:, half(h)], ps[:, h, :], k.xth[:, half(h)], ALU.subtract)

        @block.scalar
        def _(act):
            act.wait_ge(aggr_done, TT)
            act.activation(sd[:, 0, :], k.mv[:, :, 1], ACT.Sqrt, bias=k.eps5[:, :]).then_inc(sd_ready, 1)
            for h in range(2):
                act.wait_ge(turned, h + 1)
                act.activation(k.xt[:, half(h)], ps[:, h, :], ACT.Copy)
                act.activation(k.xth[:, half(h)], ps[:, h, :], ACT.Copy).then_inc(hi_ready, 1)

        @block.tensor
        def _(pe):
            for h in range(2):
                for i in range(4 * h, 4 * h + 4):
                    pe.wait_ge(rows_ready, i + 1)
                    ins = pe.transpose(ps[:, h, tile(i - 4 * h)], xn[:, i, :], k.ident[:, :])
                ins.then_inc(turned, 1)


def residual(k, tag, src_t, gate):
    nc, ps = k.nc, k.ps
    turned = k.sem(f"{tag}_turned")
    with nc.Block() as block:
        @block.tensor
        def _(pe):
            for i in range(TT):
                ins = pe.transpose(ps[:, i // 4, tile(i % 4)], src_t[:, tile(i)], k.ident[:, :])
                if i % 4 == 3:
                    ins.then_inc(turned, 1)

        @block.vector
        def _(dve):
            for h in range(2):
                dve.wait_ge(turned, h + 1)
                rows = k.x[:, 4 * h:4 * h + 4, :].rearrange("p i d -> p (i d)")
                dve.scalar_tensor_tensor(out=rows, in0=ps[:, h, :], scalar=k.tg[:, gate:gate + 1], in1=rows,
                                         op0=ALU.mult, op1=ALU.add)


def slot_attention(k, scope, slot_w):
    nc, ps = k.nc, k.ps
    w = k.sb("slot_w", [P, 3 * D + 6 * D], FP32, scope)
    wq, wk, wv = (w[:, D * n:D * n + D] for n in range(3))
    wih = [w[:, D * (3 + n):D * (4 + n)] for n in range(3)]
    whh = [w[:, D * (6 + n):D * (7 + n)] for n in range(3)]
    slots = k.xt
    t = [k.sb(f"slot_t{n}", [P, T], FP32, scope) for n in range(5)]
    qh, ql = (k.sb(n, [P, T], FP16, scope) for n in ("slot_qh", "slot_ql"))
    R = 4
    CUT = 256
    e = k.sb("slot_exps", [P, R, T], FP32, scope)
    el = k.sb("slot_exps_lo", [P, R, T], FP16, scope)
    mx = k.sb("slot_mx", [P, R, 1], FP32, scope)
    nb = k.sb("slot_nb", [P, R, 1], FP32, scope)
    sums = k.sb("slot_sums", [P, R, 1], FP32, scope)
    rec = k.sb("slot_rec", [P, R, 2], FP32, scope)
    vh, vl = (k.sb(n, [P, R, D + 1], FP16, scope) for n in ("slot_vh", "slot_vl"))
    den = k.sb("slot_den", [P, 2, TT], FP32, scope)
    ld = k.sem("slot_ld")
    sq_ready, ss_ready, rs_ready, sn_ready, q_ps, q_sb, qk_ps, qf_ready, qh_ready, q_act, q_dve = (
        k.sem(f"sq_{n}") for n in ("sq", "ss", "rs", "sn", "q_ps", "q_sb", "qk_ps", "qf", "qh", "act", "dve"))
    s_ready, nb_ready, exp_done, el_ready, v_ready, pv_done, m_dve = (
        k.sem(f"sm_{n}") for n in ("s", "nb", "exp", "el", "v", "pv", "dve"))
    u_ready, ut_ps, ut_sb, up_ps, up_sb, gate_ps, gates_ready, rh_ready, n_ready, g_dve, g_act = (
        k.sem(f"sg_{n}") for n in ("u", "ut_ps", "ut_sb", "up_ps", "up_sb", "gate_ps", "gates", "rh", "n", "dve", "act"))
    acc = [ps[:, 4 + i // 3, (D + 1) * (i % 3):(D + 1) * (i % 3) + D + 1] for i in range(TT)]

    with nc.Block() as block:
        @block.sync
        def _(sp):
            sp.dma_start(w[:, :], slot_w).then_inc(ld, 16)
            sp.wait_ge(ld, 16)

        @block.scalar
        def _(act):
            act.sem_inc(exp_done, CREDIT)

        @block.tensor
        def _(pe):
            pe.sem_inc(pv_done, R)

    with nc.Fori(0, NITER) as it:
        with nc.Block() as block:
            @block.scalar
            def _(act):
                act.activation(t[0][:, :], slots[:, :], ACT.Square).then_inc(sq_ready, 1)
                act.wait_ge(ss_ready, it + 1)
                act.activation(t[1][:, :].rearrange("p (h n) -> p h n", h=2), ps[:, 0:2, :], ACT.Ln,
                               bias=k.eps6[:, :]).then_inc(q_act, 1)
                act.wait_ge(q_act, it + 1)
                act.activation(t[2][:, :], t[1][:, :], ACT.Exp, scale=-0.5).then_inc(rs_ready, 1)
                for h in range(2):
                    act.wait_ge(q_ps, it * 2 + h + 1)
                    act.activation(t[1][:, half(h)], ps[:, 2 + h, :], ACT.Copy).then_inc(q_sb, 1)
                for h in range(2):
                    act.wait_ge(qf_ready, it * 2 + h + 1)
                    act.activation(qh[:, half(h)], t[0][:, half(h)], ACT.Copy).then_inc(qh_ready, 1)

            @block.vector
            def _(dve):
                dve.wait_ge(rs_ready, it + 1)
                dve.scalar_tensor_tensor(out=t[3][:, :], in0=slots[:, :], scalar=k.cols[:, C_WSLOT:C_WSLOT + 1],
                                         in1=t[2][:, :], op0=ALU.mult, op1=ALU.mult).then_inc(sn_ready, 1)
                for h in range(2):
                    dve.wait_ge(qk_ps, it * 2 + h + 1)
                    dve.tensor_scalar(t[0][:, half(h)], ps[:, 4 + h, :], k.win_s[:, :], None,
                                      ALU.mult).then_inc(qf_ready, 1)
                for h in range(2):
                    dve.wait_ge(qh_ready, it * 2 + h + 1)
                    dve.tensor_tensor(ql[:, half(h)], t[0][:, half(h)], qh[:, half(h)], ALU.subtract)

            @block.tensor
            def _(pe):
                pe.wait_ge(sq_ready, it + 1)
                for h in range(2):
                    ins = pe.matmul(ps[:, h, :], k.mean_w[:, :], t[0][:, half(h)], start=True, stop=True)
                ins.then_inc(ss_ready, 1)
                pe.wait_ge(sn_ready, it + 1)
                for h in range(2):
                    pe.matmul(ps[:, 2 + h, :], wq, t[3][:, half(h)], start=True, stop=True).then_inc(q_ps, 1)
                for h in range(2):
                    pe.wait_ge(q_sb, it * 2 + h + 1)
                    pe.matmul(ps[:, 4 + h, :], wk, t[1][:, half(h)], start=True, stop=True).then_inc(qk_ps, 1)

        with nc.Block() as block:
            n0 = it * MT

            @block.tensor
            def _(pe):
                def scores(j, b):
                    pe.wait_ge(exp_done, n0 + j + 1)
                    cols_j = bass.ds(j * P, P)
                    for h in range(2):
                        pe.matmul(ps[:, 2 * b + h, :], k.pth[:, cols_j], qh[:, half(h)], start=True, stop=False)
                        pe.matmul(ps[:, 2 * b + h, :], k.pth[:, cols_j], ql[:, half(h)], start=False, stop=False)
                        ins = pe.matmul(ps[:, 2 * b + h, :], k.ptl[:, cols_j], qh[:, half(h)], start=False, stop=True)
                    ins.then_inc(s_ready, 1)

                def values(j, q):
                    pe.wait_ge(v_ready, n0 + j + 1)
                    pe.wait_ge(el_ready, n0 + j + 1)
                    for i in range(TT):
                        eh = top(e[:, q, tile(i)])
                        pe.matmul(acc[i], eh, vh[:, q, :], start=False, stop=False, skip_group_check=True)
                        pe.matmul(acc[i], eh, vl[:, q, :], start=False, stop=False, skip_group_check=True)
                        ins = pe.matmul(acc[i], el[:, q, tile(i)], vh[:, q, :], start=False, stop=False,
                                        skip_group_check=True)
                    ins.then_inc(pv_done, 1)

                for n in range(3):
                    pe.matmul(ps[:, 4 + n, :], k.zero_h[:, 0:P], k.zero_h[:, :], start=True, stop=False,
                              skip_group_check=True)
                for j in range(R - 1):
                    scores(j, j % 2)
                with pe.Fori(0, MT // R - 1) as i:
                    for q in range(R):
                        values(i * R + q, q)
                        scores(i * R + q + R - 1, (q + 1) % 2)
                for j in range(MT - R, MT):
                    values(j, j % R)
                    if j + R - 1 < MT:
                        scores(j + R - 1, (j + 1) % 2)

            @block.scalar
            def _(act):
                act.preload_act_table(ACT.Exp)
                with act.Fori(0, MT // R) as i:
                    for q in range(R):
                        j, b = i * R + q, q % 2
                        act.wait_ge(nb_ready, n0 + j + 1)
                        act.wait_ge(pv_done, n0 + j + 1)
                        act.activation(e[:, q, :].rearrange("p (h n) -> p h n", h=2), ps[:, 2 * b:2 * b + 2, :],
                                       ACT.Exp, bias=nb[:, q, :], accum_out=sums[:, q, :]).then_inc(exp_done, 1)

            @block.gpsimd
            def _(pool):
                with pool.Fori(0, MT // R) as i:
                    for q in range(R):
                        pool.wait_ge(exp_done, n0 + i * R + q + 1 + CREDIT)
                        pool.tensor_tensor(el[:, q, CUT:T], e[:, q, CUT:T], top(e[:, q, CUT:T]),
                                           ALU.subtract).then_inc(el_ready, 1)

            @block.vector
            def _(dve):
                STEPS = 4

                def shift(j, q, n):
                    dve.wait_ge(s_ready, n0 + j + 1)
                    dve.tensor_reduce(mx[:, q, :], ps[:, 2 * (q % 2):2 * (q % 2) + 2, :], AX.XY, ALU.max).then_inc(m_dve, 1)
                    dve.wait_ge(m_dve, n + 1)
                    dve.tensor_scalar(nb[:, q, :], mx[:, q, :], -1.0, LIFT, ALU.mult, ALU.add).then_inc(nb_ready, 1)

                def scaled(j, q, n):
                    dve.wait_ge(exp_done, n0 + j + 1 + CREDIT)
                    dve.reciprocal(rec[:, q, 0:1], sums[:, q, :]).then_inc(m_dve, 1)
                    dve.tensor_tensor(el[:, q, 0:CUT], e[:, q, 0:CUT], top(e[:, q, 0:CUT]), ALU.subtract)
                    dve.wait_ge(m_dve, n + 1)
                    dve.tensor_scalar(rec[:, q, 1:2], rec[:, q, 0:1], VAL_SCALE, None, ALU.mult).then_inc(m_dve, 1)
                    dve.wait_ge(m_dve, n + 2)
                    dve.tensor_scalar(vh[:, q, :], k.pn[:, j, :], rec[:, q, 1:2], None, ALU.mult).then_inc(m_dve, 1)
                    dve.wait_ge(m_dve, n + 3)
                    dve.scalar_tensor_tensor(out=vl[:, q, :], in0=k.pn[:, j, :], scalar=rec[:, q, 1:2],
                                             in1=vh[:, q, :], op0=ALU.mult, op1=ALU.subtract).then_inc(v_ready, 1)

                base = it * (MT * STEPS)
                shift(0, 0, base)
                with dve.Fori(0, MT // R - 1) as i:
                    for q in range(R):
                        n = base + i * (R * STEPS) + q * STEPS + 1
                        shift(i * R + q + 1, (q + 1) % R, n)
                        scaled(i * R + q, q, n + 1)
                for j in range(MT - R, MT):
                    n = base + j * STEPS + 1
                    if j + 1 < MT:
                        shift(j + 1, (j + 1) % R, n)
                        n = n + 1
                    scaled(j, j % R, n)

        with nc.Block() as block:
            r, z, hn_r, n_t, u_t = t[0], t[1], t[2], t[3], t[4]

            @block.vector
            def _(dve):
                chain = Chain(dve, g_dve, it * 5)
                for n in range(3):
                    m = min(3, TT - 3 * n)
                    sums_n = ps[:, 4 + n, 0:m * (D + 1)].rearrange("p (i d) -> p i d", d=D + 1)[:, :, D]
                    ins = dve.tensor_scalar(den[:, 0, 3 * n:3 * n + m], sums_n, SLOT_EPS * VAL_SCALE, None, ALU.add)
                chain(ins)
                chain(dve.reciprocal(den[:, 1, :], den[:, 0, :]))
                for i in range(TT):
                    dve.tensor_scalar(t[3][:, tile(i)], acc[i][:, 0:D], den[:, 1, i:i + 1], None,
                                      ALU.mult).then_inc(u_ready, 1)
                dve.wait_ge(gates_ready, it + 1)
                chain(dve.scalar_tensor_tensor(out=hn_r[:, :].rearrange("p (h n) -> p h n", h=2), in0=ps[:, 6:8, :],
                                               scalar=k.cols[:, C_BHN:C_BHN + 1],
                                               in1=r[:, :].rearrange("p (h n) -> p h n", h=2),
                                               op0=ALU.add, op1=ALU.mult))
                dve.tensor_tensor(hn_r[:, :].rearrange("p (h n) -> p h n", h=2), ps[:, 4:6, :],
                                  hn_r[:, :].rearrange("p (h n) -> p h n", h=2), ALU.add).then_inc(rh_ready, 1)
                dve.wait_ge(n_ready, it + 1)
                chain(dve.tensor_tensor(hn_r[:, :], slots[:, :], n_t[:, :], ALU.subtract))
                chain(dve.tensor_tensor(hn_r[:, :], hn_r[:, :], z[:, :], ALU.mult))
                dve.tensor_tensor(slots[:, :], n_t[:, :], hn_r[:, :], ALU.add)

            @block.tensor
            def _(pe):
                for i in range(TT):
                    pe.wait_ge(u_ready, it * TT + i + 1)
                    ins = pe.transpose(ps[:, i // 4, tile(i % 4)], t[3][:, tile(i)], k.ident[:, :])
                    if i % 4 == 3:
                        ins.then_inc(ut_ps, 1)
                for h in range(2):
                    pe.wait_ge(ut_sb, it * 2 + h + 1)
                    pe.matmul(ps[:, 2 + h, :], wv, u_t[:, half(h)], start=True, stop=True).then_inc(up_ps, 1)
                pe.wait_ge(up_sb, it * 2 + 2)
                for h in range(2):
                    pe.matmul(ps[:, 4 + h, :], wih[2], t[2][:, half(h)], start=True, stop=True)
                    pe.matmul(ps[:, 6 + h, :], whh[2], slots[:, half(h)], start=True, stop=True)
                    for n in range(2):
                        pe.matmul(ps[:, 2 * n + h, :], wih[n], t[2][:, half(h)], start=True, stop=False)
                        ins = pe.matmul(ps[:, 2 * n + h, :], whh[n], slots[:, half(h)], start=False, stop=True)
                    ins.then_inc(gate_ps, 1)

            @block.scalar
            def _(act):
                for h in range(2):
                    act.wait_ge(ut_ps, it * 2 + h + 1)
                    act.activation(u_t[:, half(h)], ps[:, h, :], ACT.Copy,
                                   scale=k.cols[:, C_WIN:C_WIN + 1]).then_inc(ut_sb, 1)
                for h in range(2):
                    act.wait_ge(up_ps, it * 2 + h + 1)
                    act.activation(t[2][:, half(h)], ps[:, 2 + h, :], ACT.Copy).then_inc(up_sb, 1)
                act.wait_ge(gate_ps, it * 2 + 2)
                act.activation(r[:, :].rearrange("p (h n) -> p h n", h=2), ps[:, 0:2, :], ACT.Sigmoid,
                               bias=k.bsum[:, 0:1])
                act.activation(z[:, :].rearrange("p (h n) -> p h n", h=2), ps[:, 2:4, :], ACT.Sigmoid,
                               bias=k.bsum[:, 1:2]).then_inc(gates_ready, 1)
                act.wait_ge(rh_ready, it + 1)
                act.activation(n_t[:, :], hn_r[:, :], ACT.Tanh, bias=k.cols[:, C_BIN:C_BIN + 1]).then_inc(n_ready, 1)

    residual(k, "slot_res", slots, 0)


def widen(k, scope, tag, cwt, weigh):
    nc, ps = k.nc, k.ps
    turned, hi_ready = k.sem(f"{tag}_turned"), k.sem(f"{tag}_hi")
    with nc.Block() as block:
        @block.tensor
        def _(pe):
            for i in range(TT):
                ins = pe.transpose(ps[:, i // 4, tile(i % 4)], weigh[:, i, :], k.ident[:, :])
            ins.then_inc(turned, 1)

        @block.scalar
        def _(act):
            act.wait_ge(turned, 1)
            act.activation(cwt[:, 0, :].rearrange("p (h n) -> p h n", h=2), ps[:, 0:2, :], ACT.Copy).then_inc(hi_ready, 1)

        @block.vector
        def _(dve):
            dve.wait_ge(hi_ready, 1)
            dve.tensor_tensor(cwt[:, 1, :].rearrange("p (h n) -> p h n", h=2), ps[:, 0:2, :],
                              cwt[:, 0, :].rearrange("p (h n) -> p h n", h=2), ALU.subtract)


def top_experts(k, scope, cwt):
    nc, ps = k.nc, k.ps
    biased = k.sb("top_biased", [P, TT, E0], FP32, scope)
    rest = k.sb("top_rest", [P, TT, E0], FP32, scope)
    sig = k.sb("top_sig", [P, TT, E0], FP32, scope)
    best = k.sb("top_best", [P, TT, 8], FP32, scope)
    total = k.sb("top_total", [P, 2, TT], FP32, scope)
    weigh = k.sb("top_weigh", [P, TT, P], FP32, scope)
    aff_ready, e_ready, w_zero, d_ch, best_done = (k.sem(f"top_{n}") for n in ("aff", "exp", "zero", "dve", "best"))
    aff = ps[:, 0, :].rearrange("p (i e) -> p i e", e=E0)
    with nc.Block() as block:
        @block.tensor
        def _(pe):
            for i in range(TT):
                ins = pe.matmul(aff[:, i, :], k.xt[:, tile(i)], k.cent[:, :], start=True, stop=True)
            ins.then_inc(aff_ready, 1)

        @block.scalar
        def _(act):
            act.wait_ge(d_ch, 1)
            act.activation(sig[:, :, :], aff, ACT.Exp, scale=-1.0).then_inc(e_ready, 1)

        @block.gpsimd
        def _(pool):
            pool.memset(weigh[:, :, :], 0.0).then_inc(w_zero, 1)
            pool.wait_ge(w_zero, 1)
            pool.memset(weigh[:, :, E0], 1.0).then_inc(w_zero, 1)

        @block.vector
        def _(dve):
            chain = Chain(dve, d_ch)
            dve.wait_ge(aff_ready, 1)
            chain(dve.tensor_tensor(biased[:, :, :], aff, k.bias_e[:, :].unsqueeze(1).to_broadcast([P, TT, E0]), ALU.add))
            for i in range(TT):
                dve.max(best[:, i, :], biased[:, i, :]).then_inc(best_done, 1)
            for i in range(TT):
                dve.wait_ge(best_done, i + 1)
                ins = dve.match_replace(rest[:, i, :], best[:, i, :], biased[:, i, :], -3.0e38)
            chain(ins)
            chain(dve.tensor_tensor(rest[:, :, :], rest[:, :, :], biased[:, :, :], ALU.not_equal))
            dve.wait_ge(e_ready, 1)
            chain(dve.tensor_scalar(sig[:, :, :], sig[:, :, :], 1.0, None, ALU.add))
            chain(dve.reciprocal(sig[:, :, :], sig[:, :, :]))
            chain(dve.tensor_tensor(sig[:, :, :], sig[:, :, :], rest[:, :, :], ALU.mult))
            chain(dve.tensor_reduce(total[:, 0, :], sig[:, :, :], AX.X, ALU.add))
            chain(dve.tensor_scalar(total[:, 0, :], total[:, 0, :], 1e-8, None, ALU.add))
            chain(dve.reciprocal(total[:, 1, :], total[:, 0, :]))
            dve.wait_ge(w_zero, 2)
            dve.tensor_tensor(weigh[:, :, 0:E0], sig[:, :, :],
                              total[:, 1, :].unsqueeze(2).to_broadcast([P, TT, E0]), ALU.mult)

    widen(k, scope, "top", cwt, weigh)


def soft_experts(k, scope, cwt):
    nc, ps = k.nc, k.ps
    logit = k.sb("soft_logit", [P, TT, 2, E1], FP32, scope)
    prob = k.sb("soft_prob", [P, TT, 2, E1], FP32, scope)
    mx = k.sb("soft_mx", [P, TT, 2], FP32, scope)
    total = k.sb("soft_total", [P, 2, TT, 2], FP32, scope)
    cw = k.sb("soft_cw", [P, TT, E1], FP32, scope)
    cs = k.sb("soft_cs", [P, 2, TT], FP32, scope)
    weigh = k.sb("soft_weigh", [P, TT, P], FP32, scope)
    lg_ready, x_ready, e_ready, w_zero, d_ch = (k.sem(f"soft_{n}") for n in ("lg", "x", "exp", "zero", "dve"))
    lg = ps[:, 0, 0:TT * 2 * E1].rearrange("p (i g e) -> p i g e", g=2, e=E1)
    with nc.Block() as block:
        @block.tensor
        def _(pe):
            for i in range(TT):
                ins = pe.matmul(ps[:, 0, 2 * E1 * i:2 * E1 * (i + 1)], k.xt[:, tile(i)], k.rout[:, :],
                                start=True, stop=True)
            ins.then_inc(lg_ready, 1)

        @block.scalar
        def _(act):
            act.wait_ge(x_ready, 1)
            act.activation(prob[:, :, 0, :], logit[:, :, 0, :], ACT.Exp)
            act.activation(prob[:, :, 1, :], logit[:, :, 1, :], ACT.Exp, scale=10.0).then_inc(e_ready, 1)

        @block.gpsimd
        def _(pool):
            pool.memset(weigh[:, :, :], 0.0).then_inc(w_zero, 1)

        @block.vector
        def _(dve):
            chain = Chain(dve, d_ch)
            dve.wait_ge(lg_ready, 1)
            chain(dve.tensor_reduce(mx[:, :, :], lg, AX.X, ALU.max))
            dve.tensor_tensor(logit[:, :, :, :], lg, mx[:, :, :].unsqueeze(3).to_broadcast([P, TT, 2, E1]),
                              ALU.subtract).then_inc(x_ready, 1)
            dve.wait_ge(e_ready, 1)
            chain(dve.tensor_reduce(total[:, 0, :, :], prob[:, :, :, :], AX.X, ALU.add))
            chain(dve.reciprocal(total[:, 1, :, :], total[:, 0, :, :]))
            chain(dve.tensor_tensor(prob[:, :, :, :], prob[:, :, :, :],
                                    total[:, 1, :, :].unsqueeze(3).to_broadcast([P, TT, 2, E1]), ALU.mult))
            chain(dve.tensor_tensor(cw[:, :, :], prob[:, :, 0, :], prob[:, :, 1, :], ALU.mult))
            chain(dve.tensor_reduce(cs[:, 0, :], cw[:, :, :], AX.X, ALU.add))
            chain(dve.tensor_scalar(cs[:, 0, :], cs[:, 0, :], 1e-9, None, ALU.add))
            chain(dve.reciprocal(cs[:, 1, :], cs[:, 0, :]))
            dve.wait_ge(w_zero, 1)
            dve.tensor_tensor(weigh[:, :, 0:E1], cw[:, :, :], cs[:, 1, :].unsqueeze(2).to_broadcast([P, TT, E1]),
                              ALU.mult)

    widen(k, scope, "soft", cwt, weigh)


def experts(k, scope, tag, cwt, w_dram, gate):
    nc, ps = k.nc, k.ps
    gated = w_dram.shape[2] == 3 * P
    nch = w_dram.shape[0]
    nw = w_dram.shape[2] // P
    STEP = CPE if gated else 3
    npick = E1 if gated else CH0
    RAW = 4
    pick = k.sb(f"{tag}_pick", [P, npick, P], FP16, scope)
    raw = k.sb(f"{tag}_raw", [P, RAW, nw * P], FP32, scope)
    wh = k.sb(f"{tag}_wh", [P, RAW, nw * P], FP16, scope)
    wl = k.sb(f"{tag}_wl", [P, RAW, nw * P], FP16, scope)
    inner = k.sb(f"{tag}_inner", [P, 2, 512], FP32, scope)
    a = k.sb(f"{tag}_a", [P, 2, 512], FP32, scope)
    ah = k.sb(f"{tag}_ah", [P, 2, 512], FP16, scope)
    al = k.sb(f"{tag}_al", [P, 2, 512], FP16, scope)
    y = k.sb(f"{tag}_y", [P, T], FP32, scope)
    ld = [k.sem(f"{tag}_ld{n}") for n in range(RAW)]
    wh_ready, wl_ready, up_ready, in_ready, a_ready, ah_ready, al_ready, down_done, pk, y_ready, m_ready, d_ch = (
        k.sem(f"{tag}_{n}") for n in ("wh", "wl", "up", "in", "a", "ah", "al", "down", "pick", "y", "m", "dve"))
    down_w = slice((nw - 1) * P, nw * P)
    SPREAD = 4 if gated else 2
    BODIES = nch // STEP
    assert nch % STEP == 0

    with nc.Block() as block:
        @block.gpsimd
        def _(pool):
            pool.memset(pick[:, :, :], 0.0).then_inc(pk, 1)
            pool.wait_ge(pk, 1)
            if gated:
                pat, view = [[-1, npick], [0, P]], pick[:, :, :]
            else:
                pat = [[-2, npick], [-1, 2], [0, F0]]
                view = pick[:, :, :].rearrange("p c (e f) -> p c e f", e=2)
            pool.affine_select(out=view, in_=view, compare_op=ALU.not_equal, fill=1.0, base=0, pattern=pat,
                               channel_multiplier=1)

        @block.tensor
        def _(pe):
            pe.sem_inc(down_done, CREDIT)

        @block.vector
        def _(dve):
            dve.sem_inc(a_ready, CREDIT)

    with nc.Block() as block:
        def bodies(eng, body):
            with eng.Fori(0, BODIES) as i:
                for s in range(STEP):
                    body(i * STEP + s, s)

        @block.sync
        def _(sp):
            def load(c, r):
                sp.dma_start(raw[:, r, :], w_dram[c]).then_inc(ld[r], 16)

            for c in range(RAW):
                load(c, c)
            with sp.Fori(1, nch // RAW) as i:
                for r in range(RAW):
                    sp.wait_ge(wl_ready, (i - 1) * RAW + r + 1)
                    sp.dma_start(raw[:, r, :], w_dram[bass.ds(i * RAW + r, 1)].rearrange("c p n -> (c p) n")).then_inc(ld[r], 16)
            for c in range(nch // RAW * RAW, nch):
                sp.wait_ge(wl_ready, c - RAW + 1)
                load(c, c % RAW)
            for r in range(RAW):
                sp.wait_ge(ld[r], 16 * ((nch - 1 - r) // RAW + 1))

        AHEAD = 2

        def split_loop(eng, weights, halves):
            for c in range(AHEAD):
                weights(c, c, 16)
            n = (nch - AHEAD) // RAW
            with eng.Fori(0, n) as i:
                for r in range(RAW):
                    weights(i * RAW + r + AHEAD, (r + AHEAD) % RAW, i * 16 + 16 * (1 + (r + AHEAD) // RAW))
                    halves(i * RAW + r)
            for c in range(n * RAW, nch):
                if c + AHEAD < nch:
                    weights(c + AHEAD, (c + AHEAD) % RAW, 16 * ((c + AHEAD) // RAW + 1))
                halves(c)

        @block.gpsimd
        def _(pool):
            def low(c, r, loaded):
                pool.wait_ge(wh_ready, c + 1)
                pool.tensor_tensor(wl[:, r, :], raw[:, r, :], wh[:, r, :], ALU.subtract).then_inc(wl_ready, 1)

            def halves(c):
                for h in range(2):
                    n = c * 2 + h
                    pool.wait_ge(ah_ready, n + 1)
                    pool.wait_ge(down_done, n + 1)
                    pool.tensor_tensor(al[:, h, :], a[:, h, :], ah[:, h, :], ALU.subtract).then_inc(al_ready, 1)

            split_loop(pool, low, halves)

        @block.scalar
        def _(act):
            def high(c, r, loaded):
                act.wait_ge(ld[r], loaded)
                if not isinstance(c, int) or c >= AHEAD:
                    act.wait_ge(down_done, c * 2 - 2 * AHEAD)
                act.activation(wh[:, r, :], raw[:, r, :], ACT.Copy).then_inc(wh_ready, 1)

            def halves(c):
                for h in range(2):
                    n = c * 2 + h
                    act.wait_ge(up_ready, n + 1)
                    act.wait_ge(a_ready, n + 1)
                    act.activation(inner[:, h, :], ps[:, h, :], ACT.Silu).then_inc(in_ready, 1)
                for h in range(2):
                    n = c * 2 + h
                    act.wait_ge(a_ready, n + 1 + CREDIT)
                    act.wait_ge(down_done, n + 1)
                    act.activation(ah[:, h, :], a[:, h, :], ACT.Copy).then_inc(ah_ready, 1)

            act.preload_act_table(ACT.Silu)
            split_loop(act, high, halves)
            act.wait_ge(down_done, 2 * nch + CREDIT)
            act.activation(y[:, :].rearrange("p (h n) -> p h n", h=2), ps[:, 6:8, :], ACT.Copy)

        @block.vector
        def _(dve):
            def weigh(c, s):
                for h in range(2):
                    n = c * 2 + h
                    dve.wait_ge(in_ready, n + 1)
                    if gated:
                        dve.tensor_tensor(inner[:, h, :], inner[:, h, :], ps[:, 2 + h, :], ALU.mult).then_inc(m_ready, 1)
                        dve.wait_ge(m_ready, n + 1)
                    dve.wait_ge(down_done, n + 1)
                    dve.tensor_tensor(a[:, h, :], inner[:, h, :], ps[:, SPREAD + h, :], ALU.mult).then_inc(a_ready, 1)
            bodies(dve, weigh)

        @block.tensor
        def _(pe):
            def product(bank, w, h, first, last):
                b = w[0]
                pe.matmul(ps[:, bank, :], wh[:, b, w[1]], k.xth[:, half(h)], start=True, stop=False)
                pe.matmul(ps[:, bank, :], wh[:, b, w[1]], k.xtl[:, half(h)], start=False, stop=False)
                return pe.matmul(ps[:, bank, :], wl[:, b, w[1]], k.xth[:, half(h)], start=False, stop=True)

            def up(c, b, pick_at):
                pe.wait_ge(wl_ready, c + 1)
                for h in range(2):
                    pe.wait_ge(a_ready, c * 2 + h + 1)
                    for m in range(nw - 1):
                        product(2 * m + h, (b, slice(m * P, m * P + P)), h, True, True)
                    pe.matmul(ps[:, SPREAD + h, :], pick[:, pick_at, :], cwt[:, 0, half(h)], start=True, stop=False)
                    pe.matmul(ps[:, SPREAD + h, :], pick[:, pick_at, :], cwt[:, 1, half(h)], start=False,
                              stop=True).then_inc(up_ready, 1)

            def down(c, b):
                for h in range(2):
                    pe.wait_ge(al_ready, c * 2 + h + 1)
                    pe.matmul(ps[:, 6 + h, :], wh[:, b, down_w], ah[:, h, :], start=False, stop=False, skip_group_check=True)
                    pe.matmul(ps[:, 6 + h, :], wl[:, b, down_w], ah[:, h, :], start=False, stop=False, skip_group_check=True)
                    pe.matmul(ps[:, 6 + h, :], wh[:, b, down_w], al[:, h, :], start=False, stop=False,
                              skip_group_check=True).then_inc(down_done, 1)

            for h in range(2):
                pe.matmul(ps[:, 6 + h, :], k.zero_h[:, 0:P], k.zero_h[:, :], start=True, stop=False,
                          skip_group_check=True)

            def at(c):
                return c // CPE if gated else c

            up(0, 0, at(0))
            if gated:
                with pe.Fori(0, E1 - 1) as i:
                    for s in range(CPE):
                        up(i * CPE + s + 1, (s + 1) % RAW, i + (s + 1) // CPE)
                        down(i * CPE + s, s % RAW)
                for c in range(nch - CPE, nch - 1):
                    up(c + 1, (c + 1) % RAW, at(c + 1))
                    down(c, c % RAW)
            else:
                with pe.Fori(0, (nch - 1) // RAW) as i:
                    for s in range(RAW):
                        up(i * RAW + s + 1, (s + 1) % RAW, i * RAW + s + 1)
                        down(i * RAW + s, s % RAW)
            down(nch - 1, (nch - 1) % RAW)

    residual(k, f"{tag}_res", y, gate)


def cross_attention(k, scope, wq1, wkv1, wo1):
    nc, ps = k.nc, k.ps
    NB = 3
    O_BANK, SIDE_BANK = NB, NB + 2
    START, GUSES = 4, TT + 2
    C_USE = START + G * TT + (G - 1) * 2
    USES = -(-(C_USE + 2) // NB) * NB
    assert (G - 1) % NB == 0
    GU = 2 * GT
    UNITS = G * GU
    R = 4
    LEAD = R - 1
    DVE_UNITS = [3, 7]
    POOL_UNITS = [u for u in range(GU) if u not in DVE_UNITS]
    ND = len(DVE_UNITS)
    LOW_LEAD = 2
    e = k.e[:, :, :].rearrange("p a (b n) -> p (a b) n", b=2)
    el = k.el[:, :, :].rearrange("p a (b n) -> p (a b) n", b=2)
    ka, kb = (k.sb(n, [P, 2, MP], FP16, scope) for n in ("keys_a", "keys_b"))
    v = k.sb("values", [P, 2, MT, 2 * DH + 1], FP16, scope)
    qa, qb = (k.sb(n, [P, 2, T], FP16, scope) for n in ("q_a", "q_b"))
    wqh, wql, wkh, wkl = (k.sb(n, [P, HEADS * P], FP16, scope) for n in ("wq_h", "wq_l", "wk_h", "wk_l"))
    wvh, wvl = (k.sb(n, [P, HEADS * DH], FP16, scope) for n in ("wv_h", "wv_l"))
    runmax = k.sb("run_max", [P, TT, G], FP32, scope)
    cmax = k.sb("c_max", [P, TT], FP32, scope)
    cz = k.sb("c_spread", [P, TT, P], FP16, scope)
    rec = k.sb("o_rec", [P, 2, GT], FP32, scope)
    att = k.sb("att_rows", [P, 2, GT, HEADS * DH], FP32, scope)
    acc = ps[:, O_BANK:O_BANK + 2, 0:GT * (DH + 1)].rearrange("p a (i d) -> p a i d", d=DH + 1)

    ld_w, h_ready, w_ch = k.sem("a1_ldw"), k.sem("a1_wh"), k.sem("a1_wch")
    with ExitStack() as ws:
        w = att[:, :, :, :].rearrange("p a i d -> p (a i d)")[:, 0:3 * HEADS * DH]
        with nc.Block() as block:
            @block.sync
            def _(sp):
                sp.dma_start(w[:, 0:HEADS * DH], wq1).then_inc(ld_w, 16)
                sp.dma_start(w[:, HEADS * DH:3 * HEADS * DH], wkv1).then_inc(ld_w, 16)

            @block.scalar
            def _(act):
                act.wait_ge(ld_w, 32)
                for n, hi in ((0, wqh), (1, wkh)):
                    src = w[:, n * HEADS * DH:(n + 1) * HEADS * DH].rearrange("p (h d) -> p h d", d=DH)
                    for s in range(2):
                        act.activation(hi[:, :].rearrange("p (h s d) -> p h s d", s=2, d=DH)[:, :, s, :], src,
                                       ACT.Copy).then_inc(h_ready, 1)
                act.activation(wvh[:, :], w[:, 2 * HEADS * DH:3 * HEADS * DH], ACT.Copy).then_inc(h_ready, 1)

            @block.vector
            def _(dve):
                dve.wait_ge(h_ready, 5)
                for n, hi, lo in ((0, wqh, wql), (1, wkh, wkl)):
                    src = w[:, n * HEADS * DH:(n + 1) * HEADS * DH].rearrange("p (h d) -> p h d", d=DH)
                    for s in range(2):
                        at = [x[:, :].rearrange("p (h s d) -> p h s d", s=2, d=DH)[:, :, s, :] for x in (lo, hi)]
                        dve.tensor_tensor(at[0], src, at[1], ALU.subtract)
                dve.tensor_tensor(wvl[:, :], w[:, 2 * HEADS * DH:3 * HEADS * DH], wvh[:, :], ALU.subtract)
                for b in range(2):
                    dve.tensor_copy(v[:, b, :, DH], k.mask[:, :])
                dve.wait_ge(w_ch, 2)
                for b in range(2):
                    dve.memset(kb[DH:DH + 1, b, :], 1.0)

            @block.gpsimd
            def _(pool):
                for b in range(2):
                    pool.memset(qb[DH:P, b, :], 0.0)
                    pool.memset(kb[DH:P, b, :], 0.0).then_inc(w_ch, 1)
                pool.wait_ge(w_ch, 2)
                pool.memset(cz[:, :, :], 0.0)

    side_ready, side_free, qc_ready, kh_ready, kb_ready, vh_ready, c_ready, cu_ready, c_dve = (
        k.sem(f"ap_{n}") for n in ("side_ready", "side_free", "qc", "kh", "kb", "vh", "c", "cu", "cdve"))
    s_ready, exp_done, pool_low, dve_low, pv_done, o_free, o_dve = (
        k.sem(f"am_{n}") for n in ("s", "exp", "pool_low", "dve_low", "pv", "o_free", "odve"))

    with nc.Block() as block:
        @block.scalar
        def _(act):
            act.sem_inc(exp_done, R)

        @block.tensor
        def _(pe):
            pe.sem_inc(pv_done, R)

        @block.vector
        def _(dve):
            dve.sem_inc(side_free, NB)
            dve.sem_inc(o_free, 1)

    with nc.Block() as block:
        def walk(eng, start, group, stop):
            def run(h, hb, n, nb):
                if start:
                    start(h, hb, n, nb)
                with eng.Fori(0, (G - 1) // NB) as gs:
                    for gi in range(NB):
                        group(h, hb, n, nb, gs * NB + gi, gi, False)
                group(h, hb, n, nb, G - 1, 0, True)
                if stop:
                    stop(h, hb, n, nb)
            run(None, 1, 0, 0)
            with eng.Fori(0, HEADS // 2 - 1) as hp:
                run(hp * 2, 0, hp * 2 + 1, 1)
                run(hp * 2 + 1, 1, hp * 2 + 2, 0)
            run(HEADS - 2, 0, HEADS - 1, 1)
            run(HEADS - 1, 1, None, 0)

        K_USE, Q_USE, V_USE = 0, 1, 3
        V_STEP, K_STEP = 2, 5
        USE_OF = {0: 0, 1: 1, 2: 3, 3: 4, 4: 5, 5: 7, 6: 8, 7: 9}
        GV_USE, GK_USE = 2, 6

        def maxima_of(u, last):
            if not last:
                return [(u, USE_OF[u])]
            return [(i, i) for i in (2 * u, 2 * u + 1) if i < TT]

        def bank(use):
            return SIDE_BANK + use % NB

        def group_bank(gi, use):
            return bank(START + gi * GUSES + use)

        def score_bank(gi, u):
            return (gi * GU + u) % NB

        @block.tensor
        def _(pe):
            def side(n, use, products):
                pe.wait_ge(side_free, n * USES + use + 1)
                for o, l, r, first, last in products:
                    ins = pe.matmul(o, l, r, start=first, stop=last)
                ins.then_inc(side_ready, 1)

            def keys(n, g, use, at_bank):
                at, cols_g = bass.ds(n * P, P), bass.ds(g * 512, 512)
                o = ps[:, at_bank, :]
                side(n, use, [(o, wkh[:, at], k.ch[:, cols_g], True, False),
                              (o, wkh[:, at], k.cl[:, cols_g], False, False),
                              (o, wkl[:, at], k.ch[:, cols_g], False, True)])

            def vals(n, g, use, at_bank):
                prods = []
                for u in range(GT):
                    o = ps[:, at_bank, DH * u:DH * u + DH]
                    rows, at = bass.ds(g * 512 + u * P, P), bass.ds(n * DH, DH)
                    prods += [(o, k.ch[:, rows], wvh[:, at], True, False),
                              (o, k.ch[:, rows], wvl[:, at], False, False),
                              (o, k.cl[:, rows], wvh[:, at], False, True)]
                side(n, use, prods)

            def scores(h, hb, g, u, b):
                pe.wait_ge(exp_done, h * UNITS + g * GU + u + 1 + R - NB)
                at = bass.ds(g * 512 + u // 2 * P, P)
                pe.matmul(ps[:, b, :], ka[:, hb, at], qa[:, hb, half(u % 2)], start=True, stop=False)
                pe.matmul(ps[:, b, :], kb[:, hb, at], qb[:, hb, half(u % 2)], start=False,
                          stop=True).then_inc(s_ready, 1)

            def values(h, hb, g, u):
                if u in DVE_UNITS:
                    pe.wait_ge(dve_low, h * (G * ND) + g * ND + DVE_UNITS.index(u) + 1)
                else:
                    pe.wait_ge(pool_low, h * (G * (GU - ND)) + g * (GU - ND) + POOL_UNITS.index(u) + 1)
                j = g * GT + u // 2
                for i in range(GT):
                    o = acc[:, u % 2, i, :]
                    eh = top(e[:, u % R, tile(i)])
                    pe.matmul(o, eh, v[:, hb, j, 0:DH + 1], start=False, stop=False, skip_group_check=True)
                    pe.matmul(o[:, 0:DH], eh, v[:, hb, j, DH + 1:2 * DH + 1], start=False, stop=False, skip_group_check=True)
                    ins = pe.matmul(o, el[:, u % R, tile(i)], v[:, hb, j, 0:DH + 1], start=False, stop=False,
                                    skip_group_check=True)
                ins.then_inc(pv_done, 1)

            def start(h, hb, n, nb):
                if n is not None:
                    keys(n, 0, K_USE, bank(K_USE))
                    at = bass.ds(n * P, P)
                    for c in range(2):
                        o = ps[:, bank(Q_USE + c), :]
                        side(n, Q_USE + c, [(o, wqh[:, at], k.xth[:, half(c)], True, False),
                                            (o, wqh[:, at], k.xtl[:, half(c)], False, False),
                                            (o, wql[:, at], k.xth[:, half(c)], False, True)])
                    vals(n, 0, V_USE, bank(V_USE))
                if h is not None:
                    pe.wait_ge(o_free, h + 1)
                    for c in range(2):
                        pe.matmul(ps[:, O_BANK + c, :], k.zero_h[:, 0:P], k.zero_h[:, :], start=True, stop=False,
                                  skip_group_check=True)

            def group(h, hb, n, nb, g, gi, last):
                for u in range(GU):
                    if h is not None and not (last and u + LEAD >= GU):
                        scores(h, hb, g, u + LEAD, score_bank(gi, u + LEAD))
                    if n is not None and not last and u == V_STEP:
                        vals(n, g + 1, START + g * GUSES + GV_USE, group_bank(gi, GV_USE))
                    if n is not None and not last and u == K_STEP:
                        keys(n, g + 1, START + g * GUSES + GK_USE, group_bank(gi, GK_USE))
                    if h is not None:
                        values(h, hb, g, u)
                    if n is not None:
                        for i, use in maxima_of(u, last):
                            side(n, START + g * GUSES + use, [(ps[:, group_bank(gi, use), :], qa[:, nb, tile(i)],
                                                               ka[:, nb, bass.ds(g * 512, 512)], True, True)])
                    if n is not None and last:
                        if u == GU - LEAD - 1:
                            pe.wait_ge(c_ready, n + 1)
                            for c in range(2):
                                side(n, C_USE + c, [(ps[:, bank(C_USE + c), tile(i)], cz[:, 4 * c + i, :],
                                                     k.ident_h[:, :], True, True) for i in range(4)])
                        if u == GU - LEAD:
                            pe.wait_ge(side_free, n * USES + USES + NB)
                            pe.wait_ge(cu_ready, n + 1)
                            pe.sem_inc(side_ready, USES - C_USE - 2)
                            pe.wait_ge(kb_ready, n * G + G)
                            if h is not None:
                                pe.wait_ge(exp_done, h * UNITS + UNITS + R)
                        if u >= GU - LEAD:
                            scores(n, nb, 0, u + LEAD - GU, score_bank(0, u + LEAD - GU))

            walk(pe, start, group, None)

        @block.scalar
        def _(act):
            def keys(n, nb, g, use, at_bank):
                cols_g = bass.ds(g * 512, 512)
                act.wait_ge(side_ready, n * USES + use + 1)
                act.activation(ka[:, nb, cols_g], ps[:, at_bank, :], ACT.Copy).then_inc(kh_ready, 1)
                act.wait_ge(kh_ready, n * G + g + 1)
                act.activation(kb[0:DH, nb, cols_g], ka[0:DH, nb, cols_g], ACT.Copy).then_inc(kb_ready, 1)

            def vals(n, nb, g, use, at_bank):
                act.wait_ge(side_ready, n * USES + use + 1)
                act.activation(v[:, nb, bass.ds(g * GT, GT), 0:DH],
                               ps[:, at_bank, 0:GT * DH].rearrange("p (u d) -> p u d", d=DH),
                               ACT.Copy).then_inc(vh_ready, 1)

            def exps(h, g, u, b):
                act.wait_ge(s_ready, h * UNITS + g * GU + u + 1)
                act.wait_ge(pv_done, h * UNITS + g * GU + u + 1)
                act.activation(e[:, u % R, :], ps[:, b, :], ACT.Exp).then_inc(exp_done, 1)

            def start(h, hb, n, nb):
                if n is not None:
                    keys(n, nb, 0, K_USE, bank(K_USE))
                    for c in range(2):
                        act.wait_ge(side_ready, n * USES + Q_USE + c + 1)
                        act.activation(qa[:, nb, half(c)], ps[:, bank(Q_USE + c), :], ACT.Copy, scale=HEAD_SCALE).then_inc(qc_ready, 1)
                    vals(n, nb, 0, V_USE, bank(V_USE))

            def group(h, hb, n, nb, g, gi, last):
                for u in range(GU):
                    if h is not None and not (last and u + LEAD >= GU):
                        exps(h, g, u + LEAD, score_bank(gi, u + LEAD))
                    if n is not None and not last and u == V_STEP:
                        vals(n, nb, g + 1, START + g * GUSES + GV_USE, group_bank(gi, GV_USE))
                    if n is not None and not last and u == K_STEP:
                        keys(n, nb, g + 1, START + g * GUSES + GK_USE, group_bank(gi, GK_USE))
                    if n is not None and last and u == GU - LEAD - 1:
                        act.wait_ge(side_ready, n * USES + C_USE + 2)
                        act.activation(qb[DH:DH + 1, nb, half(1)], ps[DH:DH + 1, bank(C_USE + 1), :], ACT.Copy).then_inc(cu_ready, 1)
                    if n is not None and last and u >= GU - LEAD:
                        exps(n, 0, u + LEAD - GU, score_bank(0, u + LEAD - GU))

            act.preload_act_table(ACT.Exp)
            walk(act, start, group, None)

        @block.gpsimd
        def _(pool):
            def group(h, hb, n, nb, g, gi, last):
                if h is not None:
                    for u in POOL_UNITS:
                        pool.wait_ge(exp_done, h * UNITS + g * GU + u + 1 + R)
                        pool.tensor_tensor(el[:, u % R, :], e[:, u % R, :], top(e[:, u % R, :]),
                                           ALU.subtract).then_inc(pool_low, 1)

            walk(pool, None, group, None)

        @block.vector
        def _(dve):
            def low_values(n, nb, g, at_bank):
                rows = bass.ds(g * GT, GT)
                dve.wait_ge(vh_ready, n * G + g + 1)
                dve.tensor_tensor(v[:, nb, rows, DH + 1:2 * DH + 1],
                                  ps[:, at_bank, 0:GT * DH].rearrange("p (u d) -> p u d", d=DH),
                                  v[:, nb, rows, 0:DH], ALU.subtract).then_inc(side_free, 1)

            def low_keys(n, nb, g, at_bank):
                cols_g = bass.ds(g * 512, 512)
                dve.wait_ge(kh_ready, n * G + g + 1)
                dve.tensor_tensor(ka[DH:P, nb, cols_g], ps[DH:P, at_bank, :], ka[DH:P, nb, cols_g],
                                  ALU.subtract).then_inc(side_free, 1)

            def start(h, hb, n, nb):
                if n is not None:
                    low_keys(n, nb, 0, bank(K_USE))
                    for c in range(2):
                        dve.wait_ge(qc_ready, n * 2 + c + 1)
                        dve.scalar_tensor_tensor(out=qb[0:DH, nb, half(c)], in0=ps[0:DH, bank(Q_USE + c), :], scalar=HEAD_SCALE,
                                                 in1=qa[0:DH, nb, half(c)], op0=ALU.mult,
                                                 op1=ALU.subtract).then_inc(side_free, 1)
                    low_values(n, nb, 0, bank(V_USE))

            def group(h, hb, n, nb, g, gi, last):
                for u in range(GU):
                    if h is not None and (u + LOW_LEAD) % GU in DVE_UNITS and u + LOW_LEAD < GU:
                        w = u + LOW_LEAD
                        dve.wait_ge(exp_done, h * UNITS + g * GU + w + 1 + R)
                        dve.tensor_tensor(el[:, w % R, :], e[:, w % R, :], top(e[:, w % R, :]),
                                          ALU.subtract).then_inc(dve_low, 1)
                    if n is not None and not last and u == V_STEP:
                        low_values(n, nb, g + 1, group_bank(gi, GV_USE))
                    if n is not None and not last and u == K_STEP:
                        low_keys(n, nb, g + 1, group_bank(gi, GK_USE))
                    if n is not None:
                        for i, use in maxima_of(u, last):
                            dve.wait_ge(side_ready, n * USES + START + g * GUSES + use + 1)
                            dve.tensor_reduce(runmax[:, i, bass.ds(g, 1)], ps[:, group_bank(gi, use), :], AX.X,
                                              ALU.max).then_inc(side_free, 1)
                    if n is not None and last and u == TT // 2 - 1:
                        dve.wait_ge(side_free, n * USES + C_USE + NB)
                        dve.tensor_reduce(cmax[:, :], runmax[:, :, :], AX.X, ALU.max).then_inc(c_dve, 1)
                        dve.wait_ge(c_dve, n + 1)
                        dve.tensor_scalar(cz[:, :, DH], cmax[:, :], -1.0, LIFT, ALU.mult, ALU.add).then_inc(c_ready, 1)
                        rows = slice(MT - GT, MT)
                        dve.tensor_tensor(v[:, nb, rows, :], v[:, nb, rows, :],
                                          k.mask[:, rows].unsqueeze(2).to_broadcast([P, GT, 2 * DH + 1]), ALU.mult)
                    if n is not None and last and u == GU - LEAD:
                        dve.wait_ge(side_ready, n * USES + C_USE + 1)
                        dve.tensor_copy(qb[DH:DH + 1, nb, half(0)],
                                        ps[DH:DH + 1, bank(C_USE), :]).then_inc(side_free, USES - C_USE)

            def stop(h, hb, n, nb):
                if h is not None:
                    dve.wait_ge(pv_done, h * UNITS + UNITS + R)
                    dve.reciprocal(rec[:, :, :], acc[:, :, :, DH]).then_inc(o_dve, 1)
                    dve.wait_ge(o_dve, h + 1)
                    for a in range(2):
                        ins = dve.tensor_tensor(att[:, a, :, bass.ds(h * DH, DH)], acc[:, a, :, 0:DH],
                                                rec[:, a, :].unsqueeze(2).to_broadcast([P, GT, DH]), ALU.mult)
                    ins.then_inc(o_free, 1)

            walk(dve, start, group, stop)

    output_projection(k, att, wo1)


def output_projection(k, att, wo1):
    nc, ps = k.nc, k.ps
    NCK = HEADS * DH // P
    wo = k.ch[:, 0:NCK * P * 2].bitcast(FP32).rearrange("p (c d) -> p c d", c=NCK)
    at = k.e
    ld, turned, copied, y_ready = (k.sem(f"wo_{n}") for n in ("ld", "turned", "copied", "y"))
    with nc.Block() as block:
        @block.sync
        def _(sp):
            sp.dma_start(wo, wo1.rearrange("(c p) d -> p c d", p=P)).then_inc(ld, 16)

        @block.tensor
        def _(pe):
            for n in range(2):
                pe.matmul(ps[:, 4 + n, :], k.zero_h[:, 0:P], k.zero_h[:, :], start=True, stop=False, skip_group_check=True)

            def turn(c):
                if c >= 2:
                    pe.wait_ge(copied, c - 1)
                for i in range(TT):
                    ins = pe.transpose(ps[:, 2 * (c % 2) + i // GT, tile(i % GT)], att[:, i // GT, i % GT, tile(c)], k.ident[:, :])
                ins.then_inc(turned, 1)

            turn(0)
            pe.wait_ge(ld, 16)
            for c in range(NCK):
                if c + 1 < NCK:
                    turn(c + 1)
                pe.wait_ge(copied, c + 1)
                for i in range(TT):
                    ins = pe.matmul(ps[:, 4 + i // GT, tile(i % GT)], at[:, c % 2, tile(i)], wo[:, c, :],
                                    start=False, stop=False, skip_group_check=True)
            ins.then_inc(y_ready, 1)

        @block.scalar
        def _(act):
            for c in range(NCK):
                act.wait_ge(turned, c + 1)
                b = c % 2
                act.activation(at[:, b, :].rearrange("p (h n) -> p h n", h=2), ps[:, 2 * b:2 * b + 2, :],
                               ACT.Copy).then_inc(copied, 1)

        @block.vector
        def _(dve):
            dve.wait_ge(y_ready, 1)
            rows = k.x[:, :, :].rearrange("p (a i) d -> p a (i d)", a=2)
            dve.scalar_tensor_tensor(out=rows, in0=ps[:, 4:6, :], scalar=k.tg[:, 2:3], in1=rows, op0=ALU.mult, op1=ALU.add)


def kernel(**inputs):
    import numpy as np
    import concourse.bacc as bacc
    from concourse import mybir as my
    from concourse.bass_utils import run_bass_kernel_spmd as run

    a = {n: np.asarray(v) for n, v in inputs.items()}
    f = np.float32
    x = np.ascontiguousarray(a["x"])
    bih, bhh = (a[f"L0_xattn_gru_{n}"].reshape(3, 128) for n in ("bih", "bhh"))
    arrays = {
        "x": x,
        "ctx": np.ascontiguousarray(a["ctx_1024"]),
        "cols": np.ascontiguousarray(np.stack(
            [a["L0_xattn_input_norm_w"], a["L0_xattn_slot_norm_w"], *bih, *bhh, a["L1_xattn_ln_g"], a["L1_xattn_ln_b"]], 1)),
        "gates": np.ascontiguousarray(np.broadcast_to(
            np.stack([a["g_xattn"], a["g_ffn"]], 1).reshape(1, 4), (128, 4))),
        "slot_w": np.ascontiguousarray(np.concatenate(
            [a["L0_xattn_Wq"].T, a["L0_xattn_Wk"], a["L0_xattn_Wv"].T, a["L0_xattn_gru_wih"].T, a["L0_xattn_gru_whh"].T], 1)),
        "cent_t": np.ascontiguousarray(a["L0_ffn_centroids"].T),
        "bias_e": np.ascontiguousarray(np.broadcast_to(a["L0_ffn_expert_biases"][None], (128, 64))),
        "wq1": np.ascontiguousarray(a["L1_xattn_Wq"]),
        "wkv1": np.ascontiguousarray(a["L1_xattn_Wkv"]),
        "wo1": np.ascontiguousarray(a["L1_xattn_Wo"]),
        "rout_w": np.ascontiguousarray(np.concatenate([a["L1_ffn_w_router"], a["L1_ffn_w_gating"]], 1)),
    }
    up = a["L0_ffn_W_up"].reshape(32, 2, 128, 64).transpose(0, 2, 1, 3).reshape(32, 128, 128)
    dn = a["L0_ffn_W_down"].reshape(32, 128, 128)
    w0 = np.zeros((33, 128, 256), f)
    w0[:32, :, :128], w0[:32, :, 128:] = up, dn
    w0[32, :, :64], w0[32, :64, 128:] = a["L0_ffn_Ws_up"], a["L0_ffn_Ws_down"]
    arrays["ffn0_w"] = w0
    gt, up = (a[n].reshape(8, 128, 4, 128).transpose(0, 2, 1, 3).reshape(32, 128, 128) for n in ("L1_ffn_w_gate", "L1_ffn_w_up"))
    dn = a["L1_ffn_w_down"].reshape(32, 128, 128)
    arrays["ffn1_w"] = np.ascontiguousarray(np.concatenate([gt, up, dn], 2))

    nc = bacc.Bacc("TRN2", target_bir_lowering=False, num_devices=1)
    args = {n: nc.dram_tensor(f"in_{n}", v.shape, my.dt.from_np(v.dtype), kind="ExternalInput").ap() for n, v in arrays.items()}
    out = nc.dram_tensor("out", (1, 1024, 128), my.dt.float32, kind="ExternalOutput").ap()
    build(nc, args["x"], args["ctx"], *(args[n] for n in (
        "cols", "gates", "slot_w", "cent_t", "bias_e", "wq1", "wkv1", "wo1", "rout_w", "ffn0_w", "ffn1_w")), out)
    r = run(nc, [{f"in_{n}": v for n, v in arrays.items()}], core_ids=[0])
    return r.results[0]["out"]
```

```python
import math

import concourse.bass as bass
from concourse import mybir
from contextlib import ExitStack

FP32 = mybir.dt.float32
BF16 = mybir.dt.bfloat16
FP16 = mybir.dt.float16
ALU = mybir.AluOpType
ACT = mybir.ActivationFunctionType
AX = mybir.AxisListType

P = 128
D = 128
T = 1024
TT = T // P
M = 6404
GT = 4
G = -(-M // (P * GT))
MT = G * GT
MP = MT * P
FULL = M // P
TAIL = M - FULL * P
UT = -(-M // P)
HEADS, DH = 16, 64
NITER = 3
SLOT_SCALE = D ** -0.5
HEAD_SCALE = DH ** -0.5
LIFT = 12 * math.log(2.0)
VAL_SCALE = float(2 ** 20)
SLOT_EPS = 1e-6
TWO_ONES = 2.0 ** -7 * (1 + 0x3C00 / 2 ** 23)
E0, F0 = 64, 64
CH0 = E0 // 2 + 1
E1, F1 = 8, 512
CPE = F1 // P
TOPK = 8
CREDIT = 2
C_WIN, C_WSLOT, C_BIR, C_BIZ, C_BIN, C_BHR, C_BHZ, C_BHN, C_LNG, C_LNB = range(10)


def top(ap):
    return ap.bitcast(BF16).rearrange("p (n b) -> p b n", b=2)[:, 1, :]


def half(h):
    return slice(512 * h, 512 * h + 512)


def tile(i):
    return slice(P * i, P * i + P)


class Chain:

    def __init__(self, eng, sem, base=0):
        self.eng, self.sem, self.n = eng, sem, base

    def __call__(self, ins):
        self.n = self.n + 1
        ins.then_inc(self.sem, 1)
        self.eng.wait_ge(self.sem, self.n)


class Core:

    def __init__(self, nc, ctx):
        self.nc, self.ctx = nc, ctx

    def sb(self, name, shape, dt=FP32, ctx=None):
        return (ctx or self.ctx).enter_context(self.nc.sbuf_tensor(name, shape, dt))

    def sem(self, name):
        return self.ctx.enter_context(self.nc.semaphore(name))


def build(nc, x, ctx_rows, cols, gates, slot_w, cent_t, bias_e, wq1, wkv1, wo1, rout_w, ffn0_w, ffn1_w, out):
    with ExitStack() as stack:
        k = Core(nc, stack)
        k.x = k.sb("x_rows", [P, TT, D])
        k.cols = k.sb("cols_sb", [P, 10])
        k.gates = k.sb("gates_sb", [P, 4])
        k.tg = k.sb("tanh_gates", [P, 4])
        k.cent = k.sb("centroids_t", [P, E0])
        k.bias_e = k.sb("expert_bias", [P, E0])
        k.rout = k.sb("router_w", [P, 2 * E1])
        k.ident = k.sb("ident", [P, P])
        k.ident_h = k.sb("ident_h", [P, P], FP16)
        k.mean_w = k.sb("mean_w", [P, P])
        k.zero_h = k.sb("zero_h", [P, 512], FP16)
        k.eps5 = k.sb("eps5", [P, 1])
        k.eps6 = k.sb("eps6", [P, 1])
        k.bsum = k.sb("gru_bias_sum", [P, 2])
        k.win_s = k.sb("win_scaled", [P, 1])
        k.mask = k.sb("row_mask", [P, MT])
        k.ch = k.sb("ctx_t_hi", [P, MP], FP16)
        k.cl = k.sb("ctx_t_lo", [P, MP], FP16)
        k.xt = k.sb("xn_t", [P, T])
        k.xth = k.sb("xn_t_hi", [P, T], FP16)
        k.xtl = k.sb("xn_t_lo", [P, T], FP16)
        k.e = k.sb("exps", [P, 2, T])
        k.el = k.sb("exps_lo", [P, 2, T], FP16)
        k.stats = k.sb("stats", [P, TT, 6])
        k.mv = k.sb("mean_var", [P, TT, 2])
        k.ps = stack.enter_context(nc.psum_tensor("ps", [P, 8, 512], FP32))

        with ExitStack() as l0:
            k.pn = k.sb("ctx_rms", [P, MT, D + 1], FP32, l0)
            k.pth = k.sb("ctx_rms_t_hi", [P, MP], FP16, l0)
            k.ptl = k.sb("ctx_rms_t_lo", [P, MP], FP16, l0)
            with ExitStack() as pro:
                prologue(k, pro, x, ctx_rows, cols, gates, cent_t, bias_e, rout_w)
            with ExitStack() as at:
                slot_attention(k, at, slot_w)
        with ExitStack() as f0:
            normed(k, "n1")
            cwt = k.sb("ffn0_cw", [P, 2, T], FP16, f0)
            with ExitStack() as r:
                top_experts(k, r, cwt)
            experts(k, f0, "f0", cwt, ffn0_w, 1)
        with ExitStack() as a1:
            att, ld_w = attention_weights(k, a1, wq1, wkv1)
            normed(k, "n2")
            cross_attention(k, a1, att, ld_w, wo1)
        with ExitStack() as f1:
            normed(k, "n3")
            cwt = k.sb("ffn1_cw", [P, 2, T], FP16, f1)
            with ExitStack() as r:
                soft_experts(k, r, cwt)
            experts(k, f1, "f1", cwt, ffn1_w, 3)
        out_done = k.sem("out_done")
        with nc.Block() as block:
            @block.sync
            def _(sp):
                sp.dma_start(out[0].rearrange("(i p) d -> p i d", p=P), k.x[:, :, :]).then_inc(out_done, 16)
                sp.wait_ge(out_done, 16)


def prologue(k, scope, x, ctx_rows, cols, gates, cent_t, bias_e, rout_w):
    nc, ps = k.nc, k.ps
    CH = 13
    rows = k.sb("ctx_rows", [P, MT, D], FP32, scope)
    st = k.sb("ctx_stats", [P, MT, 6], FP32, scope)
    mv = k.sb("ctx_mv", [P, MT, 2], FP32, scope)
    rms = k.sb("ctx_rms_r", [P, MT], FP32, scope)
    rms_v = k.sb("ctx_rms_v", [P, MT], FP32, scope)
    lnr = k.sb("ctx_ln_r", [P, MT], FP32, scope)
    lnm = k.sb("ctx_ln_m", [P, MT], FP32, scope)
    sd = k.sb("ctx_sd", [P, 2, MT], FP32, scope)
    rn = k.sb("ctx_rn", [P, 2, GT, D], FP32, scope)
    ln = k.sb("ctx_ln", [P, 2, GT, D], FP32, scope)
    lt = k.sb("ctx_ln_t", [P, 2, 512], FP32, scope)
    ld_small, ld_x = k.sem("ld_small"), k.sem("ld_x")
    ld_ctx = [k.sem(f"ld_ctx{c}") for c in range(MT // CH)]
    ready = k.sem("pro_consts")
    d_ch, g_ch = k.sem("pro_dve"), k.sem("pro_pool")
    stats_done, aggr_done, msq_ready, sd_ready = (k.sem(n) for n in ("c_stats", "c_aggr", "c_msq", "c_sd"))
    mask_ready, rms_ready = k.sem("c_mask"), k.sem("c_rms")
    pn_ready, ln_ready, pt_ready, lt_ps, pth_done, lt_done, ch_done, ptl_done, cl_done = (
        k.sem(n) for n in ("pn_ready", "ln_ready", "pt_ready", "lt_ps", "pth_done", "lt_done", "ch_done", "ptl_done", "cl_done"))

    def groups(eng, body):
        with eng.Fori(0, G // 2) as i:
            body(i * 2, 0)
            body(i * 2 + 1, 1)
        body(G - 1, 0)

    with nc.Block() as block:
        @block.sync
        def _(sp):
            body = ctx_rows[0, 0:FULL * P, :].rearrange("(j p) d -> p j d", p=P)
            last = ctx_rows[0, M - P:M, :]
            for c in range(MT // CH):
                hi = min(FULL, CH * (c + 1))
                sp.dma_start(rows[:, CH * c:hi, :], body[:, CH * c:hi, :]).then_inc(ld_ctx[c], 16)
            for j in range(FULL, MT):
                sp.dma_start(rows[:, j, :], last).then_inc(ld_ctx[-1], 16)
            for dst, src in ((k.cols, cols), (k.gates, gates), (k.cent, cent_t), (k.bias_e, bias_e), (k.rout, rout_w)):
                sp.dma_start(dst[:, :], src).then_inc(ld_small, 16)
            sp.dma_start(k.x[:, :, :], x[0].rearrange("(i p) d -> p i d", p=P)).then_inc(ld_x, 16)
            sp.wait_ge(ld_x, 16)

        @block.gpsimd
        def _(pool):
            chain = Chain(pool, g_ch)
            chain(pool.memset(k.ident[:, :], 0.0))
            chain(pool.affine_select(out=k.ident[:, :], in_=k.ident[:, :], compare_op=ALU.not_equal, fill=1.0,
                                     base=0, pattern=[[-1, P]], channel_multiplier=1))
            pool.tensor_copy(k.ident_h[:, :], k.ident[:, :]).then_inc(ready, 1)
            chain(pool.memset(k.mask[:, :], 1.0))
            chain(pool.memset(k.mask[:, FULL + 1:MT], 0.0))
            pool.affine_select(out=k.mask[:, FULL:FULL + 1], in_=k.mask[:, FULL:FULL + 1], compare_op=ALU.is_ge,
                               fill=0.0, base=TAIL - P, pattern=[[0, 1]], channel_multiplier=1).then_inc(mask_ready, 1)
            pool.wait_ge(rms_ready, 1)

            def rest(g, b):
                tiles = bass.ds(g * GT, GT)
                pool.tensor_tensor(k.pn[:, tiles, 0:D], rows[:, tiles, :],
                                   rms_v[:, tiles].unsqueeze(2).to_broadcast([P, GT, D]), ALU.mult)
                pool.wait_ge(ch_done, g + 1)
                pool.tensor_tensor(k.cl[:, bass.ds(g * 512, 512)], lt[:, b, :], k.ch[:, bass.ds(g * 512, 512)],
                                   ALU.subtract).then_inc(cl_done, 1)

            groups(pool, rest)

        @block.vector
        def _(dve):
            chain = Chain(dve, d_ch)
            dve.memset(k.mean_w[:, :], 1.0 / D)
            dve.memset(k.zero_h[:, :], 0.0)
            dve.memset(k.eps5[:, :], 1e-5)
            chain(dve.memset(k.eps6[:, :], 1e-6))
            for c in range(MT // CH):
                dve.wait_ge(ld_ctx[c], 16 * (1 + (c == MT // CH - 1) * (MT - FULL)))
                for j in range(CH * c, CH * c + CH):
                    dve.bn_stats(st[:, j, :], rows[:, j, :]).then_inc(stats_done, 1)
                dve.wait_ge(stats_done, CH * c + CH)
                for j in range(CH * c, CH * c + CH):
                    dve.bn_aggr(mv[:, j, :], st[:, j, :]).then_inc(aggr_done, 1)
            dve.wait_ge(aggr_done, MT)
            chain(dve.tensor_tensor(lnm[:, :], mv[:, :, 0], mv[:, :, 0], ALU.mult))
            dve.tensor_tensor(rms[:, :], lnm[:, :], mv[:, :, 1], ALU.add).then_inc(msq_ready, 1)
            dve.wait_ge(sd_ready, 2)
            chain(dve.reciprocal(rms[:, :], sd[:, 0, :]))
            chain(dve.reciprocal(lnr[:, :], sd[:, 1, :]))
            dve.scalar_tensor_tensor(out=lnm[:, :], in0=mv[:, :, 0], scalar=-1.0, in1=lnr[:, :],
                                     op0=ALU.mult, op1=ALU.mult)
            dve.wait_ge(mask_ready, 1)
            dve.tensor_scalar(k.pn[:, :, D], k.mask[:, :], VAL_SCALE, None, ALU.mult)
            chain(dve.tensor_tensor(rms[:, :], rms[:, :], k.mask[:, :], ALU.mult))
            dve.tensor_scalar(rms_v[:, :], rms[:, :], VAL_SCALE, None, ALU.mult).then_inc(rms_ready, 1)
            dve.wait_ge(ld_small, 16 * 5)
            dve.tensor_tensor(k.bsum[:, :], k.cols[:, C_BIR:C_BIZ + 1], k.cols[:, C_BHR:C_BHZ + 1], ALU.add)
            dve.tensor_scalar(k.win_s[:, :], k.cols[:, C_WIN:C_WIN + 1], SLOT_SCALE, None, ALU.mult)

            def rows_of(g, b):
                dve.wait_ge(pt_ready, g + 1)
                for u in range(GT):
                    j = g * GT + u
                    ins = dve.tensor_scalar(rn[:, b, u, :], rows[:, j, :], rms[:, bass.ds(j, 1)], None, ALU.mult)
                ins.then_inc(pn_ready, 1)
                dve.wait_ge(lt_ps, g + 1)
                for u in range(GT):
                    j = g * GT + u
                    ins = dve.tensor_scalar(ln[:, b, u, :], rows[:, j, :], lnr[:, bass.ds(j, 1)], lnm[:, bass.ds(j, 1)],
                                            ALU.mult, ALU.add)
                ins.then_inc(ln_ready, 1)

            def lows(g, b):
                dve.wait_ge(pth_done, g + 1)
                dve.tensor_tensor(k.ptl[:, bass.ds(g * 512, 512)], ps[:, b, :], k.pth[:, bass.ds(g * 512, 512)],
                                  ALU.subtract).then_inc(ptl_done, 1)

            rows_of(0, 0)
            with dve.Fori(0, G // 2) as i:
                for b in range(2):
                    rows_of(i * 2 + b + 1, 1 - b)
                    lows(i * 2 + b, b)
            lows(G - 1, 0)

        @block.tensor
        def _(pe):
            pe.sem_inc(lt_ps, CREDIT)
            pe.sem_inc(pt_ready, CREDIT)
            pe.wait_ge(ready, 1)

            def turn(g, b):
                pe.wait_ge(pn_ready, g + 1)
                pe.wait_ge(ptl_done, g + 1)
                for u in range(GT):
                    ins = pe.transpose(ps[:, b, tile(u)], rn[:, b, u, :], k.ident[:, :])
                ins.then_inc(pt_ready, 1)
                pe.wait_ge(ln_ready, g + 1)
                pe.wait_ge(lt_done, g + 1)
                for u in range(GT):
                    ins = pe.transpose(ps[:, 2 + b, tile(u)], ln[:, b, u, :], k.ident[:, :])
                ins.then_inc(lt_ps, 1)

            groups(pe, turn)

        @block.scalar
        def _(act):
            act.sem_inc(lt_done, CREDIT)
            act.sem_inc(ptl_done, CREDIT)
            act.sem_inc(cl_done, CREDIT)
            act.wait_ge(msq_ready, 1)
            act.activation(sd[:, 0, :], rms[:, :], ACT.Sqrt, bias=k.eps6[:, :]).then_inc(sd_ready, 1)
            act.activation(sd[:, 1, :], mv[:, :, 1], ACT.Sqrt, bias=k.eps5[:, :]).then_inc(sd_ready, 1)
            act.wait_ge(ld_small, 16 * 5)
            act.wait_ge(rms_ready, 1)

            def split(g, b):
                act.wait_ge(pt_ready, g + 1 + CREDIT)
                act.activation(k.pth[:, bass.ds(g * 512, 512)], ps[:, b, :], ACT.Copy).then_inc(pth_done, 1)
                act.wait_ge(lt_ps, g + 1 + CREDIT)
                act.wait_ge(cl_done, g + 1)
                act.activation(lt[:, b, :], ps[:, 2 + b, :], ACT.Identity, bias=k.cols[:, C_LNB:C_LNB + 1],
                               scale=k.cols[:, C_LNG:C_LNG + 1]).then_inc(lt_done, 1)
                act.wait_ge(lt_done, g + 1 + CREDIT)
                act.activation(k.ch[:, bass.ds(g * 512, 512)], lt[:, b, :], ACT.Copy).then_inc(ch_done, 1)

            groups(act, split)
            act.activation(k.tg[:, :], k.gates[:, :], ACT.Tanh)

    norm_rows(k, scope, "n0")


def normed(k, tag):
    with ExitStack() as scope:
        norm_rows(k, scope, tag)


def norm_rows(k, scope, tag):
    nc, ps = k.nc, k.ps
    xn = k.sb(f"{tag}_rows", [P, TT, D], FP32, scope)
    sd = k.sb(f"{tag}_sd", [P, 3, TT], FP32, scope)
    stats_done, aggr_done, sd_ready, rows_ready, turned, hi_ready, d_ch = (
        k.sem(f"{tag}_{n}") for n in ("stats", "aggr", "sdr", "rows_ready", "turned", "hi", "dve"))
    with nc.Block() as block:
        @block.vector
        def _(dve):
            chain = Chain(dve, d_ch)
            for i in range(TT):
                dve.bn_stats(k.stats[:, i, :], k.x[:, i, :]).then_inc(stats_done, 1)
            dve.wait_ge(stats_done, TT)
            for i in range(TT):
                dve.bn_aggr(k.mv[:, i, :], k.stats[:, i, :]).then_inc(aggr_done, 1)
            dve.wait_ge(sd_ready, 1)
            chain(dve.reciprocal(sd[:, 1, :], sd[:, 0, :]))
            chain(dve.scalar_tensor_tensor(out=sd[:, 2, :], in0=k.mv[:, :, 0], scalar=-1.0, in1=sd[:, 1, :],
                                           op0=ALU.mult, op1=ALU.mult))
            for i in range(TT):
                dve.tensor_scalar(xn[:, i, :], k.x[:, i, :], sd[:, 1, i:i + 1], sd[:, 2, i:i + 1],
                                  ALU.mult, ALU.add).then_inc(rows_ready, 1)
            for h in range(2):
                dve.wait_ge(hi_ready, h + 1)
                dve.tensor_tensor(k.xtl[:, half(h)], ps[:, h, :], k.xth[:, half(h)], ALU.subtract)

        @block.scalar
        def _(act):
            act.wait_ge(aggr_done, TT)
            act.activation(sd[:, 0, :], k.mv[:, :, 1], ACT.Sqrt, bias=k.eps5[:, :]).then_inc(sd_ready, 1)
            for h in range(2):
                act.wait_ge(turned, h + 1)
                act.activation(k.xt[:, half(h)], ps[:, h, :], ACT.Copy)
                act.activation(k.xth[:, half(h)], ps[:, h, :], ACT.Copy).then_inc(hi_ready, 1)

        @block.tensor
        def _(pe):
            for h in range(2):
                for i in range(4 * h, 4 * h + 4):
                    pe.wait_ge(rows_ready, i + 1)
                    ins = pe.transpose(ps[:, h, tile(i - 4 * h)], xn[:, i, :], k.ident[:, :])
                ins.then_inc(turned, 1)


def residual(k, tag, src_t, gate):
    nc, ps = k.nc, k.ps
    turned = k.sem(f"{tag}_turned")
    with nc.Block() as block:
        @block.tensor
        def _(pe):
            for i in range(TT):
                ins = pe.transpose(ps[:, i // 4, tile(i % 4)], src_t[:, tile(i)], k.ident[:, :])
                if i % 4 == 3:
                    ins.then_inc(turned, 1)

        @block.vector
        def _(dve):
            for h in range(2):
                dve.wait_ge(turned, h + 1)
                rows = k.x[:, 4 * h:4 * h + 4, :].rearrange("p i d -> p (i d)")
                dve.scalar_tensor_tensor(out=rows, in0=ps[:, h, :], scalar=k.tg[:, gate:gate + 1], in1=rows,
                                         op0=ALU.mult, op1=ALU.add)


def slot_attention(k, scope, slot_w):
    nc, ps = k.nc, k.ps
    w = k.sb("slot_w", [P, 3 * D + 6 * D], FP32, scope)
    wq, wk, wv = (w[:, D * n:D * n + D] for n in range(3))
    wih = w[:, 3 * D:6 * D]
    whh = [w[:, D * (6 + n):D * (7 + n)] for n in range(3)]
    slots = k.xt
    wqk = k.sb("slot_wqk", [P, D], FP32, scope)
    wvi = k.sb("slot_wvi", [P, 3 * D], FP32, scope)
    wqv_t = k.sb("slot_wqv_t", [P, 2 * D], FP32, scope)
    t = [k.sb(f"slot_t{n}", [P, T], FP32, scope) for n in range(5)]
    qh, ql = (k.sb(n, [P, T], FP16, scope) for n in ("slot_qh", "slot_ql"))
    R = 4
    LOOPS = (UT - R + 1) // R
    assert LOOPS * R + R - 1 == UT
    CUT = 320
    e = k.sb("slot_exps", [P, R, T], FP32, scope)
    el = k.sb("slot_exps_lo", [P, R, T], FP16, scope)
    mx = k.sb("slot_mx", [P, R, 1], FP32, scope)
    nb = k.sb("slot_nb", [P, R, 1], FP32, scope)
    sums = k.sb("slot_sums", [P, R, 1], FP32, scope)
    rec = k.sb("slot_rec", [P, R, 1], FP32, scope)
    vh, vl = (k.sb(n, [P, R, D + 1], FP16, scope) for n in ("slot_vh", "slot_vl"))
    den = k.sb("slot_den", [P, 2, TT], FP32, scope)
    ld = k.sem("slot_ld")
    w_turned, wt_ready, w_ps = (k.sem(f"sw_{n}") for n in ("turned", "wt", "ps"))
    sq_ready, ss_ready, ln_ready, rs_ready, q_ps, qf_ready, qh_ready = (
        k.sem(f"sq_{n}") for n in ("sq", "ss", "ln", "rs", "q_ps", "qf", "qh"))
    s_ready, nb_ready, exp_done, el_ready, v_ready, pv_done, m_dve = (
        k.sem(f"sm_{n}") for n in ("s", "nb", "exp", "el", "v", "pv", "dve"))
    u_ready, ut_ps, ut_sb, gate_ps, gates_ready, rh_ready, n_ready, g_dve = (
        k.sem(f"sg_{n}") for n in ("u", "ut_ps", "ut_sb", "gate_ps", "gates", "rh", "n", "dve"))
    acc = [ps[:, 4 + i // 3, (D + 1) * (i % 3):(D + 1) * (i % 3) + D + 1] for i in range(TT)]

    with nc.Block() as block:
        @block.sync
        def _(sp):
            sp.dma_start(w[:, :], slot_w).then_inc(ld, 16)

        @block.scalar
        def _(act):
            act.sem_inc(exp_done, CREDIT)
            act.wait_ge(w_turned, 1)
            act.activation(wqv_t[:, :], ps[:, 0, 0:2 * D], ACT.Copy).then_inc(wt_ready, 1)
            act.wait_ge(w_ps, 1)
            act.activation(wqk[:, :], ps[:, 1, 0:D], ACT.Copy, scale=k.cols[:, C_WSLOT:C_WSLOT + 1])
            act.wait_ge(w_ps, 2)
            act.activation(wvi[:, :], ps[:, 2, 0:3 * D], ACT.Copy, scale=k.cols[:, C_WIN:C_WIN + 1])

        @block.tensor
        def _(pe):
            pe.sem_inc(pv_done, R)
            pe.wait_ge(ld, 16)
            pe.transpose(ps[:, 0, 0:D], wq, k.ident[:, :])
            pe.transpose(ps[:, 0, D:2 * D], wv, k.ident[:, :]).then_inc(w_turned, 1)
            pe.wait_ge(wt_ready, 1)
            pe.matmul(ps[:, 1, 0:D], wqv_t[:, 0:D], wk, start=True, stop=True).then_inc(w_ps, 1)
            pe.matmul(ps[:, 2, 0:3 * D], wqv_t[:, D:2 * D], wih, start=True, stop=True).then_inc(w_ps, 1)

    with nc.Fori(0, NITER) as it:
        with nc.Block() as block:
            @block.scalar
            def _(act):
                for h in range(2):
                    act.activation(t[0][:, half(h)], slots[:, half(h)], ACT.Square).then_inc(sq_ready, 1)
                act.preload_act_table(ACT.Ln)
                for h in range(2):
                    act.wait_ge(ss_ready, it * 2 + h + 1)
                    act.activation(t[1][:, half(h)], ps[:, h, :], ACT.Ln, bias=k.eps6[:, :]).then_inc(ln_ready, 1)
                for h in range(2):
                    act.wait_ge(ln_ready, it * 2 + h + 1)
                    act.activation(t[2][:, half(h)], t[1][:, half(h)], ACT.Exp, scale=-0.5).then_inc(rs_ready, 1)
                for h in range(2):
                    act.wait_ge(qf_ready, it * 2 + h + 1)
                    act.activation(qh[:, half(h)], t[3][:, half(h)], ACT.Copy, scale=k.win_s[:, :]).then_inc(qh_ready, 1)

            @block.vector
            def _(dve):
                for h in range(2):
                    dve.wait_ge(rs_ready, it * 2 + h + 1)
                    dve.wait_ge(q_ps, it * 2 + h + 1)
                    dve.tensor_tensor(t[3][:, half(h)], t[2][:, half(h)], ps[:, 2 + h, :], ALU.mult).then_inc(qf_ready, 1)
                for h in range(2):
                    dve.wait_ge(qh_ready, it * 2 + h + 1)
                    dve.scalar_tensor_tensor(out=ql[:, half(h)], in0=t[3][:, half(h)], scalar=k.win_s[:, :],
                                             in1=qh[:, half(h)], op0=ALU.mult, op1=ALU.subtract)

            @block.tensor
            def _(pe):
                for h in range(2):
                    pe.wait_ge(sq_ready, it * 2 + h + 1)
                    pe.matmul(ps[:, h, :], k.mean_w[:, :], t[0][:, half(h)], start=True, stop=True).then_inc(ss_ready, 1)
                for h in range(2):
                    pe.matmul(ps[:, 2 + h, :], wqk[:, :], slots[:, half(h)], start=True, stop=True).then_inc(q_ps, 1)

        with nc.Block() as block:
            n0 = it * UT

            @block.tensor
            def _(pe):
                def scores(j, b):
                    pe.wait_ge(exp_done, n0 + j + 1)
                    cols_j = bass.ds(j * P, P)
                    for h in range(2):
                        pe.matmul(ps[:, 2 * b + h, :], k.pth[:, cols_j], qh[:, half(h)], start=True, stop=False)
                        pe.matmul(ps[:, 2 * b + h, :], k.pth[:, cols_j], ql[:, half(h)], start=False, stop=False)
                        ins = pe.matmul(ps[:, 2 * b + h, :], k.ptl[:, cols_j], qh[:, half(h)], start=False, stop=True)
                    ins.then_inc(s_ready, 1)

                def values(j, q):
                    pe.wait_ge(v_ready, n0 + j + 1)
                    pe.wait_ge(el_ready, n0 + j + 1)
                    for i in range(TT):
                        eh = top(e[:, q, tile(i)])
                        pe.matmul(acc[i], eh, vh[:, q, :], start=False, stop=False, skip_group_check=True)
                        pe.matmul(acc[i], eh, vl[:, q, :], start=False, stop=False, skip_group_check=True)
                        ins = pe.matmul(acc[i], el[:, q, tile(i)], vh[:, q, :], start=False, stop=False,
                                        skip_group_check=True)
                    ins.then_inc(pv_done, 1)

                for n in range(3):
                    pe.matmul(ps[:, 4 + n, :], k.zero_h[:, 0:P], k.zero_h[:, :], start=True, stop=False,
                              skip_group_check=True)
                for j in range(R - 1):
                    scores(j, j % 2)
                with pe.Fori(0, LOOPS) as i:
                    for q in range(R):
                        values(i * R + q, q)
                        scores(i * R + q + R - 1, (q + 1) % 2)
                for j in range(LOOPS * R, UT):
                    values(j, j % R)

            @block.scalar
            def _(act):
                act.preload_act_table(ACT.Exp)

                def exps(j, q):
                    b = q % 2
                    act.wait_ge(nb_ready, n0 + j + 1)
                    act.wait_ge(pv_done, n0 + j + 1)
                    act.activation(e[:, q, :].rearrange("p (h n) -> p h n", h=2), ps[:, 2 * b:2 * b + 2, :],
                                   ACT.Exp, bias=nb[:, q, :], accum_out=sums[:, q, :]).then_inc(exp_done, 1)

                with act.Fori(0, LOOPS) as i:
                    for q in range(R):
                        exps(i * R + q, q)
                for j in range(LOOPS * R, UT):
                    exps(j, j % R)

            @block.gpsimd
            def _(pool):
                def lows(j, q):
                    pool.wait_ge(exp_done, n0 + j + 1 + CREDIT)
                    pool.tensor_tensor(el[:, q, CUT:T], e[:, q, CUT:T], top(e[:, q, CUT:T]),
                                       ALU.subtract).then_inc(el_ready, 1)

                with pool.Fori(0, LOOPS) as i:
                    for q in range(R):
                        lows(i * R + q, q)
                for j in range(LOOPS * R, UT):
                    lows(j, j % R)

            @block.vector
            def _(dve):
                STEPS = 3

                def shift(j, q, n):
                    dve.wait_ge(s_ready, n0 + j + 1)
                    dve.tensor_reduce(mx[:, q, :], ps[:, 2 * (q % 2):2 * (q % 2) + 2, :], AX.XY, ALU.max).then_inc(m_dve, 1)
                    dve.wait_ge(m_dve, n + 1)
                    dve.tensor_scalar(nb[:, q, :], mx[:, q, :], -1.0, LIFT, ALU.mult, ALU.add).then_inc(nb_ready, 1)

                def scaled(j, q, n):
                    dve.wait_ge(exp_done, n0 + j + 1 + CREDIT)
                    dve.reciprocal(rec[:, q, :], sums[:, q, :]).then_inc(m_dve, 1)
                    dve.tensor_tensor(el[:, q, 0:CUT], e[:, q, 0:CUT], top(e[:, q, 0:CUT]), ALU.subtract)
                    dve.wait_ge(m_dve, n + 1)
                    dve.tensor_scalar(vh[:, q, :], k.pn[:, j, :], rec[:, q, :], None, ALU.mult).then_inc(m_dve, 1)
                    dve.wait_ge(m_dve, n + 2)
                    dve.scalar_tensor_tensor(out=vl[:, q, :], in0=k.pn[:, j, :], scalar=rec[:, q, :],
                                             in1=vh[:, q, :], op0=ALU.mult, op1=ALU.subtract).then_inc(v_ready, 1)

                base = it * (UT * STEPS)
                shift(0, 0, base)
                with dve.Fori(0, LOOPS) as i:
                    for q in range(R):
                        n = base + i * (R * STEPS) + q * STEPS + 1
                        shift(i * R + q + 1, (q + 1) % R, n)
                        scaled(i * R + q, q, n + 1)
                for j in range(LOOPS * R, UT):
                    n = base + j * STEPS + 1
                    if j + 1 < UT:
                        shift(j + 1, (j + 1) % R, n)
                        n = n + 1
                    scaled(j, j % R, n)

        with nc.Block() as block:
            r, z, hn_r, n_t, u_t = t

            @block.vector
            def _(dve):
                chain = Chain(dve, g_dve, it * 8)
                for n in range(3):
                    m = min(3, TT - 3 * n)
                    sums_n = ps[:, 4 + n, 0:m * (D + 1)].rearrange("p (i d) -> p i d", d=D + 1)[:, :, D]
                    ins = dve.tensor_scalar(den[:, 0, 3 * n:3 * n + m], sums_n, SLOT_EPS * VAL_SCALE, None, ALU.add)
                chain(ins)
                chain(dve.reciprocal(den[:, 1, :], den[:, 0, :]))
                for i in range(TT):
                    dve.tensor_scalar(n_t[:, tile(i)], acc[i][:, 0:D], den[:, 1, i:i + 1], None,
                                      ALU.mult).then_inc(u_ready, 1)
                for h in range(2):
                    dve.wait_ge(gates_ready, it * 2 + h + 1)
                    chain(dve.scalar_tensor_tensor(out=hn_r[:, half(h)], in0=ps[:, 6 + h, :],
                                                   scalar=k.cols[:, C_BHN:C_BHN + 1], in1=r[:, half(h)],
                                                   op0=ALU.add, op1=ALU.mult))
                    dve.tensor_tensor(hn_r[:, half(h)], ps[:, 4 + h, :], hn_r[:, half(h)], ALU.add).then_inc(rh_ready, 1)
                for h in range(2):
                    dve.wait_ge(n_ready, it * 2 + h + 1)
                    chain(dve.tensor_tensor(hn_r[:, half(h)], slots[:, half(h)], n_t[:, half(h)], ALU.subtract))
                    chain(dve.tensor_tensor(hn_r[:, half(h)], hn_r[:, half(h)], z[:, half(h)], ALU.mult))
                    dve.tensor_tensor(slots[:, half(h)], n_t[:, half(h)], hn_r[:, half(h)], ALU.add)

            @block.tensor
            def _(pe):
                def gate(bank, n, h, of_slots, first, last):
                    lhs, rhs = (whh[n], slots) if of_slots else (wvi[:, n * D:n * D + D], u_t)
                    return pe.matmul(ps[:, bank, :], lhs, rhs[:, half(h)], start=first, stop=last)

                gate(2, 1, 0, True, True, False)
                gate(3, 1, 1, True, True, False)
                gate(7, 2, 1, True, True, True)
                for i in range(TT):
                    pe.wait_ge(u_ready, it * TT + i + 1)
                    ins = pe.transpose(ps[:, i // 4, tile(i % 4)], n_t[:, tile(i)], k.ident[:, :])
                    if i % 4 == 3:
                        ins.then_inc(ut_ps, 1)
                gate(6, 2, 0, True, True, True)
                for h in range(2):
                    pe.wait_ge(ut_sb, it * 2 + h + 1)
                    gate(h, 0, h, True, True, False)
                    gate(h, 0, h, False, False, True)
                    gate(2 + h, 1, h, False, False, True)
                    gate(4 + h, 2, h, False, True, True).then_inc(gate_ps, 1)

            @block.scalar
            def _(act):
                act.preload_act_table(ACT.Sigmoid)
                for h in range(2):
                    act.wait_ge(ut_ps, it * 2 + h + 1)
                    act.activation(u_t[:, half(h)], ps[:, h, :], ACT.Copy).then_inc(ut_sb, 1)
                for h in range(2):
                    act.wait_ge(gate_ps, it * 2 + h + 1)
                    act.activation(r[:, half(h)], ps[:, h, :], ACT.Sigmoid, bias=k.bsum[:, 0:1]).then_inc(gates_ready, 1)
                    act.activation(z[:, half(h)], ps[:, 2 + h, :], ACT.Sigmoid, bias=k.bsum[:, 1:2])
                for h in range(2):
                    act.wait_ge(rh_ready, it * 2 + h + 1)
                    act.activation(n_t[:, half(h)], hn_r[:, half(h)], ACT.Tanh, bias=k.cols[:, C_BIN:C_BIN + 1]).then_inc(n_ready, 1)

    residual(k, "slot_res", slots, 0)


def widen(k, scope, tag, cwt, weigh):
    nc, ps = k.nc, k.ps
    turned, hi_ready = k.sem(f"{tag}_turned"), k.sem(f"{tag}_hi")
    with nc.Block() as block:
        @block.tensor
        def _(pe):
            for i in range(TT):
                ins = pe.transpose(ps[:, i // 4, tile(i % 4)], weigh[:, i, :], k.ident[:, :])
            ins.then_inc(turned, 1)

        @block.scalar
        def _(act):
            act.wait_ge(turned, 1)
            act.activation(cwt[:, 0, :].rearrange("p (h n) -> p h n", h=2), ps[:, 0:2, :], ACT.Copy).then_inc(hi_ready, 1)

        @block.vector
        def _(dve):
            dve.wait_ge(hi_ready, 1)
            dve.tensor_tensor(cwt[:, 1, :].rearrange("p (h n) -> p h n", h=2), ps[:, 0:2, :],
                              cwt[:, 0, :].rearrange("p (h n) -> p h n", h=2), ALU.subtract)


def top_experts(k, scope, cwt):
    nc, ps = k.nc, k.ps
    biased = k.sb("top_biased", [P, TT, E0], FP32, scope)
    rest = k.sb("top_rest", [P, TT, E0], FP32, scope)
    sig = k.sb("top_sig", [P, TT, E0], FP32, scope)
    best = k.sb("top_best", [P, TT, 8], FP32, scope)
    total = k.sb("top_total", [P, 2, TT], FP32, scope)
    weigh = k.sb("top_weigh", [P, TT, P], FP32, scope)
    aff_ready, e_ready, w_zero, d_ch, best_done = (k.sem(f"top_{n}") for n in ("aff", "exp", "zero", "dve", "best"))
    aff = ps[:, 0, :].rearrange("p (i e) -> p i e", e=E0)
    with nc.Block() as block:
        @block.tensor
        def _(pe):
            for i in range(TT):
                ins = pe.matmul(aff[:, i, :], k.xt[:, tile(i)], k.cent[:, :], start=True, stop=True)
            ins.then_inc(aff_ready, 1)

        @block.scalar
        def _(act):
            act.wait_ge(d_ch, 1)
            act.activation(sig[:, :, :], aff, ACT.Exp, scale=-1.0).then_inc(e_ready, 1)

        @block.gpsimd
        def _(pool):
            pool.memset(weigh[:, :, :], 0.0).then_inc(w_zero, 1)
            pool.wait_ge(w_zero, 1)
            pool.memset(weigh[:, :, E0], 1.0).then_inc(w_zero, 1)

        @block.vector
        def _(dve):
            chain = Chain(dve, d_ch)
            dve.wait_ge(aff_ready, 1)
            chain(dve.tensor_tensor(biased[:, :, :], aff, k.bias_e[:, :].unsqueeze(1).to_broadcast([P, TT, E0]), ALU.add))
            for i in range(TT):
                dve.max(best[:, i, :], biased[:, i, :]).then_inc(best_done, 1)
            for i in range(TT):
                dve.wait_ge(best_done, i + 1)
                ins = dve.match_replace(rest[:, i, :], best[:, i, :], biased[:, i, :], -3.0e38)
            chain(ins)
            chain(dve.tensor_tensor(rest[:, :, :], rest[:, :, :], biased[:, :, :], ALU.not_equal))
            dve.wait_ge(e_ready, 1)
            chain(dve.tensor_scalar(sig[:, :, :], sig[:, :, :], 1.0, None, ALU.add))
            chain(dve.reciprocal(sig[:, :, :], sig[:, :, :]))
            chain(dve.tensor_tensor(sig[:, :, :], sig[:, :, :], rest[:, :, :], ALU.mult))
            chain(dve.tensor_reduce(total[:, 0, :], sig[:, :, :], AX.X, ALU.add))
            chain(dve.tensor_scalar(total[:, 0, :], total[:, 0, :], 1e-8, None, ALU.add))
            chain(dve.reciprocal(total[:, 1, :], total[:, 0, :]))
            dve.wait_ge(w_zero, 2)
            dve.tensor_tensor(weigh[:, :, 0:E0], sig[:, :, :],
                              total[:, 1, :].unsqueeze(2).to_broadcast([P, TT, E0]), ALU.mult)

    widen(k, scope, "top", cwt, weigh)


def soft_experts(k, scope, cwt):
    nc, ps = k.nc, k.ps
    logit = k.sb("soft_logit", [P, TT, 2, E1], FP32, scope)
    prob = k.sb("soft_prob", [P, TT, 2, E1], FP32, scope)
    mx = k.sb("soft_mx", [P, TT, 2], FP32, scope)
    total = k.sb("soft_total", [P, 2, TT, 2], FP32, scope)
    cw = k.sb("soft_cw", [P, TT, E1], FP32, scope)
    cs = k.sb("soft_cs", [P, 2, TT], FP32, scope)
    weigh = k.sb("soft_weigh", [P, TT, P], FP32, scope)
    lg_ready, x_ready, e_ready, w_zero, d_ch = (k.sem(f"soft_{n}") for n in ("lg", "x", "exp", "zero", "dve"))
    lg = ps[:, 0, 0:TT * 2 * E1].rearrange("p (i g e) -> p i g e", g=2, e=E1)
    with nc.Block() as block:
        @block.tensor
        def _(pe):
            for i in range(TT):
                ins = pe.matmul(ps[:, 0, 2 * E1 * i:2 * E1 * (i + 1)], k.xt[:, tile(i)], k.rout[:, :],
                                start=True, stop=True)
            ins.then_inc(lg_ready, 1)

        @block.scalar
        def _(act):
            act.wait_ge(x_ready, 1)
            act.activation(prob[:, :, 0, :], logit[:, :, 0, :], ACT.Exp)
            act.activation(prob[:, :, 1, :], logit[:, :, 1, :], ACT.Exp, scale=10.0).then_inc(e_ready, 1)

        @block.gpsimd
        def _(pool):
            pool.memset(weigh[:, :, :], 0.0).then_inc(w_zero, 1)

        @block.vector
        def _(dve):
            chain = Chain(dve, d_ch)
            dve.wait_ge(lg_ready, 1)
            chain(dve.tensor_reduce(mx[:, :, :], lg, AX.X, ALU.max))
            dve.tensor_tensor(logit[:, :, :, :], lg, mx[:, :, :].unsqueeze(3).to_broadcast([P, TT, 2, E1]),
                              ALU.subtract).then_inc(x_ready, 1)
            dve.wait_ge(e_ready, 1)
            chain(dve.tensor_reduce(total[:, 0, :, :], prob[:, :, :, :], AX.X, ALU.add))
            chain(dve.reciprocal(total[:, 1, :, :], total[:, 0, :, :]))
            chain(dve.tensor_tensor(prob[:, :, :, :], prob[:, :, :, :],
                                    total[:, 1, :, :].unsqueeze(3).to_broadcast([P, TT, 2, E1]), ALU.mult))
            chain(dve.tensor_tensor(cw[:, :, :], prob[:, :, 0, :], prob[:, :, 1, :], ALU.mult))
            chain(dve.tensor_reduce(cs[:, 0, :], cw[:, :, :], AX.X, ALU.add))
            chain(dve.tensor_scalar(cs[:, 0, :], cs[:, 0, :], 1e-9, None, ALU.add))
            chain(dve.reciprocal(cs[:, 1, :], cs[:, 0, :]))
            dve.wait_ge(w_zero, 1)
            dve.tensor_tensor(weigh[:, :, 0:E1], cw[:, :, :], cs[:, 1, :].unsqueeze(2).to_broadcast([P, TT, E1]),
                              ALU.mult)

    widen(k, scope, "soft", cwt, weigh)


def experts(k, scope, tag, cwt, w_dram, gate):
    nc, ps = k.nc, k.ps
    gated = w_dram.shape[2] == 3 * P
    nch = w_dram.shape[0]
    nw = w_dram.shape[2] // P
    STEP = CPE if gated else 3
    npick = E1 if gated else CH0
    RAW = 4
    pick = k.sb(f"{tag}_pick", [P, npick, P], FP16, scope)
    raw = k.sb(f"{tag}_raw", [P, RAW, nw * P], FP32, scope)
    wh = k.sb(f"{tag}_wh", [P, RAW, nw * P], FP16, scope)
    wl = k.sb(f"{tag}_wl", [P, RAW, nw * P], FP16, scope)
    inner = k.sb(f"{tag}_inner", [P, 2, 512], FP32, scope)
    a = k.sb(f"{tag}_a", [P, 2, 512], FP32, scope)
    ah = k.sb(f"{tag}_ah", [P, 2, 512], FP16, scope)
    al = k.sb(f"{tag}_al", [P, 2, 512], FP16, scope)
    y = k.sb(f"{tag}_y", [P, T], FP32, scope)
    ld = [k.sem(f"{tag}_ld{n}") for n in range(RAW)]
    wh_ready, wl_ready, up_ready, in_ready, a_ready, ah_ready, al_ready, down_done, pk, m_ready = (
        k.sem(f"{tag}_{n}") for n in ("wh", "wl", "up", "in", "a", "ah", "al", "down", "pick", "m"))
    down_w = slice((nw - 1) * P, nw * P)
    SPREAD = 4 if gated else 2
    BODIES = nch // STEP
    assert nch % STEP == 0

    with nc.Block() as block:
        @block.gpsimd
        def _(pool):
            pool.memset(pick[:, :, :], 0.0).then_inc(pk, 1)
            pool.wait_ge(pk, 1)
            if gated:
                pat, view = [[-1, npick], [0, P]], pick[:, :, :]
            else:
                pat = [[-2, npick], [-1, 2], [0, F0]]
                view = pick[:, :, :].rearrange("p c (e f) -> p c e f", e=2)
            pool.affine_select(out=view, in_=view, compare_op=ALU.not_equal, fill=1.0, base=0, pattern=pat,
                               channel_multiplier=1)

        @block.tensor
        def _(pe):
            pe.sem_inc(down_done, CREDIT)

        @block.vector
        def _(dve):
            dve.sem_inc(a_ready, CREDIT)
            dve.sem_inc(al_ready, CREDIT)

    with nc.Block() as block:
        def bodies(eng, body):
            with eng.Fori(0, BODIES) as i:
                for s in range(STEP):
                    body(i * STEP + s, s)

        @block.sync
        def _(sp):
            def load(c, r):
                sp.dma_start(raw[:, r, :], w_dram[c]).then_inc(ld[r], 16)

            for c in range(RAW):
                load(c, c)
            with sp.Fori(1, nch // RAW) as i:
                for r in range(RAW):
                    sp.wait_ge(wl_ready, (i - 1) * RAW + r + 1)
                    sp.dma_start(raw[:, r, :], w_dram[bass.ds(i * RAW + r, 1)].rearrange("c p n -> (c p) n")).then_inc(ld[r], 16)
            for c in range(nch // RAW * RAW, nch):
                sp.wait_ge(wl_ready, c - RAW + 1)
                load(c, c % RAW)
            for r in range(RAW):
                sp.wait_ge(ld[r], 16 * ((nch - 1 - r) // RAW + 1))

        AHEAD = 2

        def split_loop(eng, weights, halves):
            for c in range(AHEAD):
                weights(c, c, 16)
            n = (nch - AHEAD) // RAW
            with eng.Fori(0, n) as i:
                for r in range(RAW):
                    weights(i * RAW + r + AHEAD, (r + AHEAD) % RAW, i * 16 + 16 * (1 + (r + AHEAD) // RAW))
                    halves(i * RAW + r)
            for c in range(n * RAW, nch):
                if c + AHEAD < nch:
                    weights(c + AHEAD, (c + AHEAD) % RAW, 16 * ((c + AHEAD) // RAW + 1))
                halves(c)

        @block.gpsimd
        def _(pool):
            def low(c, r, loaded):
                pool.wait_ge(wh_ready, c + 1)
                pool.tensor_tensor(wl[:, r, :], raw[:, r, :], wh[:, r, :], ALU.subtract).then_inc(wl_ready, 1)

            split_loop(pool, low, lambda c: None)

        @block.scalar
        def _(act):
            def high(c, r, loaded):
                act.wait_ge(ld[r], loaded)
                if not isinstance(c, int) or c >= AHEAD:
                    act.wait_ge(down_done, c * 2 - 2 * AHEAD)
                act.activation(wh[:, r, :], raw[:, r, :], ACT.Copy).then_inc(wh_ready, 1)

            def halves(c):
                for h in range(2):
                    n = c * 2 + h
                    act.wait_ge(up_ready, n + 1)
                    act.wait_ge(a_ready, n + 1)
                    act.activation(inner[:, h, :], ps[:, h, :], ACT.Silu).then_inc(in_ready, 1)
                for h in range(2):
                    n = c * 2 + h
                    act.wait_ge(a_ready, n + 1 + CREDIT)
                    act.wait_ge(down_done, n + 1)
                    act.activation(ah[:, h, :], a[:, h, :], ACT.Copy).then_inc(ah_ready, 1)

            act.preload_act_table(ACT.Silu)
            split_loop(act, high, halves)
            act.wait_ge(down_done, 2 * nch + CREDIT)
            act.activation(y[:, :].rearrange("p (h n) -> p h n", h=2), ps[:, 6:8, :], ACT.Copy)

        @block.vector
        def _(dve):
            def weigh(c, s):
                for h in range(2):
                    n = c * 2 + h
                    dve.wait_ge(in_ready, n + 1)
                    if gated:
                        dve.tensor_tensor(inner[:, h, :], inner[:, h, :], ps[:, 2 + h, :], ALU.mult).then_inc(m_ready, 1)
                        dve.wait_ge(m_ready, n + 1)
                    dve.wait_ge(al_ready, n + 1)
                    dve.tensor_tensor(a[:, h, :], inner[:, h, :], ps[:, SPREAD + h, :], ALU.mult).then_inc(a_ready, 1)
                for h in range(2):
                    n = c * 2 + h
                    dve.wait_ge(ah_ready, n + 1)
                    dve.wait_ge(down_done, n + 1)
                    dve.tensor_tensor(al[:, h, :], a[:, h, :], ah[:, h, :], ALU.subtract).then_inc(al_ready, 1)
            bodies(dve, weigh)

        @block.tensor
        def _(pe):
            def product(bank, w, h):
                b = w[0]
                pe.matmul(ps[:, bank, :], wh[:, b, w[1]], k.xth[:, half(h)], start=True, stop=False)
                pe.matmul(ps[:, bank, :], wh[:, b, w[1]], k.xtl[:, half(h)], start=False, stop=False)
                return pe.matmul(ps[:, bank, :], wl[:, b, w[1]], k.xth[:, half(h)], start=False, stop=True)

            def up(c, b, pick_at):
                pe.wait_ge(wl_ready, c + 1)
                for h in range(2):
                    pe.wait_ge(a_ready, c * 2 + h + 1)
                    for m in range(nw - 1):
                        product(2 * m + h, (b, slice(m * P, m * P + P)), h)
                    pe.matmul(ps[:, SPREAD + h, :], pick[:, pick_at, :], cwt[:, 0, half(h)], start=True, stop=False)
                    pe.matmul(ps[:, SPREAD + h, :], pick[:, pick_at, :], cwt[:, 1, half(h)], start=False,
                              stop=True).then_inc(up_ready, 1)

            def down(c, b):
                for h in range(2):
                    pe.wait_ge(al_ready, c * 2 + h + 1 + CREDIT)
                    pe.matmul(ps[:, 6 + h, :], wh[:, b, down_w], ah[:, h, :], start=False, stop=False, skip_group_check=True)
                    pe.matmul(ps[:, 6 + h, :], wl[:, b, down_w], ah[:, h, :], start=False, stop=False, skip_group_check=True)
                    pe.matmul(ps[:, 6 + h, :], wh[:, b, down_w], al[:, h, :], start=False, stop=False,
                              skip_group_check=True).then_inc(down_done, 1)

            for h in range(2):
                pe.matmul(ps[:, 6 + h, :], k.zero_h[:, 0:P], k.zero_h[:, :], start=True, stop=False,
                          skip_group_check=True)

            def at(c):
                return c // CPE if gated else c

            up(0, 0, at(0))
            if gated:
                with pe.Fori(0, E1 - 1) as i:
                    for s in range(CPE):
                        up(i * CPE + s + 1, (s + 1) % RAW, i + (s + 1) // CPE)
                        down(i * CPE + s, s % RAW)
                for c in range(nch - CPE, nch - 1):
                    up(c + 1, (c + 1) % RAW, at(c + 1))
                    down(c, c % RAW)
            else:
                with pe.Fori(0, (nch - 1) // RAW) as i:
                    for s in range(RAW):
                        up(i * RAW + s + 1, (s + 1) % RAW, i * RAW + s + 1)
                        down(i * RAW + s, s % RAW)
            down(nch - 1, (nch - 1) % RAW)

    residual(k, f"{tag}_res", y, gate)


def attention_weights(k, scope, wq1, wkv1):
    att = k.sb("att_rows", [P, 2, GT, HEADS * DH], FP32, scope)
    w = att[:, :, :, :].rearrange("p a i d -> p (a i d)")
    ld_w = [k.sem(f"a1_ldw{n}") for n in range(3)]
    with k.nc.Block() as block:
        @block.sync
        def _(sp):
            for n, src in enumerate((wq1, wkv1[:, 0:HEADS * DH], wkv1[:, HEADS * DH:2 * HEADS * DH])):
                sp.dma_start(w[:, n * HEADS * DH:(n + 1) * HEADS * DH], src).then_inc(ld_w[n], 16)
    return att, ld_w


def cross_attention(k, scope, att, ld_w, wo1):
    nc, ps = k.nc, k.ps
    w = att[:, :, :, :].rearrange("p a i d -> p (a i d)")
    NB = 3
    O_BANK, SIDE_BANK = NB, NB + 2
    K_USE, C_USE, Q_USE, V_USE, START = 0, 1, 3, 5, 7
    GUSES = TT + 2
    USES = START + G * TT + (G - 1) * 2
    assert (G - 1) % NB == 0 and USES % NB == 0
    GU = 2 * GT
    LU = 2 * (UT - (G - 1) * GT)
    UNITS = (G - 1) * GU + LU
    R = 4
    LEAD = R - 1
    DVE_UNITS = [3, 7]
    POOL_UNITS = [u for u in range(GU) if u not in DVE_UNITS]
    ND = len(DVE_UNITS)
    D_HEAD = (G - 1) * ND + sum(u < LU for u in DVE_UNITS)
    P_HEAD = UNITS - D_HEAD
    TAIL_UNITS = range(LU - 2, LU)
    assert UNITS % NB == 0 and 2 * UNITS % R == 0
    LOW_LEAD = 2
    e = k.e[:, :, :].rearrange("p a (b n) -> p (a b) n", b=2)
    el = k.el[:, :, :].rearrange("p a (b n) -> p (a b) n", b=2)
    ka, kb = (k.sb(n, [P, 2, MP], FP16, scope) for n in ("keys_a", "keys_b"))
    v = k.sb("values", [P, 2, MT, 2 * DH + 1], FP16, scope)
    qa, qb = (k.sb(n, [P, 2, T], FP16, scope) for n in ("q_a", "q_b"))
    wqh, wql, wkh, wkl = (k.sb(n, [P, HEADS * P], FP16, scope) for n in ("wq_h", "wq_l", "wk_h", "wk_l"))
    wvh, wvl = (k.sb(n, [P, HEADS * DH], FP16, scope) for n in ("wv_h", "wv_l"))
    runmax = k.sb("run_max", [P, TT, G], FP32, scope)
    cmax = k.sb("c_max", [P, TT], FP32, scope)
    cz = k.sb("c_spread", [P, TT, P], FP16, scope)
    rec = k.sb("o_rec", [P, 2, GT], FP32, scope)
    acc = ps[:, O_BANK:O_BANK + 2, 0:GT * (DH + 1)].rearrange("p a (i d) -> p a i d", d=DH + 1)

    h_ready, w_ch = k.sem("a1_wh"), k.sem("a1_wch")

    with nc.Block() as block:
        @block.scalar
        def _(act):
            for n, hi in ((0, wqh), (1, wkh)):
                act.wait_ge(ld_w[n], 16)
                src = w[:, n * HEADS * DH:(n + 1) * HEADS * DH].rearrange("p (h d) -> p h d", d=DH)
                for s in range(2):
                    act.activation(hi[:, :].rearrange("p (h s d) -> p h s d", s=2, d=DH)[:, :, s, :], src,
                                   ACT.Copy).then_inc(h_ready, 1)
            act.wait_ge(ld_w[2], 16)
            act.activation(wvh[:, :], w[:, 2 * HEADS * DH:3 * HEADS * DH], ACT.Copy).then_inc(h_ready, 1)

        @block.vector
        def _(dve):
            for n, hi, lo in ((0, wqh, wql), (1, wkh, wkl)):
                src = w[:, n * HEADS * DH:(n + 1) * HEADS * DH].rearrange("p (h d) -> p h d", d=DH)
                for s in range(2):
                    at = [x[:, :].rearrange("p (h s d) -> p h s d", s=2, d=DH)[:, :, s, :] for x in (lo, hi)]
                    dve.wait_ge(h_ready, 2 * n + s + 1)
                    dve.tensor_tensor(at[0], src, at[1], ALU.subtract)
            dve.wait_ge(h_ready, 5)
            dve.tensor_tensor(wvl[:, :], w[:, 2 * HEADS * DH:3 * HEADS * DH], wvh[:, :], ALU.subtract)
            for b in range(2):
                dve.tensor_copy(v[:, b, :, DH], k.mask[:, :])

        @block.gpsimd
        def _(pool):
            for b in range(2):
                pool.memset(qb[DH:P, b, :].bitcast(FP32), 0.0).then_inc(w_ch, 1)
            pool.wait_ge(w_ch, 2)
            for b in range(2):
                pool.memset(kb[DH:P, b, :].bitcast(FP32), TWO_ONES).then_inc(w_ch, 1)
            pool.wait_ge(w_ch, 4)
            pool.memset(cz[:, :, :].rearrange("p a b -> p (a b)").bitcast(FP32), 0.0)

    side_ready, side_free, qc_ready, kh_ready, kb_ready, vh_ready, c_ready, cu_ready, c_dve = (
        k.sem(f"ap_{n}") for n in ("side_ready", "side_free", "qc", "kh", "kb", "vh", "c", "cu", "cdve"))
    s_ready, exp_done, pool_low, dve_low, pv_done, o_free, o_dve = (
        k.sem(f"am_{n}") for n in ("s", "exp", "pool_low", "dve_low", "pv", "o_free", "odve"))

    with nc.Block() as block:
        @block.scalar
        def _(act):
            act.sem_inc(exp_done, R)

        @block.tensor
        def _(pe):
            pe.sem_inc(pv_done, R)

        @block.vector
        def _(dve):
            dve.sem_inc(side_free, NB)
            dve.sem_inc(o_free, 1)

    with nc.Block() as block:
        def walk(eng, start, group):
            def run(p, h, hb, n, nb):
                start(p, h, hb, n, nb)
                with eng.Fori(0, (G - 1) // NB) as gs:
                    for gi in range(NB):
                        group(h, hb, n, nb, gs * NB + gi, gi, False)
                group(h, hb, n, nb, G - 1, 0, True)
            run(None, None, 1, 0, 0)
            run(None, 0, 0, 1, 1)
            with eng.Fori(0, HEADS // 2 - 1) as hp:
                run(hp * 2, hp * 2 + 1, 1, hp * 2 + 2, 0)
                run(hp * 2 + 1, hp * 2 + 2, 0, hp * 2 + 3, 1)
            run(HEADS - 2, HEADS - 1, 1, None, 0)
            start(HEADS - 1, None, 0, None, 1)

        V_STEP, K_STEP = 2, 5
        USE_OF = {0: 0, 1: 1, 2: 3, 3: 4, 4: 5, 5: 7, 6: 8, 7: 9}
        GV_USE, GK_USE = 2, 6
        LAST_MAXIMA = [(0, 1, 2), (3, 4, 5), (6, 7), ()]

        def steps(last):
            return range(LU - 2 if last else GU)

        def maxima_of(u, last):
            return [(i, i) for i in LAST_MAXIMA[u]] if last else [(u, USE_OF[u])]

        def width(last):
            return P * (UT - (G - 1) * GT) if last else 512

        def bank(use):
            return SIDE_BANK + use % NB

        def group_bank(gi, use):
            return bank(START + gi * GUSES + use)

        def score_bank(gi, u):
            return (gi * GU + u) % NB

        def buf(hb, u):
            return (UNITS * hb + u) % R

        def c_use(n):
            return C_USE if n is not None else 0

        @block.tensor
        def _(pe):
            def side(n, use, products, count=1):
                pe.wait_ge(side_free, n * USES + use + 1)
                for o, l, r, first, last in products:
                    ins = pe.matmul(o, l, r, start=first, stop=last)
                ins.then_inc(side_ready, count)

            def keys(n, g, use, at_bank, count=1):
                at, cols_g = bass.ds(n * P, P), bass.ds(g * 512, 512)
                o = ps[:, at_bank, :]
                side(n, use, [(o, wkh[:, at], k.ch[:, cols_g], True, False),
                              (o, wkh[:, at], k.cl[:, cols_g], False, False),
                              (o, wkl[:, at], k.ch[:, cols_g], False, True)], count)

            def vals(n, g, use, at_bank, count=1):
                prods = []
                for u in range(GT):
                    o = ps[:, at_bank, DH * u:DH * u + DH]
                    rows, at = bass.ds(g * 512 + u * P, P), bass.ds(n * DH, DH)
                    prods += [(o, k.ch[:, rows], wvh[:, at], True, False),
                              (o, k.ch[:, rows], wvl[:, at], False, False),
                              (o, k.cl[:, rows], wvh[:, at], False, True)]
                side(n, use, prods, count)

            def queries(n, c):
                at = bass.ds(n * P, P)
                o = ps[:, bank(Q_USE + c), :]
                side(n, Q_USE + c, [(o, wqh[:, at], k.xth[:, half(c)], True, False),
                                    (o, wqh[:, at], k.xtl[:, half(c)], False, False),
                                    (o, wql[:, at], k.xth[:, half(c)], False, True)])

            def scores(h, hb, g, u, b):
                pe.wait_ge(exp_done, h * UNITS + g * GU + u + 1 + R - NB)
                at = bass.ds(g * 512 + u // 2 * P, P)
                pe.matmul(ps[:, b, :], ka[:, hb, at], qa[:, hb, half(u % 2)], start=True, stop=False)
                pe.matmul(ps[:, b, :], kb[:, hb, at], qb[:, hb, half(u % 2)], start=False,
                          stop=True).then_inc(s_ready, 1)

            def values(h, hb, g, u):
                if u in DVE_UNITS:
                    pe.wait_ge(dve_low, h * D_HEAD + g * ND + DVE_UNITS.index(u) + 1)
                else:
                    pe.wait_ge(pool_low, h * P_HEAD + g * (GU - ND) + POOL_UNITS.index(u) + 1)
                j, q = g * GT + u // 2, buf(hb, u)
                for i in range(GT):
                    o = acc[:, u % 2, i, :]
                    eh = top(e[:, q, tile(i)])
                    pe.matmul(o, eh, v[:, hb, j, 0:DH + 1], start=False, stop=False, skip_group_check=True)
                    pe.matmul(o[:, 0:DH], eh, v[:, hb, j, DH + 1:2 * DH + 1], start=False, stop=False, skip_group_check=True)
                    ins = pe.matmul(o, el[:, q, tile(i)], v[:, hb, j, 0:DH + 1], start=False, stop=False,
                                    skip_group_check=True)
                ins.then_inc(pv_done, 1)

            def start(p, h, hb, n, nb):
                if n is not None:
                    keys(n, 0, K_USE, bank(K_USE), 1 if h is not None else Q_USE)
                if h is not None:
                    pe.wait_ge(c_ready, h + 1)
                    for c in range(2):
                        use = c_use(n) + c
                        side(h + 1, use, [(ps[:, bank(use), tile(i)], cz[:, 4 * c + i, :],
                                           k.ident_h[:, :], True, True) for i in range(4)])
                for c in range(2):
                    if n is not None:
                        queries(n, c)
                    if p is not None:
                        values(p, nb, G - 1, TAIL_UNITS[c])
                if h is not None:
                    pe.wait_ge(side_free, (h + 1) * USES + c_use(n) + 1 + NB)
                    pe.wait_ge(cu_ready, h + 1)
                    pe.wait_ge(kb_ready, h * G + G)
                    scores(h, hb, 0, 0, 0)
                if n is not None:
                    vals(n, 0, V_USE, bank(V_USE), START - V_USE)
                if h is not None:
                    for u in range(1, LEAD):
                        scores(h, hb, 0, u, score_bank(0, u))
                    pe.wait_ge(o_free, h + 1)
                    for c in range(2):
                        pe.matmul(ps[:, O_BANK + c, :], k.zero_h[:, 0:P], k.zero_h[:, :], start=True, stop=False,
                                  skip_group_check=True)

            def group(h, hb, n, nb, g, gi, last):
                for u in steps(last):
                    if h is not None and not (last and u + LEAD >= LU):
                        scores(h, hb, g, u + LEAD, score_bank(gi, u + LEAD))
                    if n is not None and not last and u == V_STEP:
                        vals(n, g + 1, START + g * GUSES + GV_USE, group_bank(gi, GV_USE))
                    if n is not None and not last and u == K_STEP:
                        keys(n, g + 1, START + g * GUSES + GK_USE, group_bank(gi, GK_USE))
                    if h is not None:
                        values(h, hb, g, u)
                    if n is not None:
                        for i, use in maxima_of(u, last):
                            side(n, START + g * GUSES + use,
                                 [(ps[:, group_bank(gi, use), 0:width(last)], qa[:, nb, tile(i)],
                                   ka[:, nb, bass.ds(g * 512, width(last))], True, True)])

            walk(pe, start, group)

        @block.scalar
        def _(act):
            def keys(n, nb, g, use, at_bank):
                cols_g = bass.ds(g * 512, 512)
                act.wait_ge(side_ready, n * USES + use + 1)
                act.activation(ka[:, nb, cols_g], ps[:, at_bank, :], ACT.Copy).then_inc(kh_ready, 1)
                act.wait_ge(kh_ready, n * G + g + 1)
                act.activation(kb[0:DH, nb, cols_g], ka[0:DH, nb, cols_g], ACT.Copy).then_inc(kb_ready, 1)

            def vals(n, nb, g, use, at_bank):
                act.wait_ge(side_ready, n * USES + use + 1)
                act.activation(v[:, nb, bass.ds(g * GT, GT), 0:DH],
                               ps[:, at_bank, 0:GT * DH].rearrange("p (u d) -> p u d", d=DH),
                               ACT.Copy).then_inc(vh_ready, 1)

            def exps(h, hb, g, u, b):
                act.wait_ge(s_ready, h * UNITS + g * GU + u + 1)
                act.wait_ge(pv_done, h * UNITS + g * GU + u + 1)
                act.activation(e[:, buf(hb, u), :], ps[:, b, :], ACT.Exp).then_inc(exp_done, 1)

            def start(p, h, hb, n, nb):
                if n is not None:
                    keys(n, nb, 0, K_USE, bank(K_USE))
                if h is not None:
                    use = c_use(n) + 1
                    act.wait_ge(side_ready, (h + 1) * USES + use + 1)
                    act.activation(qb[DH:DH + 1, hb, half(1)], ps[DH:DH + 1, bank(use), :], ACT.Copy).then_inc(cu_ready, 1)
                if n is not None:
                    for c in range(2):
                        act.wait_ge(side_ready, n * USES + Q_USE + c + 1)
                        act.activation(qa[:, nb, half(c)], ps[:, bank(Q_USE + c), :], ACT.Copy, scale=HEAD_SCALE).then_inc(qc_ready, 1)
                if h is not None:
                    exps(h, hb, 0, 0, 0)
                if n is not None:
                    vals(n, nb, 0, V_USE, bank(V_USE))
                if h is not None:
                    for u in range(1, LEAD):
                        exps(h, hb, 0, u, score_bank(0, u))

            def group(h, hb, n, nb, g, gi, last):
                for u in steps(last):
                    if h is not None and not (last and u + LEAD >= LU):
                        exps(h, hb, g, u + LEAD, score_bank(gi, u + LEAD))
                    if n is not None and not last and u == V_STEP:
                        vals(n, nb, g + 1, START + g * GUSES + GV_USE, group_bank(gi, GV_USE))
                    if n is not None and not last and u == K_STEP:
                        keys(n, nb, g + 1, START + g * GUSES + GK_USE, group_bank(gi, GK_USE))

            act.preload_act_table(ACT.Exp)
            walk(act, start, group)

        @block.gpsimd
        def _(pool):
            def group(h, hb, n, nb, g, gi, last):
                if h is not None:
                    for u in POOL_UNITS:
                        if not (last and u >= LU):
                            q = buf(hb, u)
                            pool.wait_ge(exp_done, h * UNITS + g * GU + u + 1 + R)
                            pool.tensor_tensor(el[:, q, :], e[:, q, :], top(e[:, q, :]), ALU.subtract).then_inc(pool_low, 1)

            walk(pool, lambda *heads: None, group)

        @block.vector
        def _(dve):
            def low_values(n, nb, g, at_bank, count=1):
                rows = bass.ds(g * GT, GT)
                dve.wait_ge(vh_ready, n * G + g + 1)
                dve.tensor_tensor(v[:, nb, rows, DH + 1:2 * DH + 1],
                                  ps[:, at_bank, 0:GT * DH].rearrange("p (u d) -> p u d", d=DH),
                                  v[:, nb, rows, 0:DH], ALU.subtract).then_inc(side_free, count)

            def low_keys(n, nb, g, at_bank, count=1):
                cols_g = bass.ds(g * 512, 512)
                dve.wait_ge(kh_ready, n * G + g + 1)
                dve.tensor_tensor(ka[DH:P, nb, cols_g], ps[DH:P, at_bank, :], ka[DH:P, nb, cols_g],
                                  ALU.subtract).then_inc(side_free, count)

            def start(p, h, hb, n, nb):
                if n is not None:
                    low_keys(n, nb, 0, bank(K_USE), 1 if h is not None else Q_USE)
                if h is not None:
                    use = c_use(n)
                    dve.wait_ge(side_ready, (h + 1) * USES + use + 1)
                    dve.tensor_copy(qb[DH:DH + 1, hb, half(0)], ps[DH:DH + 1, bank(use), :]).then_inc(side_free, 1)
                if n is not None:
                    for c in range(2):
                        dve.wait_ge(qc_ready, n * 2 + c + 1)
                        dve.scalar_tensor_tensor(out=qb[0:DH, nb, half(c)], in0=ps[0:DH, bank(Q_USE + c), :],
                                                 scalar=HEAD_SCALE, in1=qa[0:DH, nb, half(c)], op0=ALU.mult,
                                                 op1=ALU.subtract).then_inc(side_free, 2 if h is not None and c == 0 else 1)
                if p is not None:
                    dve.wait_ge(pv_done, p * UNITS + UNITS + R)
                    dve.reciprocal(rec[:, :, :], acc[:, :, :, DH]).then_inc(o_dve, 1)
                    dve.wait_ge(o_dve, p + 1)
                    for a in range(2):
                        ins = dve.tensor_tensor(att[:, a, :, bass.ds(p * DH, DH)], acc[:, a, :, 0:DH],
                                                rec[:, a, :].unsqueeze(2).to_broadcast([P, GT, DH]), ALU.mult)
                    ins.then_inc(o_free, 1)
                if n is not None:
                    low_values(n, nb, 0, bank(V_USE), START - V_USE)

            def group(h, hb, n, nb, g, gi, last):
                for u in steps(last):
                    w = u + LOW_LEAD
                    if h is not None and w in DVE_UNITS and not (last and w >= LU):
                        q = buf(hb, w)
                        dve.wait_ge(exp_done, h * UNITS + g * GU + w + 1 + R)
                        dve.tensor_tensor(el[:, q, :], e[:, q, :], top(e[:, q, :]), ALU.subtract).then_inc(dve_low, 1)
                    if n is not None and not last and u == V_STEP:
                        low_values(n, nb, g + 1, group_bank(gi, GV_USE))
                    if n is not None and not last and u == K_STEP:
                        low_keys(n, nb, g + 1, group_bank(gi, GK_USE))
                    if n is not None:
                        for i, use in maxima_of(u, last):
                            dve.wait_ge(side_ready, n * USES + START + g * GUSES + use + 1)
                            dve.tensor_reduce(runmax[:, i, bass.ds(g, 1)], ps[:, group_bank(gi, use), 0:width(last)],
                                              AX.X, ALU.max).then_inc(side_free, 1)
                if n is not None and last:
                    dve.wait_ge(side_free, n * USES + USES + NB)
                    dve.tensor_reduce(cmax[:, :], runmax[:, :, :], AX.X, ALU.max).then_inc(c_dve, 1)
                    dve.wait_ge(c_dve, n + 1)
                    dve.tensor_scalar(cz[:, :, DH], cmax[:, :], -1.0, LIFT, ALU.mult, ALU.add).then_inc(c_ready, 1)
                    dve.tensor_tensor(v[:, nb, FULL, :], v[:, nb, FULL, :],
                                      k.mask[:, FULL:FULL + 1].to_broadcast([P, 2 * DH + 1]), ALU.mult)

            walk(dve, start, group)

    output_projection(k, att, wo1)


def output_projection(k, att, wo1):
    nc, ps = k.nc, k.ps
    NCK = HEADS * DH // P
    wo = k.ch[:, 0:NCK * P * 2].bitcast(FP32).rearrange("p (c d) -> p c d", c=NCK)
    at = k.e
    ld, turned, copied, y_ready = (k.sem(f"wo_{n}") for n in ("ld", "turned", "copied", "y"))
    with nc.Block() as block:
        @block.sync
        def _(sp):
            sp.dma_start(wo, wo1.rearrange("(c p) d -> p c d", p=P)).then_inc(ld, 16)

        @block.tensor
        def _(pe):
            for n in range(2):
                pe.matmul(ps[:, 4 + n, :], k.zero_h[:, 0:P], k.zero_h[:, :], start=True, stop=False, skip_group_check=True)

            def turn(c):
                if c >= 2:
                    pe.wait_ge(copied, c - 1)
                for i in range(TT):
                    ins = pe.transpose(ps[:, 2 * (c % 2) + i // GT, tile(i % GT)], att[:, i // GT, i % GT, tile(c)], k.ident[:, :])
                ins.then_inc(turned, 1)

            turn(0)
            pe.wait_ge(ld, 16)
            for c in range(NCK):
                if c + 1 < NCK:
                    turn(c + 1)
                pe.wait_ge(copied, c + 1)
                for i in range(TT):
                    ins = pe.matmul(ps[:, 4 + i // GT, tile(i % GT)], at[:, c % 2, tile(i)], wo[:, c, :],
                                    start=False, stop=False, skip_group_check=True)
            ins.then_inc(y_ready, 1)

        @block.scalar
        def _(act):
            for c in range(NCK):
                act.wait_ge(turned, c + 1)
                b = c % 2
                act.activation(at[:, b, :].rearrange("p (h n) -> p h n", h=2), ps[:, 2 * b:2 * b + 2, :],
                               ACT.Copy).then_inc(copied, 1)

        @block.vector
        def _(dve):
            dve.wait_ge(y_ready, 1)
            rows = k.x[:, :, :].rearrange("p (a i) d -> p a (i d)", a=2)
            dve.scalar_tensor_tensor(out=rows, in0=ps[:, 4:6, :], scalar=k.tg[:, 2:3], in1=rows, op0=ALU.mult, op1=ALU.add)


def kernel(**inputs):
    import numpy as np
    import concourse.bacc as bacc
    from concourse import mybir as my
    from concourse.bass_utils import run_bass_kernel_spmd as run

    a = {n: np.asarray(v) for n, v in inputs.items()}
    f = np.float32
    x = np.ascontiguousarray(a["x"])
    bih, bhh = (a[f"L0_xattn_gru_{n}"].reshape(3, 128) for n in ("bih", "bhh"))
    arrays = {
        "x": x,
        "ctx": np.ascontiguousarray(a["ctx_1024"]),
        "cols": np.ascontiguousarray(np.stack(
            [a["L0_xattn_input_norm_w"], a["L0_xattn_slot_norm_w"], *bih, *bhh, a["L1_xattn_ln_g"], a["L1_xattn_ln_b"]], 1)),
        "gates": np.ascontiguousarray(np.broadcast_to(
            np.stack([a["g_xattn"], a["g_ffn"]], 1).reshape(1, 4), (128, 4))),
        "slot_w": np.ascontiguousarray(np.concatenate(
            [a["L0_xattn_Wq"].T, a["L0_xattn_Wk"], a["L0_xattn_Wv"].T, a["L0_xattn_gru_wih"].T, a["L0_xattn_gru_whh"].T], 1)),
        "cent_t": np.ascontiguousarray(a["L0_ffn_centroids"].T),
        "bias_e": np.ascontiguousarray(np.broadcast_to(a["L0_ffn_expert_biases"][None], (128, 64))),
        "wq1": np.ascontiguousarray(a["L1_xattn_Wq"]),
        "wkv1": np.ascontiguousarray(a["L1_xattn_Wkv"]),
        "wo1": np.ascontiguousarray(a["L1_xattn_Wo"]),
        "rout_w": np.ascontiguousarray(np.concatenate([a["L1_ffn_w_router"], a["L1_ffn_w_gating"]], 1)),
    }
    up = a["L0_ffn_W_up"].reshape(32, 2, 128, 64).transpose(0, 2, 1, 3).reshape(32, 128, 128)
    dn = a["L0_ffn_W_down"].reshape(32, 128, 128)
    w0 = np.zeros((33, 128, 256), f)
    w0[:32, :, :128], w0[:32, :, 128:] = up, dn
    w0[32, :, :64], w0[32, :64, 128:] = a["L0_ffn_Ws_up"], a["L0_ffn_Ws_down"]
    arrays["ffn0_w"] = w0
    gt, up = (a[n].reshape(8, 128, 4, 128).transpose(0, 2, 1, 3).reshape(32, 128, 128) for n in ("L1_ffn_w_gate", "L1_ffn_w_up"))
    dn = a["L1_ffn_w_down"].reshape(32, 128, 128)
    arrays["ffn1_w"] = np.ascontiguousarray(np.concatenate([gt, up, dn], 2))

    nc = bacc.Bacc("TRN2", target_bir_lowering=False, num_devices=1)
    args = {n: nc.dram_tensor(f"in_{n}", v.shape, my.dt.from_np(v.dtype), kind="ExternalInput").ap() for n, v in arrays.items()}
    out = nc.dram_tensor("out", (1, 1024, 128), my.dt.float32, kind="ExternalOutput").ap()
    build(nc, args["x"], args["ctx"], *(args[n] for n in (
        "cols", "gates", "slot_w", "cent_t", "bias_e", "wq1", "wkv1", "wo1", "rout_w", "ffn0_w", "ffn1_w")), out)
    r = run(nc, [{f"in_{n}": v for n, v in arrays.items()}], core_ids=[0])
    return r.results[0]["out"]
```
